# Optimizing a Trainium2 kernel written in Bass

```python
import numpy as np
import jax
import jax.numpy as jnp

def _softmax(x, axis=-1):
    return jax.nn.softmax(x, axis=axis)

def _gelu(x):
    return jax.nn.gelu(x, approximate=True)

def _silu(x):
    return jax.nn.silu(x)

def _sigmoid(x):
    return jax.nn.sigmoid(x)

def _layernorm(x, axis=-1, eps=1e-05):
    m = jnp.mean(x, axis=axis, keepdims=True)
    v = jnp.var(x, axis=axis, keepdims=True)
    return (x - m) / jnp.sqrt(v + eps)

def _scatter_add(tgt, idx, src, axis=0):
    return tgt.at[idx].add(src)

def _segment_sum(src, seg, n):
    return jax.ops.segment_sum(src, seg, n)
kernel_name = 'mk_xattn_ffn_d1_seqx_r2_e8336a'

def setup_inputs(seed: int=0):
    np.random.seed(seed)
    _w = jnp.asarray

    def _rec_inputs():
        import jax
        import jax.numpy as jnp
        _rk = jax.random.key(seed)
        x = 7.22e-05 + 1 * jax.random.normal(jax.random.fold_in(_rk, 1), (8, 512, 512), jnp.float32)
        _lenS = 512 - jax.random.randint(jax.random.fold_in(_rk, 7), (8,), 0, max(1, 512 // 4) + 1, jnp.int32)
        _lenS2 = 512 - jax.random.randint(jax.random.fold_in(_rk, 8), (8,), 0, max(1, 512 // 4) + 1, jnp.int32)
        _ctx_1024P = jax.random.normal(jax.random.fold_in(_rk, 11), (8, 16, 512), jnp.float32)
        _ctx_1024c = jax.random.dirichlet(jax.random.fold_in(_rk, 511), 0.3 * jnp.ones((16,), jnp.float32), (8, 512))
        _ctx_1024t = jnp.einsum('bsk,bkd->bsd', _ctx_1024c, _ctx_1024P)
        _ctx_1024t = _ctx_1024t * jax.lax.rsqrt(jnp.mean(jnp.square(_ctx_1024t)) + 1e-12) * 0.953939
        ctx_1024 = 4.13588e-05 + 0.999923 * (_ctx_1024t + 0.3 * jax.random.normal(jax.random.fold_in(_rk, 611), (8, 512, 512), jnp.float32))
        fside_1x16xSxS2_0 = 7.48737e-07 + 0.100011 * jax.random.normal(jax.random.fold_in(_rk, 13), (1, 16, 512, 512), jnp.float32)
        _validS = jnp.arange(512)[None, :] < _lenS[:, None]
        _validS2 = jnp.arange(512)[None, :] < _lenS2[:, None]
        _causal = jnp.tril(jnp.ones((512, 512), dtype=bool))
        mask_Bx1xSxS2_ik1 = jnp.where(jnp.broadcast_to(_validS2[:, None, None, :], (8, 1, 512, 512)), 1, 0).astype(jnp.int32)
        return (x, ctx_1024, fside_1x16xSxS2_0, mask_Bx1xSxS2_ik1)
    x, ctx_1024, fside_1x16xSxS2_0, mask_Bx1xSxS2_ik1 = _rec_inputs()

    def _L0_xattn_setup():
        import jax, jax.numpy as jnp
        import numpy as np
        B, S, D, H = (4, 1024, 512, 16)
        DK = D // H

        def _split_heads(x):
            b, s, _ = x.shape
            return x.reshape(b, s, H, DK).transpose(0, 2, 1, 3)
        key = jax.random.key(seed)
        ks = jax.random.split(key, 14)
        scale = 1.0 / np.sqrt(D)
        inp = {'Q': jax.random.normal(ks[0], (B, S, D), jnp.float32), 'K': jax.random.normal(ks[1], (B, S, D), jnp.float32), 'V': jax.random.normal(ks[2], (B, S, D), jnp.float32), 'mask': jax.random.randint(ks[3], (B, 1, S, S), 0, 2, jnp.int32), 'attn_bias': jax.random.normal(ks[4], (1, H, S, S), jnp.float32) * 0.1, 'Wq': jax.random.normal(ks[5], (D, D), jnp.float32) * scale, 'bq': jnp.zeros((D,), jnp.float32), 'Wk': jax.random.normal(ks[6], (D, D), jnp.float32) * scale, 'bk': jnp.zeros((D,), jnp.float32), 'Wv': jax.random.normal(ks[7], (D, D), jnp.float32) * scale, 'bv': jnp.zeros((D,), jnp.float32), 'Wo': jax.random.normal(ks[8], (D, D), jnp.float32) * scale, 'bo': jnp.zeros((D,), jnp.float32)}
        return inp
    _L0_xattn_all = _L0_xattn_setup()
    _L0_xattn_in = {k: v for k, v in _L0_xattn_all.items() if k in ('Wq', 'bq', 'Wk', 'bk', 'Wv', 'bv', 'Wo', 'bo')}
    del _L0_xattn_all

    def _L0_ffn_setup():
        import jax, jax.numpy as jnp
        import numpy as np
        TAU = 10.0
        EPS = 1e-06
        TOP_K = 8

        def _layernorm(x, g, b):
            mu = jnp.mean(x, axis=-1, keepdims=True)
            var = jnp.var(x, axis=-1, keepdims=True)
            return (x - mu) * jax.lax.rsqrt(var + 1e-05) * g + b

        def _unit_rows(W):
            n = jnp.linalg.norm(W, axis=1, keepdims=True)
            return W / jnp.maximum(n, EPS)
        key = jax.random.key(seed)
        ks = jax.random.split(key, 5)
        D, NB, H = (512, 256, 2048)
        B, S = (4, 1024)
        x = jax.random.normal(ks[0], (B, S, D), dtype=jnp.float32)
        W1 = jax.random.normal(ks[1], (H, D), dtype=jnp.float32) * (1.0 / np.sqrt(D))
        W2 = jax.random.normal(ks[2], (D, H), dtype=jnp.float32) * (1.0 / np.sqrt(H))
        ln_g = jnp.ones((D,), jnp.float32)
        ln_b = jnp.zeros((D,), jnp.float32)
        router_W = jax.random.normal(ks[3], (NB, D), dtype=jnp.float32) * 0.01
        router_b = jnp.zeros((NB,), jnp.float32)
        raw_U = jax.random.normal(ks[4], (NB, D), dtype=jnp.float32) * 0.02
        raw_V = jax.random.normal(jax.random.fold_in(key, 7), (NB, D), dtype=jnp.float32) * 0.02
        gamma = jnp.ones((1, 1, D), jnp.float32) * 0.1
        return {'x': x, 'W1': W1, 'W2': W2, 'ln_g': ln_g, 'ln_b': ln_b, 'router_W': router_W, 'router_b': router_b, 'raw_U': raw_U, 'raw_V': raw_V, 'gamma': gamma}
    _L0_ffn_all = _L0_ffn_setup()
    _L0_ffn_in = {k: v for k, v in _L0_ffn_all.items() if k in ('W1', 'W2', 'ln_g', 'ln_b', 'router_W', 'router_b', 'raw_U', 'raw_V', 'gamma')}
    del _L0_ffn_all
    return {'x': x, 'ctx_1024': ctx_1024, 'fside_1x16xSxS2_0': fside_1x16xSxS2_0, 'mask_Bx1xSxS2_ik1': mask_Bx1xSxS2_ik1, 'L0_xattn_Wq': _L0_xattn_in['Wq'], 'L0_xattn_bq': _L0_xattn_in['bq'], 'L0_xattn_Wk': _L0_xattn_in['Wk'], 'L0_xattn_bk': _L0_xattn_in['bk'], 'L0_xattn_Wv': _L0_xattn_in['Wv'], 'L0_xattn_bv': _L0_xattn_in['bv'], 'L0_xattn_Wo': _L0_xattn_in['Wo'], 'L0_xattn_bo': _L0_xattn_in['bo'], 'L0_ffn_W1': _L0_ffn_in['W1'], 'L0_ffn_W2': _L0_ffn_in['W2'], 'L0_ffn_ln_g': _L0_ffn_in['ln_g'], 'L0_ffn_ln_b': _L0_ffn_in['ln_b'], 'L0_ffn_router_W': _L0_ffn_in['router_W'], 'L0_ffn_router_b': _L0_ffn_in['router_b'], 'L0_ffn_raw_U': _L0_ffn_in['raw_U'], 'L0_ffn_raw_V': _L0_ffn_in['raw_V'], 'L0_ffn_gamma': _L0_ffn_in['gamma']}

def reference(x, ctx_1024, fside_1x16xSxS2_0, mask_Bx1xSxS2_ik1, L0_xattn_Wq, L0_xattn_bq, L0_xattn_Wk, L0_xattn_bk, L0_xattn_Wv, L0_xattn_bv, L0_xattn_Wo, L0_xattn_bo, L0_ffn_W1, L0_ffn_W2, L0_ffn_ln_g, L0_ffn_ln_b, L0_ffn_router_W, L0_ffn_router_b, L0_ffn_raw_U, L0_ffn_raw_V, L0_ffn_gamma):
    import jax
    import jax.numpy as jnp

    def _L0_xattn_ref(Q, K, V, mask, attn_bias, Wq, bq, Wk, bk, Wv, bv, Wo, bo):
        import jax, jax.numpy as jnp
        import numpy as np
        B, S, D, H = (4, 1024, 512, 16)
        DK = D // H

        def _split_heads(x):
            b, s, _ = x.shape
            return x.reshape(b, s, H, DK).transpose(0, 2, 1, 3)
        q = _split_heads(Q @ Wq.T + bq)
        k = _split_heads(K @ Wk.T + bk)
        v = _split_heads(V @ Wv.T + bv)
        scores = jnp.einsum('bhqd,bhkd->bhqk', q, k) / jnp.sqrt(jnp.float32(DK))
        scores = jnp.where(mask == 0, jnp.float32(-1000000000.0), scores)
        scores = scores + attn_bias
        probs = jax.nn.softmax(scores, axis=-1)
        out = jnp.einsum('bhqk,bhkd->bhqd', probs, v)
        out = out.transpose(0, 2, 1, 3).reshape(Q.shape[0], Q.shape[1], D)
        return out @ Wo.T + bo

    def _L0_ffn_ref(x, W1, W2, ln_g, ln_b, router_W, router_b, raw_U, raw_V, gamma):
        import jax, jax.numpy as jnp
        import numpy as np
        TAU = 10.0
        EPS = 1e-06
        TOP_K = 8

        def _layernorm(x, g, b):
            mu = jnp.mean(x, axis=-1, keepdims=True)
            var = jnp.var(x, axis=-1, keepdims=True)
            return (x - mu) * jax.lax.rsqrt(var + 1e-05) * g + b

        def _unit_rows(W):
            n = jnp.linalg.norm(W, axis=1, keepdims=True)
            return W / jnp.maximum(n, EPS)
        B, S, D = x.shape
        x_flat = x.reshape(-1, D)
        r_raw = _layernorm(x_flat, ln_g, ln_b) @ router_W.T + router_b
        r = jnp.clip(r_raw, -TAU, TAU)
        alpha = jax.nn.softplus(r)
        phi, idx = jax.lax.top_k(alpha, TOP_K)
        S_sum = jnp.sum(phi, axis=-1, keepdims=True)
        Z = phi / (S_sum + EPS) * jnp.tanh(S_sum)
        U_sel = _unit_rows(raw_U)[idx]
        V_sel = _unit_rows(raw_V)[idx]
        h_lat = jnp.einsum('nd,nkd->nk', x_flat, U_sel)
        dyn = jnp.einsum('nk,nkd->nd', h_lat * Z, V_sel).reshape(B, S, D) * gamma
        static = (jax.nn.gelu(x_flat @ W1.T, approximate=False) @ W2.T).reshape(B, S, D)
        return static + dyn
    x = x + _L0_xattn_ref(_layernorm(x, axis=-1), ctx_1024, ctx_1024, mask_Bx1xSxS2_ik1, fside_1x16xSxS2_0, L0_xattn_Wq, L0_xattn_bq, L0_xattn_Wk, L0_xattn_bk, L0_xattn_Wv, L0_xattn_bv, L0_xattn_Wo, L0_xattn_bo)
    x = x + _L0_ffn_ref(_layernorm(x, axis=-1), L0_ffn_W1, L0_ffn_W2, L0_ffn_ln_g, L0_ffn_ln_b, L0_ffn_router_W, L0_ffn_router_b, L0_ffn_raw_U, L0_ffn_raw_V, L0_ffn_gamma)
    return x

_drawn_inputs = setup_inputs


def setup_inputs(seed=0):
    import zlib

    import numpy as np

    out = dict(_drawn_inputs(seed))
    spreads = {'L0_xattn_bq': (0.0, 0.443),
     'L0_xattn_bk': (0.0, 0.8),
     'L0_xattn_bv': (0.0, 0.1),
     'L0_xattn_bo': (0.0, 0.1),
     'L0_ffn_ln_g': (1.0, 0.6),
     'L0_ffn_ln_b': (0.0, 0.8),
     'L0_ffn_router_b': (0.0, 0.8),
     'L0_ffn_gamma': (0.10000000149011612, 0.6)}
    factors = {'fside_1x16xSxS2_0': 8.0, 'L0_ffn_router_W': 8.0, 'L0_ffn_raw_U': 8.0, 'L0_ffn_raw_V': 8.0}
    for name, (base, spread) in spreads.items():
        noise = np.random.default_rng([zlib.crc32(name.encode()), seed]).standard_normal(out[name].shape)
        drawn = base * np.exp(spread * noise) if base else spread * noise
        out[name] = jnp.asarray(drawn.astype(out[name].dtype))
    for name, factor in factors.items():
        out[name] = (out[name] * factor).astype(out[name].dtype)
    return out
```

```python
from contextlib import ExitStack

import concourse.bass as bass
from concourse import mybir

P = 128
F32 = mybir.dt.float32
F32R = mybir.dt.float32r
I32 = mybir.dt.int32
ALU = mybir.AluOpType
ACT = mybir.ActivationFunctionType
AX_X = mybir.AxisListType.X

PASSES = ((0, 0), (0, 1), (1, 0))

B, S, D, H = 8, 512, 512, 16
DK = D // H
NT = S // P
NC = D // P
HG = P // DK
VW = 2 * DK + 2
FF = 2048
NF = FF // P
NB = 256
NL = NB // P
LN_EPS = 1e-5
UNIT_EPS = 1e-6
TAU = 10.0
MASKED = 1.0e9
QSCALE = -1.0 / float(DK) ** 0.5


def build(nc, x, ctxT, bias, mask, WqT, bq, WkT, bk, WvT, bv, WoT, bo, W1T, W2T,
          ln_g, ln_b, rWT, rb, rawU, rawV, gamma, out):
    qh_d, ql_d, kh_d, kl_d = (
        nc.dram_tensor(n, (NC * B, P, S), F32, kind="Internal").ap() for n in ("qh_d", "ql_d", "kh_d", "kl_d"))
    v_d = nc.dram_tensor("v_d", (NC * B, S, HG * VW), F32, kind="Internal").ap()
    pos_d = nc.dram_tensor("pos_d", (B, S, S), F32, kind="Internal").ap()
    att_d = nc.dram_tensor("att_d", (NC * B, S, P), F32, kind="Internal").ap()
    part_d = nc.dram_tensor("part_d", (B, S, D), F32, kind="Internal").ap()
    zh_d, zl_d = (nc.dram_tensor(n, (B, P, NC, S), F32, kind="Internal").ap() for n in ("zh_d", "zl_d"))

    with ExitStack() as top:
        ident = top.enter_context(nc.sbuf_tensor("ident", [P, P], F32))
        ones = top.enter_context(nc.sbuf_tensor("ones", [P, P], F32))
        neg_half = top.enter_context(nc.sbuf_tensor("neg_half", [P, NT], F32))
        comb = top.enter_context(nc.sbuf_tensor("comb", [2 * DK + 1, DK + 1], F32))
        project(nc, ident, ones, neg_half, comb, x, ctxT, mask, WqT, bq, WkT, bk, WvT, bv,
                qh_d, ql_d, kh_d, kl_d, v_d, pos_d)
        attend(nc, ident, comb, bias, qh_d, ql_d, kh_d, kl_d, v_d, pos_d, att_d)
        mix(nc, ident, neg_half, x, att_d, WoT, bo, ln_g, ln_b, rWT, rb, rawU, rawV, gamma,
            part_d, zh_d, zl_d)
        feed(nc, W1T, W2T, zh_d, zl_d, part_d, out)


def tokens(ap):
    return ap.rearrange("(t p) n -> p t n", p=P)


def need(eng, semaphore, count):
    if not isinstance(count, int) or count > 0:
        eng.wait_ge(semaphore, count)


def gate(eng, passed):
    eng.sem_inc(passed, 1)


def behind(g, j, lag, steps, rounds):
    if j - lag >= 0:
        return None if isinstance(g, int) and g == rounds else (g, j - lag)
    return None if isinstance(g, int) and g == 0 else (g - 1, j - lag + steps)


def walk_rounds(eng, step, last, steps, rounds):
    for j in range(steps):
        step(0, j, True)
    with eng.Fori(1, rounds) as g:
        for j in range(steps):
            step(g, j, True)
    for j in range(last):
        step(rounds, j, False)


def project(nc, ident, ones, neg_half, comb, x, ctxT, mask, WqT, bq, WkT, bk, WvT, bv,
            qh_d, ql_d, kh_d, kl_d, v_d, pos_d):
    NPJ = 3 * NC
    NPB = 4
    NTB = 3
    with ExitStack() as ctx:
        def sb(name, shape, dt=F32):
            return ctx.enter_context(nc.sbuf_tensor("p_" + name, shape, dt))

        def sem(name):
            return ctx.enter_context(nc.semaphore("p_" + name))

        x_raw = sb("x_raw", [P, NT, D])
        c_raw = sb("c_raw", [P, NC, S])
        m_raw = sb("m_raw", [P, NT, S], I32)
        raws = [x_raw[:, :, :], c_raw[:, :, :], m_raw[:, :, :].bitcast(F32)]
        w_h = [sb(f"w{n}_h", [P, NC, D], F32R) for n in "qkv"]
        w_l = [sb(f"w{n}_l", [P, NC, D], F32R) for n in "qkv"]
        xn = sb("xn", [P, NT, D])
        xT_h, xT_l = sb("xT_h", [P, NC, S], F32R), sb("xT_l", [P, NC, S], F32R)
        cT_h, cT_l = sb("cT_h", [P, NC, S], F32R), sb("cT_l", [P, NC, S], F32R)
        q_f = sb("q_f", [P, 2, S])
        v_f = sb("v_f", [P, 2, D])
        qk = [sb(n, [P, NC, S], F32R) for n in ("q_h", "q_l", "k_h", "k_l")]
        v_s = sb("v_s", [P, NT, H * VW], F32R)
        v_s4 = v_s[:, :, :].rearrange("p t (h w) -> p t h w", h=H)
        pos = sb("pos", [P, NT, S])
        pos_min = sb("pos_min", [P, NT])
        q_fac = sb("q_fac", [P, NT])
        fac_cols = sb("fac_cols", [P, NT, P])
        fac_row = sb("fac_row", [P, S])
        bq_c, bk_c = sb("bq_c", [P, NC]), sb("bk_c", [P, NC])
        bv_r = sb("bv_r", [P, D])
        stats = sb("stats", [P, NT, 6])
        mv = sb("mv", [P, NT, 2])
        var_e = sb("var_e", [P, NT])
        rstd = sb("rstd", [P, NT])

        ps_t = ctx.enter_context(nc.psum_tensor("p_ps_t", [P, NTB, S], F32))
        ps_j = ctx.enter_context(nc.psum_tensor("p_ps_j", [P, NPB, D], F32))
        ps_f = ctx.enter_context(nc.psum_tensor("p_ps_f", [P, S], F32))

        consts_made = sem("consts_made")
        consts_zeroed = sem("consts_zeroed")
        small_in = sem("small_in")
        x_in, c_in, m_in = sem("x_in"), sem("c_in"), sem("m_in")
        raw_in = [x_in, c_in, m_in]
        w_high, w_low = sem("w_high"), sem("w_low")
        pos_done, min_done, fac_done, cols_done = sem("pos_done"), sem("min_done"), sem("fac_done"), sem("cols_done")
        stats_done, mv_done, var_done, rstd_done, xn_done = (
            sem("stats_done"), sem("mv_done"), sem("var_done"), sem("rstd_done"), sem("xn_done"))
        x_turned, xT_high, xT_low = sem("x_turned"), sem("xT_high"), sem("xT_low")
        cT_high, cT_low = sem("cT_high"), sem("cT_low")
        fac_turned, fac_row_done = sem("fac_turned"), sem("fac_row_done")
        projected, bank_free = sem("projected"), sem("bank_free")
        qf_done, q_high, q_low = sem("qf_done"), sem("q_high"), sem("q_low")
        k_high = sem("k_high")
        vf_done, v_high, v_low = sem("vf_done"), sem("v_high"), sem("v_low")
        pos_out, qk_out, v_out = sem("pos_out"), sem("qk_out"), sem("v_out")
        v_ones = sem("v_ones")
        passed = sem("passed")

        block = ctx.enter_context(nc.Block())

        @block.sync
        def _(sp):
            for n, w in enumerate((WqT, WkT, WvT)):
                sp.dma_start(raws[n], tokens(w)).then_inc(raw_in[n], 16)
            sp.dma_start(bq_c[:, :], bq).then_inc(small_in, 16)
            sp.dma_start(bk_c[:, :], bk).then_inc(small_in, 16)
            sp.dma_start(bv_r[:, :], bv.rearrange("(a n) -> a n", a=1).broadcast_to([P, D])).then_inc(small_in, 16)
            sp.sem_inc(pos_out, 16)
            sp.sem_inc(qk_out, 64)
            sp.sem_inc(v_out, 16 * NC)

            def load(b, seen):
                sp.wait_ge(w_low, 3)
                if seen:
                    sp.wait_ge(xn_done, NT * b)
                    sp.wait_ge(x_in, 16 * b + 16)
                sp.dma_start(x_raw[:, :, :], tokens(x[b])).then_inc(x_in, 16)
                if seen:
                    sp.wait_ge(cT_low, b)
                sp.dma_start(c_raw[:, :, :], tokens(ctxT[b])).then_inc(c_in, 16)
                if seen:
                    sp.wait_ge(pos_done, b)
                sp.dma_start(m_raw[:, :, :], tokens(mask[b])).then_inc(m_in, 16)

            def store(b):
                sp.wait_ge(pos_done, b + 1)
                sp.dma_start(tokens(pos_d[b]), pos[:, :, :]).then_inc(pos_out, 16)
                sp.wait_ge(q_high, NC * (b + 1))
                sp.wait_ge(q_low, NC * (b + 1))
                for n, dst in ((0, qh_d), (1, ql_d)):
                    sp.dma_start(dst.rearrange("(c b) p n -> b p c n", c=NC)[b],
                                 qk[n][:, :, :].bitcast(F32)).then_inc(qk_out, 16)
                sp.wait_ge(bank_free, NPB + NPJ * b + 2 * NC)
                for n, dst in ((2, kh_d), (3, kl_d)):
                    sp.dma_start(dst.rearrange("(c b) p n -> b p c n", c=NC)[b],
                                 qk[n][:, :, :].bitcast(F32)).then_inc(qk_out, 16)
                sp.wait_ge(v_high, NT * (b + 1))
                sp.wait_ge(v_low, NT * (b + 1))
                for c in range(NC):
                    sp.dma_start(tokens(v_d[B * c + b]),
                                 v_s[:, :, c * HG * VW:(c + 1) * HG * VW].bitcast(F32)).then_inc(v_out, 16)

            load(0, False)
            with sp.Fori(0, B - 1) as b:
                load(b + 1, True)
                store(b)
            store(B - 1)
            sp.wait_ge(pos_out, 16 * (B + 1))
            sp.wait_ge(qk_out, 64 * (B + 1))
            sp.wait_ge(v_out, 16 * NC * (B + 1))

        @block.gpsimd
        def _(pool):
            pool.memset(ident[:, :], 0.0).then_inc(consts_zeroed, 1)
            pool.memset(comb[:, :], 0.0).then_inc(consts_zeroed, 1)
            pool.memset(ones[:, :], 1.0).then_inc(consts_made, 1)
            pool.memset(neg_half[:, :], -0.5).then_inc(consts_made, 1)
            pool.wait_ge(consts_zeroed, 2)
            pool.affine_select(out=ident[:, :], in_=ident[:, :], compare_op=ALU.not_equal, fill=1.0, base=0,
                               pattern=[[-1, P]], channel_multiplier=1).then_inc(consts_made, 1)
            pool.affine_select(out=comb[:, 0:DK], in_=comb[:, 0:DK], compare_op=ALU.not_equal, fill=1.0, base=0,
                               pattern=[[-1, DK]], channel_multiplier=1).then_inc(consts_zeroed, 1)
            pool.wait_ge(consts_zeroed, 3)
            pool.affine_select(out=comb[:, 0:DK], in_=comb[:, 0:DK], compare_op=ALU.not_equal, fill=1.0, base=-DK,
                               pattern=[[-1, DK]], channel_multiplier=1).then_inc(consts_made, 1)
            pool.affine_select(out=comb[:, DK:DK + 1], in_=comb[:, DK:DK + 1], compare_op=ALU.not_equal, fill=1.0,
                               base=-2 * DK, pattern=[[-1, 1]], channel_multiplier=1).then_inc(consts_made, 1)
            pool.wait_ge(consts_made, 5)
            with pool.Fori(0, B) as b:
                pool.wait_ge(var_done, b + 1)
                pool.tensor_tensor(out=rstd[:, :], in0=var_e[:, :], in1=neg_half[:, :], op=ALU.pow) \
                    .then_inc(rstd_done, 1)
                for c in range(NC):
                    pool.wait_ge(q_high, NC * b + c + 1)
                    pool.wait_ge(qk_out, 64 * (b + 1))
                    pool.tensor_tensor(out=qk[1][:, c, :], in0=q_f[:, c % 2, :], in1=qk[0][:, c, :].bitcast(F32),
                                       op=ALU.subtract).then_inc(q_low, 1)
                for t in range(NT):
                    pool.wait_ge(v_high, NT * b + t + 1)
                    pool.wait_ge(v_out, 16 * NC * (b + 1))
                    pool.tensor_tensor(
                        out=v_s4[:, t, :, DK:2 * DK],
                        in0=v_f[:, t % 2, :].rearrange("p (h d) -> p h d", h=H),
                        in1=v_s4[:, t, :, 0:DK].bitcast(F32), op=ALU.subtract).then_inc(v_low, 1)

        @block.vector
        def _(dve):
            dve.sem_inc(bank_free, NPB)
            dve.memset(v_s4[:, :, :, 2 * DK:2 * DK + 1].bitcast(F32), 1.0).then_inc(v_ones, 1)
            dve.memset(v_s4[:, :, :, 2 * DK + 1:VW].bitcast(F32), 0.0).then_inc(v_ones, 1)
            for n in range(3):
                dve.wait_ge(raw_in[n], 16)
                dve.tensor_copy(w_h[n][:, :, :], raws[n]).then_inc(w_high, 1)
                dve.wait_ge(w_high, n + 1)
                dve.tensor_tensor(out=w_l[n][:, :, :], in0=raws[n], in1=w_h[n][:, :, :].bitcast(F32),
                                  op=ALU.subtract).then_inc(w_low, 1)
            dve.wait_ge(consts_made, 5)
            dve.wait_ge(small_in, 48)
            with dve.Fori(0, B) as b:
                dve.wait_ge(x_in, 16 * b + 32)
                for t in range(NT):
                    dve.bn_stats(stats[:, t, :], x_raw[:, t, :]).then_inc(stats_done, 1)
                dve.wait_ge(stats_done, NT * (b + 1))
                gate(dve, passed)
                for t in range(NT):
                    dve.bn_aggr(mv[:, t, :], stats[:, t, :]).then_inc(mv_done, 1)
                dve.wait_ge(mv_done, NT * (b + 1))
                dve.tensor_scalar(var_e[:, :], mv[:, :, 1], LN_EPS, None, ALU.add).then_inc(var_done, 1)
                dve.wait_ge(m_in, 16 * b + 32)
                dve.wait_ge(pos_out, 16 * (b + 1))
                dve.tensor_scalar(pos[:, :, :], m_raw[:, :, :], 0.0, MASKED, ALU.is_equal, ALU.mult) \
                    .then_inc(pos_done, 1)
                dve.wait_ge(pos_done, b + 1)
                dve.tensor_reduce(pos_min[:, :], pos[:, :, :], AX_X, ALU.min).then_inc(min_done, 1)
                dve.wait_ge(min_done, b + 1)
                dve.tensor_scalar(q_fac[:, :], pos_min[:, :], 0.0, QSCALE, ALU.is_equal, ALU.mult) \
                    .then_inc(fac_done, 1)
                dve.wait_ge(fac_done, b + 1)
                for t in range(NT):
                    dve.tensor_scalar(fac_cols[:, t, :], ones[:, :], q_fac[:, t:t + 1], None, ALU.mult) \
                        .then_inc(cols_done, 1)
                dve.wait_ge(rstd_done, b + 1)
                for t in range(NT):
                    dve.tensor_scalar(xn[:, t, :], x_raw[:, t, :], mv[:, t, 0:1], rstd[:, t:t + 1],
                                      ALU.subtract, ALU.mult).then_inc(xn_done, 1)
                for c in range(NC):
                    dve.wait_ge(xT_high, NC * b + c + 1)
                    dve.tensor_tensor(out=xT_l[:, c, :], in0=ps_t[:, c % NTB, :], in1=xT_h[:, c, :].bitcast(F32),
                                      op=ALU.subtract).then_inc(xT_low, 1)
                dve.wait_ge(cT_high, b + 1)
                dve.tensor_tensor(out=cT_l[:, :, :], in0=c_raw[:, :, :], in1=cT_h[:, :, :].bitcast(F32),
                                  op=ALU.subtract).then_inc(cT_low, 1)
                dve.wait_ge(fac_row_done, b + 1)
                for c in range(NC):
                    n = NPJ * b + c
                    dve.wait_ge(projected, n + 1)
                    if c >= 2:
                        dve.wait_ge(q_low, NC * b + c - 1)
                    dve.scalar_tensor_tensor(out=q_f[:, c % 2, :], in0=ps_j[:, c % NPB, :], scalar=bq_c[:, c:c + 1],
                                             in1=fac_row[:, :], op0=ALU.add, op1=ALU.mult) \
                        .then_inc(bank_free, 1)
                for c in range(NC):
                    n = NC + c
                    dve.wait_ge(k_high, NC * b + c + 1)
                    dve.scalar_tensor_tensor(out=qk[3][:, c, :], in0=ps_j[:, n % NPB, :], scalar=bk_c[:, c:c + 1],
                                             in1=qk[2][:, c, :].bitcast(F32), op0=ALU.add, op1=ALU.subtract) \
                        .then_inc(bank_free, 1)
                for t in range(NT):
                    n = 2 * NC + t
                    dve.wait_ge(projected, NPJ * b + n + 1)
                    if t >= 2:
                        dve.wait_ge(v_low, NT * b + t - 1)
                    dve.tensor_tensor(out=v_f[:, t % 2, :], in0=ps_j[:, n % NPB, :], in1=bv_r[:, :], op=ALU.add) \
                        .then_inc(bank_free, 1)

        @block.scalar
        def _(act):
            act.wait_ge(small_in, 48)
            act.wait_ge(v_ones, 2)
            with act.Fori(0, B) as b:
                act.wait_ge(c_in, 16 * b + 32)
                act.activation(cT_h[:, :, :], c_raw[:, :, :], ACT.Copy).then_inc(cT_high, 1)
                act.wait_ge(fac_turned, b + 1)
                act.activation(fac_row[:, :], ps_f[:, :], ACT.Copy).then_inc(fac_row_done, 1)
                for c in range(NC):
                    act.wait_ge(x_turned, NC * b + c + 1)
                    act.activation(xT_h[:, c, :], ps_t[:, c % NTB, :], ACT.Copy).then_inc(xT_high, 1)
                act.wait_ge(qk_out, 64 * (b + 1))
                for c in range(NC):
                    act.wait_ge(bank_free, NPB + NPJ * b + c + 1)
                    act.activation(qk[0][:, c, :], q_f[:, c % 2, :], ACT.Copy).then_inc(q_high, 1)
                for c in range(NC):
                    n = NC + c
                    act.wait_ge(projected, NPJ * b + n + 1)
                    act.activation(qk[2][:, c, :], ps_j[:, n % NPB, :], ACT.Identity, bias=bk_c[:, c:c + 1]) \
                        .then_inc(k_high, 1)
                act.wait_ge(v_out, 16 * NC * (b + 1))
                for t in range(NT):
                    n = 2 * NC + t
                    act.wait_ge(bank_free, NPB + NPJ * b + n + 1)
                    act.activation(v_s4[:, t, :, 0:DK], v_f[:, t % 2, :].rearrange("p (h d) -> p h d", h=H),
                                   ACT.Copy).then_inc(v_high, 1)

        @block.tensor
        def _(pe):
            pe.wait_ge(w_low, 3)
            pe.wait_ge(consts_made, 5)
            with pe.Fori(0, B) as b:
                pe.wait_ge(cols_done, NT * (b + 1))
                for t in range(NT):
                    last = pe.matmul(ps_f[:, t * P:(t + 1) * P], fac_cols[:, t, :], ident[:, :], start=True, stop=True)
                last.then_inc(fac_turned, 1)
                pe.wait_ge(xn_done, NT * (b + 1))
                for c in range(NC):
                    if c >= NTB:
                        pe.wait_ge(xT_low, NC * b + c - NTB + 1)
                    for t in range(NT):
                        last = pe.transpose(ps_t[:, c % NTB, t * P:(t + 1) * P], xn[:, t, c * P:(c + 1) * P],
                                            ident[:, :])
                    last.then_inc(x_turned, 1)

                def product(n, pairs):
                    pe.wait_ge(bank_free, NPJ * b + n + 1)
                    for k, (w, m) in enumerate(pairs):
                        last = pe.matmul(ps_j[:, n % NPB, :], w, m, start=k == 0, stop=k == len(pairs) - 1)
                    last.then_inc(projected, 1)

                def features(w_h, w_l, a_h, a_l, c):
                    cs = slice(c * P, (c + 1) * P)
                    return [(w[:, k, cs], a[:, k, :]) for k in range(NC)
                            for w, a in ((w_h, a_h), (w_h, a_l), (w_l, a_h))]

                pe.wait_ge(xT_low, NC * (b + 1))
                for c in range(NC):
                    product(c, features(w_h[0], w_l[0], xT_h, xT_l, c))
                pe.wait_ge(cT_low, b + 1)
                for c in range(NC):
                    product(NC + c, features(w_h[1], w_l[1], cT_h, cT_l, c))
                for t in range(NT):
                    ts = slice(t * P, (t + 1) * P)
                    product(2 * NC + t, [(a[:, k, ts], w[:, k, :]) for k in range(NC)
                                         for a, w in ((cT_h, w_h[2]), (cT_h, w_l[2]), (cT_l, w_h[2]))])


def attend(nc, ident, comb, bias, qh_d, ql_d, kh_d, kl_d, v_d, pos_d, att_d):
    UR = 2 * NT
    TR = UR * HG
    ROUNDS = NC * B // 2
    NN = 8
    NE = 4
    NP = 4
    TURN, PV, COMB = 2, 4, 7
    HIGH, OUT = 1, 6
    LOW, NORM = 2, 7
    with ExitStack() as ctx:
        def sb(name, shape, dt=F32):
            return ctx.enter_context(nc.sbuf_tensor("a_" + name, shape, dt))

        def sem(name):
            return ctx.enter_context(nc.semaphore("a_" + name))

        q4 = sb("q4", [P, 2, HG, S], F32R)
        k4 = sb("k4", [P, 2, HG, S], F32R)
        v = sb("v", [P, 2, NT, HG * VW], F32R)
        pos = sb("pos", [P, 2, NT, S])
        bias_t = sb("bias_t", [P, NT, HG, S])
        nbm = sb("nbm", [P, NN, S])
        sc = sb("sc", [P, NE, S])
        nmax = sb("nmax", [P, NE])
        pr = sb("pr", [P, NE, S])
        pT_h, pT_l = sb("pT_h", [P, NP, S], F32R), sb("pT_l", [P, NP, S], F32R)
        o_sb = sb("o_sb", [2 * DK + 1, 2, HG * P])
        rsum = sb("rsum", [P, 2, HG])
        y = sb("y", [P, 2, HG * DK])

        ps_s = ctx.enter_context(nc.psum_tensor("a_ps_s", [P, 2, S], F32))
        ps_t = ctx.enter_context(nc.psum_tensor("a_ps_t", [P, 2, S], F32))
        ps_o = ctx.enter_context(nc.psum_tensor("a_ps_o", [P, 2, HG * P], F32))
        ps_c = ctx.enter_context(nc.psum_tensor("a_ps_c", [P, HG, DK + 1], F32))

        qkv_in = [sem("qkv_in0"), sem("qkv_in1")]
        pos_in = [sem("pos_in0"), sem("pos_in1")]
        bias_in = sem("bias_in")
        nbm_done = sem("nbm_done")
        scored, summed, exped, turned, high, low, pv_done = (
            sem("scored"), sem("summed"), sem("exped"), sem("turned"), sem("high"), sem("low"), sem("pv_done"))
        o_copied, combined, inverted, y_done = sem("o_copied"), sem("combined"), sem("inverted"), sem("y_done")
        y_out = [sem("y_out0"), sem("y_out1")]
        passed = sem("passed")

        NLD = 9

        def lagged(g, j, lag):
            return behind(g, j, lag, TR, ROUNDS)

        def walk(eng, step, last):
            walk_rounds(eng, step, last, TR, ROUNDS)

        block = ctx.enter_context(nc.Block())

        @block.sync
        def _(sp):
            def load(g, j):
                n = 2 * g + j
                for t, (q_d, k_d) in enumerate(((qh_d, kh_d), (qh_d, kl_d), (ql_d, kh_d), (ql_d, kl_d))):
                    rows = slice(DK * t, DK * (t + 1))
                    sp.dma_start(q4[rows, j, :, :].bitcast(F32), q_d[n].rearrange("(i p) n -> p i n", p=DK)) \
                        .then_inc(qkv_in[j], 16)
                    sp.dma_start(k4[rows, j, :, :].bitcast(F32), k_d[n].rearrange("(i p) n -> p i n", p=DK)) \
                        .then_inc(qkv_in[j], 16)
                sp.dma_start(v[:, j, :, :].bitcast(F32), tokens(v_d[n])).then_inc(qkv_in[j], 16)

            def load_pos(g, j):
                sp.dma_start(pos[:, j, :, :], tokens(pos_d[g % (B // 2) * 2 + j])).then_inc(pos_in[j], 16)

            def store(g, j):
                for qt in range(NT):
                    u = NT * j + qt
                    sp.wait_ge(y_done, UR * g + u + 1)
                    sp.dma_start(att_d[2 * g + j, qt * P:(qt + 1) * P, :], y[:, u % 2, :]).then_inc(y_out[u % 2], 16)

            for j in range(2):
                load_pos(0, j)
                load(0, j)
            sp.sem_inc(y_out[0], 16)
            sp.sem_inc(y_out[1], 16)
            with sp.Fori(0, ROUNDS - 1) as g:
                for j in range(2):
                    sp.wait_ge(nbm_done, TR * g + (j + 1) * NT * HG)
                    load_pos(g + 1, j)
                    store(g, j)
                    sp.wait_ge(pv_done, TR * g + (j + 1) * NT * HG)
                    load(g + 1, j)
            for j in range(2):
                store(ROUNDS - 1, j)
            for n in range(2):
                sp.wait_ge(y_out[n], 16 * (ROUNDS * UR // 2 + 1))

        @block.gpsimd
        def _(pool):
            def load_bias(hg):
                src = bias[0].rearrange("(c i) (t p) n -> c p t i n", c=NC, p=P)[hg]
                for t in range(NT):
                    pool.dma_start(bias_t[:, t, :, :], src[:, t, :, :]).then_inc(bias_in, 16)

            def group(hg):
                pool.wait_ge(bias_in, 16 * NT * (hg + 1))
                with pool.Fori(0, B // 2) as r:
                    g = hg * (B // 2) + r
                    for j in range(TR):
                        b, qt, i = j // (NT * HG), j // HG % NT, j % HG
                        if j % (NT * HG) == 0:
                            pool.wait_ge(pos_in[b], 16 * g + 16)
                        pool.wait_ge(summed, TR * g + j + 1)
                        pool.tensor_tensor(out=nbm[:, j % NN, :], in0=pos[:, b, qt, :], in1=bias_t[:, qt, i, :],
                                           op=ALU.subtract).then_inc(nbm_done, 1)

            load_bias(0)
            for hg in range(NC):
                group(hg)
                if hg < NC - 1:
                    pool.wait_ge(nbm_done, (hg + 1) * TR * B // 2)
                    load_bias(hg + 1)

        def tile(at):
            t = at[1]
            return t // (NT * HG), t // HG % NT, t % HG, t // HG

        @block.tensor
        def _(pe):
            def step(g, j, more):
                if more:
                    b, qt, i, _ = tile((g, j))
                    if j % (NT * HG) == 0:
                        pe.wait_ge(qkv_in[b], 16 * NLD * g + 16 * NLD)
                    need(pe, summed, NN + TR * g + j - 1 if lagged(g, j, 2) else 0)
                    pe.matmul(ps_s[:, j % 2, :], q4[:, b, i, qt * P:(qt + 1) * P], k4[:, b, i, :],
                              start=True, stop=True).then_inc(scored, 1)
                if at := lagged(g, j, TURN):
                    n = TR * at[0] + at[1]
                    need(pe, low, n - 1)
                    pe.wait_ge(exped, n + 1)
                    for kt in range(NT):
                        last = pe.transpose(ps_t[:, at[1] % 2, kt * P:(kt + 1) * P],
                                            pr[:, at[1] % NE, kt * P:(kt + 1) * P], ident[:, :])
                    last.then_inc(turned, 1)
                if at := lagged(g, j, PV):
                    n = TR * at[0] + at[1]
                    b, _, i, u = tile(at)
                    pe.wait_ge(low, n + 1)
                    if i == 0:
                        need(pe, o_copied, UR * at[0] + u - 1)
                    vt = v[:, b, :, :].rearrange("p t (h w) -> p t h w", h=HG)
                    for kt in range(NT):
                        for part in (pT_h, pT_l):
                            last = pe.matmul(ps_o[0:2 * DK + 1, u % 2, i * P:(i + 1) * P],
                                             vt[:, kt, i, 0:2 * DK + 1], part[:, at[1] % NP, kt * P:(kt + 1) * P],
                                             start=kt == 0 and part is pT_h, stop=kt == NT - 1 and part is pT_l)
                    last.then_inc(pv_done, 1)
                if (at := lagged(g, j, COMB)) and at[1] % HG == HG - 1:
                    u = at[1] // HG
                    pe.wait_ge(o_copied, UR * at[0] + u + 1)
                    need(pe, y_done, UR * at[0] + u)
                    for i in range(HG):
                        last = pe.matmul(ps_c[:, i, :], o_sb[:, u % 2, i * P:(i + 1) * P], comb[:, :],
                                         start=True, stop=True)
                    last.then_inc(combined, 1)

            walk(pe, step, COMB)

        @block.vector
        def _(dve):
            dve.sem_inc(summed, NN)

            def step(g, j, more):
                if more:
                    n = TR * g + j
                    dve.wait_ge(scored, n + 1)
                    dve.wait_ge(nbm_done, n + 1)
                    need(dve, exped, n - NE + 1)
                    gate(dve, passed)
                    dve.tensor_tensor_reduce(sc[:, j % NE, :], ps_s[:, j % 2, :], nbm[:, j % NN, :], 1.0, 3.0e38,
                                             ALU.add, ALU.min, nmax[:, j % NE:j % NE + 1]).then_inc(summed, 1)
                if at := lagged(g, j, LOW):
                    n = TR * at[0] + at[1]
                    dve.wait_ge(high, n + 1)
                    dve.tensor_tensor(out=pT_l[:, at[1] % NP, :], in0=ps_t[:, at[1] % 2, :],
                                      in1=pT_h[:, at[1] % NP, :].bitcast(F32), op=ALU.subtract).then_inc(low, 1)
                if (at := lagged(g, j, NORM)) and at[1] % HG == HG - 1:
                    u = at[1] // HG
                    n = UR * at[0] + u
                    dve.wait_ge(combined, n + 1)
                    dve.reciprocal(rsum[:, u % 2, :], ps_c[:, :, DK]).then_inc(inverted, 1)
                    dve.wait_ge(inverted, n + 1)
                    dve.wait_ge(y_out[u % 2], 8 * UR * at[0] + 16 * (u // 2) + 16)
                    for i in range(HG):
                        last = dve.tensor_scalar(y[:, u % 2, i * DK:(i + 1) * DK], ps_c[:, i, 0:DK],
                                                 rsum[:, u % 2, i:i + 1], None, ALU.mult)
                    last.then_inc(y_done, 1)

            walk(dve, step, NORM)

        @block.scalar
        def _(act):
            def step(g, j, more):
                if more:
                    n = TR * g + j
                    act.wait_ge(summed, NN + n + 1)
                    need(act, turned, n - NE + 1)
                    act.activation(pr[:, j % NE, :], sc[:, j % NE, :], ACT.Exp, scale=-1.0,
                                   bias=nmax[:, j % NE:j % NE + 1]).then_inc(exped, 1)
                if at := lagged(g, j, HIGH):
                    n = TR * at[0] + at[1]
                    act.wait_ge(turned, n + 1)
                    need(act, pv_done, n - NP + 1)
                    act.activation(pT_h[:, at[1] % NP, :], ps_t[:, at[1] % 2, :], ACT.Copy).then_inc(high, 1)
                if (at := lagged(g, j, OUT)) and at[1] % HG == HG - 1:
                    u = at[1] // HG
                    n = UR * at[0] + u
                    act.wait_ge(pv_done, TR * at[0] + at[1] + 1)
                    need(act, combined, n - 1)
                    act.activation(o_sb[:, u % 2, :], ps_o[0:2 * DK + 1, u % 2, :], ACT.Copy).then_inc(o_copied, 1)

            walk(act, step, OUT)


def mix(nc, ident, neg_half, x, att_d, WoT, bo, ln_g, ln_b, rWT, rb, rawU, rawV, gamma, part_d, zh_d, zl_d):
    with ExitStack() as ctx:
        def sb(name, shape, dt=F32):
            return ctx.enter_context(nc.sbuf_tensor("m_" + name, shape, dt))

        def sem(name):
            return ctx.enter_context(nc.semaphore("m_" + name))

        att = sb("att", [P, NT, D])
        x_in_t = sb("x_in_t", [P, NT, D])
        aT = [sb("aT_h", [P, NC, S], F32R), sb("aT_l", [P, NC, S], F32R)]
        zT = [sb("zT_h", [P, NC, S], F32R), sb("zT_l", [P, NC, S], F32R)]
        rT = [sb("rT_h", [P, NC, S], F32R), sb("rT_l", [P, NC, S], F32R)]
        hT = [sb("hT_h", [P, NL, S], F32R), sb("hT_l", [P, NL, S], F32R)]
        x1 = sb("x1", [P, NT, D])
        z = sb("z", [P, NT, D])
        rin = sb("rin", [P, NT, D])
        wo = [sb("wo_h", [P, NC, D], F32R), sb("wo_l", [P, NC, D], F32R)]
        rw = [sb("rw_h", [P, NC, NB], F32R), sb("rw_l", [P, NC, NB], F32R)]
        ut = [sb("ut_h", [P, NC, NB], F32R), sb("ut_l", [P, NC, NB], F32R)]
        vg = [sb("vg_h", [P, NL, D], F32R), sb("vg_l", [P, NL, D], F32R)]
        bo_r, g_r, b_r, gam_r = sb("bo_r", [P, D]), sb("g_r", [P, D]), sb("b_r", [P, D]), sb("gam_r", [P, D])
        rb_r = sb("rb_r", [P, NB])
        rc, hl = sb("rc", [P, NT, NB]), sb("hl", [P, NT, NB])
        top = sb("top", [P, NT, 8])
        sel = sb("sel", [P, NT, NB])
        e_u, e_d = sb("e_u", [P, NT, NB]), sb("e_d", [P, NT, NB])
        lnw = sb("lnw", [P, NT, NB])
        ssum, tanh_s, coef = sb("ssum", [P, NT]), sb("tanh_s", [P, NT]), sb("coef", [P, NT])
        stats, mv = sb("stats", [P, 2, NT, 6]), sb("mv", [P, 2, NT, 2])
        var_e, rstd = sb("var_e", [P, 2, NT]), sb("rstd", [P, 2, NT])
        nrm = sb("nrm", [P, 2 * NL])
        nrm_s = sb("nrm_s", [P, 2 * NL])
        nrm_r = sb("nrm_r", [P, 2 * NL])

        ps_t = ctx.enter_context(nc.psum_tensor("m_ps_t", [P, 2, S], F32))
        ps_o = ctx.enter_context(nc.psum_tensor("m_ps_o", [P, 4, D], F32))
        ps_r = ctx.enter_context(nc.psum_tensor("m_ps_r", [P, 2, 2, NB], F32))

        rows_in, w_in = sem("rows_in"), sem("w_in")
        lat_in, lat_sq, lat_root, lat_max, lat_inv, lat_unit, lat_gam, lat_turned = (
            sem(n) for n in ("lat_in", "lat_sq", "lat_root", "lat_max", "lat_inv", "lat_unit", "lat_gam", "lat_turned"))
        w_high, w_low = sem("w_high"), sem("w_low")
        att_in, x_in = sem("att_in"), sem("x_in")
        turned, t_high, t_low = sem("turned"), sem("t_high"), sem("t_low")
        o_ready, o_read = sem("o_ready"), sem("o_read")
        x1_half, x1_done = sem("x1_half"), sem("x1_done")
        stats_done, mv_done, var_done, rstd_done = (
            sem("stats_done"), sem("mv_done"), sem("var_done"), sem("rstd_done"))
        z_done, rz_done, rg_done, rin_done = sem("z_done"), sem("rz_done"), sem("rg_done"), sem("rin_done")
        r_ready, rb_done, hl_done, clip_done, top_done = (
            sem("r_ready"), sem("rb_done"), sem("hl_done"), sem("clip_done"), sem("top_done"))
        rep_done, sel_done, abs_done, u_done, d_done, w_done, err_done, sp_done, al_done = (
            sem(n) for n in ("rep_done", "sel_done", "abs_done", "u_done", "d_done", "w_done", "err_done",
                             "sp_done", "al_done"))
        sum_done, tanh_done, den_done, dinv_done, coef_done, hz_done = (
            sem(n) for n in ("sum_done", "tanh_done", "den_done", "dinv_done", "coef_done", "hz_done"))
        z_out, part_out = sem("z_out"), sem("part_out")
        passed = sem("passed")

        NTR = 3 * NC + NL
        NO = 2 * NT

        block = ctx.enter_context(nc.Block())

        @block.sync
        def _(sp):
            def row(v, n):
                return v.rearrange("(a n) -> a n", a=1).broadcast_to([P, n])

            sp.dma_start(att[:, :, :], tokens(WoT)).then_inc(w_in, 16)
            sp.dma_start(x_in_t[:, 0:2, :].rearrange("p t (s n) -> p (t s) n", n=NB), tokens(rWT)).then_inc(w_in, 16)
            sp.dma_start(z[:, 0:NL, :], tokens(rawU)).then_inc(lat_in, 16)
            sp.dma_start(z[:, NL:2 * NL, :], tokens(rawV)).then_inc(lat_in, 16)
            for dst, v, n in ((bo_r, bo, D), (g_r, ln_g, D), (b_r, ln_b, D), (gam_r, gamma, D), (rb_r, rb, NB)):
                sp.dma_start(dst[:, :], row(v, n)).then_inc(rows_in, 16)
            sp.sem_inc(z_out, 32)
            sp.sem_inc(part_out, 16)
            sp.wait_ge(w_low, 2)

            def load(b):
                for c in range(NC):
                    sp.dma_start(att[:, :, c * P:(c + 1) * P], tokens(att_d[B * c + b])).then_inc(att_in, 16)
                sp.dma_start(x_in_t[:, :, :], tokens(x[b])).then_inc(x_in, 16)

            def store(b):
                sp.wait_ge(t_high, NTR * b + 2 * NC)
                sp.wait_ge(t_low, NTR * b + 2 * NC)
                sp.dma_start(zh_d[b], zT[0][:, :, :].bitcast(F32)).then_inc(z_out, 16)
                sp.dma_start(zl_d[b], zT[1][:, :, :].bitcast(F32)).then_inc(z_out, 16)
                sp.wait_ge(o_read, 4 + NO * b + NO)
                sp.dma_start(tokens(part_d[b]), x1[:, :, :]).then_inc(part_out, 16)

            load(0)
            with sp.Fori(0, B - 1) as b:
                sp.wait_ge(turned, NTR * b + NC)
                sp.wait_ge(x1_done, NT * b + NT)
                load(b + 1)
                store(b)
            store(B - 1)
            sp.wait_ge(z_out, 32 * (B + 1))
            sp.wait_ge(part_out, 16 * (B + 1))

        @block.gpsimd
        def _(pool):
            with pool.Fori(0, B) as b:
                for n in range(2):
                    pool.wait_ge(var_done, 2 * b + n + 1)
                    pool.tensor_tensor(out=rstd[:, n, :], in0=var_e[:, n, :], in1=neg_half[:, :], op=ALU.pow) \
                        .then_inc(rstd_done, 1)
                for t in range(NT):
                    pool.wait_ge(rz_done, NT * b + t + 1)
                    pool.tensor_tensor(out=rin[:, t, :], in0=rin[:, t, :], in1=g_r[:, :], op=ALU.mult) \
                        .then_inc(rg_done, 1)
                    pool.wait_ge(rg_done, NT * b + t + 1)
                    pool.tensor_tensor(out=rin[:, t, :], in0=rin[:, t, :], in1=b_r[:, :], op=ALU.add) \
                        .then_inc(rin_done, 1)

        @block.vector
        def _(dve):
            dve.sem_inc(o_read, 4)

            def split(n, hi, lo, src):
                dve.tensor_copy(hi[:, :, :], src).then_inc(w_high, 1)
                dve.wait_ge(w_high, n + 1)
                dve.tensor_tensor(out=lo[:, :, :], in0=src, in1=hi[:, :, :].bitcast(F32), op=ALU.subtract) \
                    .then_inc(w_low, 1)

            dve.wait_ge(w_in, 32)
            dve.wait_ge(rows_in, 80)
            split(0, wo[0], wo[1], att[:, :, :])
            split(1, rw[0], rw[1], x_in_t[:, 0:2, :].rearrange("p t (s n) -> p (t s) n", n=NB))
            dve.wait_ge(lat_in, 32)
            for n in range(2 * NL):
                dve.tensor_tensor_reduce(rin[:, n, :], z[:, n, :], z[:, n, :], 1.0, 0.0, ALU.mult, ALU.add,
                                         nrm[:, n:n + 1]).then_inc(lat_sq, 1)
            dve.wait_ge(lat_root, 1)
            dve.tensor_scalar(nrm[:, :], nrm_s[:, :], UNIT_EPS, None, ALU.max).then_inc(lat_max, 1)
            dve.wait_ge(lat_max, 1)
            dve.reciprocal(nrm_r[:, :], nrm[:, :]).then_inc(lat_inv, 1)
            dve.wait_ge(lat_inv, 1)
            for n in range(2 * NL):
                dve.tensor_scalar(x1[:, n, :], z[:, n, :], nrm_r[:, n:n + 1], None, ALU.mult).then_inc(lat_unit, 1)
            dve.wait_ge(lat_unit, 2 * NL)
            for n in range(NL, 2 * NL):
                dve.tensor_tensor(out=rin[:, n, :], in0=x1[:, n, :], in1=gam_r[:, :], op=ALU.mult) \
                    .then_inc(lat_gam, 1)
            dve.wait_ge(lat_gam, NL)
            split(2, vg[0], vg[1], rin[:, NL:2 * NL, :])
            for h in range(2):
                dve.wait_ge(lat_turned, h + 1)
                src = ps_t[:, h, :].rearrange("p (c n) -> p c n", n=NB)
                dve.tensor_copy(ut[0][:, 2 * h:2 * h + 2, :], src).then_inc(w_high, 1)
                dve.wait_ge(w_high, 4 + h)
                dve.tensor_tensor(out=ut[1][:, 2 * h:2 * h + 2, :], in0=src,
                                  in1=ut[0][:, 2 * h:2 * h + 2, :].bitcast(F32), op=ALU.subtract).then_inc(w_low, 1)

            def low(b, k, dst, c):
                dve.wait_ge(t_high, NTR * b + k + 1)
                dve.tensor_tensor(out=dst[1][:, c, :], in0=ps_t[:, k % 2, :], in1=dst[0][:, c, :].bitcast(F32),
                                  op=ALU.subtract).then_inc(t_low, 1)

            with dve.Fori(0, B) as b:
                for c in range(NC):
                    low(b, c, aT, c)
                dve.wait_ge(x_in, 16 * b + 16)
                dve.wait_ge(part_out, 16 * b + 16)
                for t in range(NT):
                    dve.wait_ge(o_ready, NO * b + t + 1)
                    dve.tensor_tensor(out=x1[:, t, :], in0=ps_o[:, t, :], in1=bo_r[:, :], op=ALU.add) \
                        .then_inc(o_read, 1)
                dve.wait_ge(o_read, 4 + NO * b + NT)
                for t in range(NT):
                    dve.tensor_tensor(out=x1[:, t, :], in0=x1[:, t, :], in1=x_in_t[:, t, :], op=ALU.add) \
                        .then_inc(x1_done, 1)

                def norm(n, src, dst, done):
                    for t in range(NT):
                        dve.bn_stats(stats[:, n, t, :], src[:, t, :]).then_inc(stats_done, 1)
                    dve.wait_ge(stats_done, 2 * NT * b + (n + 1) * NT)
                    gate(dve, passed)
                    for t in range(NT):
                        dve.bn_aggr(mv[:, n, t, :], stats[:, n, t, :]).then_inc(mv_done, 1)
                    dve.wait_ge(mv_done, 2 * NT * b + (n + 1) * NT)
                    dve.tensor_scalar(var_e[:, n, :], mv[:, n, :, 1], LN_EPS, None, ALU.add).then_inc(var_done, 1)
                    dve.wait_ge(rstd_done, 2 * b + n + 1)
                    for t in range(NT):
                        dve.tensor_scalar(dst[:, t, :], src[:, t, :], mv[:, n, t, 0:1], rstd[:, n, t:t + 1],
                                          ALU.subtract, ALU.mult).then_inc(done, 1)

                dve.wait_ge(x1_done, NT * (b + 1))
                norm(0, x1, z, z_done)
                dve.wait_ge(z_done, NT * (b + 1))
                norm(1, z, rin, rz_done)
                for c in range(NC):
                    low(b, NC + c, zT, c)
                for c in range(NC):
                    low(b, 2 * NC + c, rT, c)
                for t in range(NT):
                    dve.wait_ge(r_ready, NT * b + t + 1)
                    dve.tensor_tensor(out=rc[:, t, :], in0=ps_r[:, t % 2, 0, :], in1=rb_r[:, :], op=ALU.add) \
                        .then_inc(rb_done, 1)
                    dve.tensor_copy(hl[:, t, :], ps_r[:, t % 2, 1, :]).then_inc(hl_done, 1)
                dve.wait_ge(rb_done, NT * (b + 1))
                dve.tensor_scalar(rc[:, :, :], rc[:, :, :], -TAU, TAU, ALU.max, ALU.min).then_inc(clip_done, 1)
                dve.wait_ge(clip_done, b + 1)
                dve.scalar_tensor_tensor(out=e_d[:, :, :], in0=rc[:, :, :], scalar=-1.0, in1=rc[:, :, :],
                                         op0=ALU.mult, op1=ALU.max).then_inc(abs_done, 1)
                for t in range(NT):
                    dve.max(top[:, t, :], rc[:, t, :]).then_inc(top_done, 1)
                dve.wait_ge(top_done, NT * (b + 1))
                gate(dve, passed)
                for t in range(NT):
                    dve.match_replace(sel[:, t, :], top[:, t, :], rc[:, t, :], -1.0e30).then_inc(rep_done, 1)
                dve.wait_ge(rep_done, NT * (b + 1))
                dve.tensor_tensor(out=sel[:, :, :], in0=sel[:, :, :], in1=rc[:, :, :], op=ALU.not_equal) \
                    .then_inc(sel_done, 1)
                dve.wait_ge(u_done, b + 1)
                dve.tensor_scalar(e_d[:, :, :], e_u[:, :, :], 1.0, 1.0, ALU.add, ALU.subtract).then_inc(d_done, 1)
                dve.wait_ge(d_done, b + 1)
                dve.wait_ge(w_done, b + 1)
                dve.tensor_tensor(out=e_u[:, :, :], in0=e_u[:, :, :], in1=e_d[:, :, :], op=ALU.subtract) \
                    .then_inc(err_done, 1)
                dve.wait_ge(err_done, b + 1)
                dve.scalar_tensor_tensor(out=e_u[:, :, :], in0=rc[:, :, :], scalar=0.0, in1=e_u[:, :, :],
                                         op0=ALU.max, op1=ALU.add).then_inc(sp_done, 1)
                dve.wait_ge(sp_done, b + 1)
                dve.tensor_tensor(out=e_u[:, :, :], in0=e_u[:, :, :], in1=lnw[:, :, :], op=ALU.add) \
                    .then_inc(al_done, 1)
                dve.wait_ge(al_done, b + 1)
                dve.wait_ge(sel_done, b + 1)
                for t in range(NT):
                    dve.tensor_tensor_reduce(sel[:, t, :], e_u[:, t, :], sel[:, t, :], 1.0, 0.0, ALU.mult, ALU.add,
                                             ssum[:, t:t + 1]).then_inc(sum_done, 1)
                dve.wait_ge(sum_done, NT * (b + 1))
                dve.tensor_scalar(coef[:, :], ssum[:, :], UNIT_EPS, None, ALU.add).then_inc(den_done, 1)
                dve.wait_ge(den_done, b + 1)
                dve.reciprocal(coef[:, :], coef[:, :]).then_inc(dinv_done, 1)
                dve.wait_ge(dinv_done, b + 1)
                dve.wait_ge(tanh_done, b + 1)
                dve.tensor_tensor(out=coef[:, :], in0=coef[:, :], in1=tanh_s[:, :], op=ALU.mult).then_inc(coef_done, 1)
                dve.wait_ge(coef_done, b + 1)
                dve.wait_ge(hl_done, NT * (b + 1))
                for t in range(NT):
                    dve.scalar_tensor_tensor(out=hl[:, t, :], in0=sel[:, t, :], scalar=coef[:, t:t + 1],
                                             in1=hl[:, t, :], op0=ALU.mult, op1=ALU.mult).then_inc(hz_done, 1)
                for c in range(NL):
                    low(b, 3 * NC + c, hT, c)
                for t in range(NT):
                    dve.wait_ge(o_ready, NO * b + NT + t + 1)
                    dve.tensor_tensor(out=x1[:, t, :], in0=ps_o[:, t, :], in1=x1[:, t, :], op=ALU.add) \
                        .then_inc(o_read, 1)

        @block.scalar
        def _(act):
            act.wait_ge(lat_sq, 2 * NL)
            act.activation(nrm_s[:, :], nrm[:, :], ACT.Sqrt).then_inc(lat_root, 1)

            def high(b, k, dst, c):
                act.wait_ge(turned, NTR * b + k + 1)
                act.activation(dst[0][:, c, :], ps_t[:, k % 2, :], ACT.Copy).then_inc(t_high, 1)

            with act.Fori(0, B) as b:
                for c in range(NC):
                    high(b, c, aT, c)
                act.wait_ge(z_out, 32 * b + 32)
                for c in range(NC):
                    high(b, NC + c, zT, c)
                for c in range(NC):
                    high(b, 2 * NC + c, rT, c)
                act.wait_ge(abs_done, b + 1)
                act.activation(e_u[:, :, :], e_d[:, :, :], ACT.Exp, scale=-1.0).then_inc(u_done, 1)
                act.wait_ge(u_done, b + 1)
                act.activation(lnw[:, :, :], e_u[:, :, :], ACT.Ln, bias=1.0).then_inc(w_done, 1)
                act.wait_ge(sum_done, NT * (b + 1))
                act.activation(tanh_s[:, :], ssum[:, :], ACT.Tanh).then_inc(tanh_done, 1)
                for c in range(NL):
                    high(b, 3 * NC + c, hT, c)

        @block.tensor
        def _(pe):
            pe.wait_ge(lat_unit, 2 * NL)
            for c in range(NC):
                for n in range(NL):
                    last = pe.transpose(ps_t[:, c // 2, (c % 2 * NL + n) * P:(c % 2 * NL + n + 1) * P],
                                        x1[:, n, c * P:(c + 1) * P], ident[:, :])
                if c % 2:
                    last.then_inc(lat_turned, 1)
            pe.wait_ge(w_low, 5)

            def turn(b, k, src, c):
                if k >= 2:
                    pe.wait_ge(t_low, NTR * b + k - 1)
                for t in range(NT):
                    last = pe.transpose(ps_t[:, k % 2, t * P:(t + 1) * P], src[:, t, c * P:(c + 1) * P], ident[:, :])
                last.then_inc(turned, 1)

            def sums(dst, a, w, n):
                passes = [(a[x_][:, k, :], w[y_][:, k, :]) for k in range(n) for x_, y_ in ((0, 0), (0, 1), (1, 0))]
                for m, (s_, t_) in enumerate(passes):
                    last = pe.matmul(dst, s_, t_, start=m == 0, stop=m == len(passes) - 1)
                return last

            def of_tile(pair, t):
                return [a[:, :, t * P:(t + 1) * P] for a in pair]

            with pe.Fori(0, B) as b:
                pe.wait_ge(att_in, 16 * NC * (b + 1))
                for c in range(NC):
                    turn(b, c, att, c)
                pe.wait_ge(t_low, NTR * b + NC)
                for t in range(NT):
                    pe.wait_ge(o_read, NO * b + t + 1)
                    sums(ps_o[:, t, :], of_tile(aT, t), wo, NC).then_inc(o_ready, 1)
                pe.wait_ge(z_done, NT * (b + 1))
                for c in range(NC):
                    turn(b, NC + c, z, c)
                pe.wait_ge(rin_done, NT * (b + 1))
                for c in range(NC):
                    turn(b, 2 * NC + c, rin, c)
                pe.wait_ge(t_low, NTR * b + 3 * NC)
                for t in range(NT):
                    if t >= 2:
                        pe.wait_ge(hl_done, NT * b + t - 1)
                    sums(ps_r[:, t % 2, 0, :], of_tile(rT, t), rw, NC)
                    sums(ps_r[:, t % 2, 1, :], of_tile(zT, t), ut, NC).then_inc(r_ready, 1)
                pe.wait_ge(hz_done, NT * (b + 1))
                for c in range(NL):
                    turn(b, 3 * NC + c, hl, c)
                pe.wait_ge(t_low, NTR * b + NTR)
                for t in range(NT):
                    pe.wait_ge(o_read, NO * b + NT + t + 1)
                    sums(ps_o[:, t, :], of_tile(hT, t), vg, NL).then_inc(o_ready, 1)


def feed(nc, W1T, W2T, zh_d, zl_d, part_d, out):
    LAG = 2
    NG = 4
    STEPS = 2 * NF
    ROUNDS = B // 2
    with ExitStack() as ctx:
        def sb(name, shape, dt=F32):
            return ctx.enter_context(nc.sbuf_tensor("f_" + name, shape, dt))

        def sem(name):
            return ctx.enter_context(nc.semaphore("f_" + name))

        w1 = [sb("w1_h", [P, NC, FF], F32R), sb("w1_l", [P, NC, FF], F32R)]
        w2 = [sb("w2_h", [P, NF, D], F32R), sb("w2_l", [P, NF, D], F32R)]
        zT = [sb("zT_h", [P, 2, NC, S], F32R), sb("zT_l", [P, 2, NC, S], F32R)]
        part = sb("part", [P, NT, D])
        y = sb("y", [P, NT, D])
        g_f = sb("g_f", [P, NG, S])
        g_h, g_l = sb("g_h", [P, NG, S], F32R), sb("g_l", [P, NG, S], F32R)
        ps_h = ctx.enter_context(nc.psum_tensor("f_ps_h", [P, NG, S], F32))
        ps_y = ctx.enter_context(nc.psum_tensor("f_ps_y", [P, NT, D], F32))

        stage_in = [sem("stage_in0"), sem("stage_in1")]
        w_high, w_low = sem("w_high"), sem("w_low")
        z_in = [sem("z_in0"), sem("z_in1")]
        part_in = sem("part_in")
        hidden, gelu_done, g_high, g_low, g_used = (
            sem("hidden"), sem("gelu_done"), sem("g_high"), sem("g_low"), sem("g_used"))
        y_done, y_out = sem("y_done"), sem("y_out")

        pieces = [(W1T[c * P:(c + 1) * P, :], w1, c) for c in range(NC)] + \
                 [(tokens(W2T[n * 4 * P:(n + 1) * 4 * P, :]), w2, n) for n in range(NF // 4)]
        stages = [part, y]

        def staged(n):
            ap = stages[n % 2][:, :, :]
            return ap.rearrange("p k n -> p (k n)") if pieces[n][1] is w1 else ap

        def placed(n, w):
            _, kind, m = pieces[n]
            return w[:, m, :] if kind is w1 else w[:, 4 * m:4 * m + 4, :]

        block = ctx.enter_context(nc.Block())

        @block.sync
        def _(sp):
            for n, (src, _, _) in enumerate(pieces):
                need(sp, w_low, n - 1)
                sp.dma_start(staged(n), src).then_inc(stage_in[n % 2], 16)
            sp.wait_ge(w_low, len(pieces))
            sp.sem_inc(y_out, 16)

            def load(g, j):
                for h, z_d in enumerate((zh_d, zl_d)):
                    sp.dma_start(zT[h][:, j, :, :].bitcast(F32), z_d[2 * g + j]).then_inc(z_in[j], 16)

            def load_part(b):
                sp.dma_start(part[:, :, :], tokens(part_d[b])).then_inc(part_in, 16)

            def store(b):
                sp.wait_ge(y_done, NT * (b + 1))
                sp.dma_start(tokens(out[b]), y[:, :, :]).then_inc(y_out, 16)

            load(0, 0)
            load(0, 1)
            load_part(0)
            with sp.Fori(0, ROUNDS - 1) as g:
                for j in range(2):
                    sp.wait_ge(hidden, STEPS * g + (j + 1) * NF)
                    load(g + 1, j)
                    store(2 * g + j)
                    load_part(2 * g + j + 1)
            store(B - 2)
            load_part(B - 1)
            store(B - 1)
            sp.wait_ge(y_out, 16 * (B + 1))

        @block.gpsimd
        def _(pool):
            pool.sem_inc(g_low, NG)
            with pool.Fori(0, B * NF // NG) as r:
                for k in range(NG):
                    pool.wait_ge(g_high, NG * r + k + 1)
                    pool.tensor_tensor(out=g_l[:, k, :], in0=g_f[:, k, :], in1=g_h[:, k, :].bitcast(F32),
                                       op=ALU.subtract).then_inc(g_low, 1)

        @block.scalar
        def _(act):
            act.sem_inc(gelu_done, NG)
            with act.Fori(0, B * NF // NG) as r:
                for k in range(NG):
                    act.wait_ge(hidden, NG * r + k + 1)
                    act.wait_ge(g_low, NG * r + k + 1)
                    act.activation(g_f[:, k, :], ps_h[:, k, :], ACT.Gelu).then_inc(gelu_done, 1)

        @block.vector
        def _(dve):
            for n in range(len(pieces)):
                kind = pieces[n][1]
                dve.wait_ge(stage_in[n % 2], 16 * (n // 2 + 1))
                dve.tensor_copy(placed(n, kind[0]), staged(n)).then_inc(w_high, 1)
                dve.wait_ge(w_high, n + 1)
                dve.tensor_tensor(out=placed(n, kind[1]), in0=staged(n), in1=placed(n, kind[0]).bitcast(F32),
                                  op=ALU.subtract).then_inc(w_low, 1)

            def step(g, j, more):
                if more:
                    n = STEPS * g + j
                    dve.wait_ge(gelu_done, NG + n + 1)
                    need(dve, g_used, n - NG + 1)
                    dve.tensor_copy(g_h[:, j % NG, :], g_f[:, j % NG, :]).then_inc(g_high, 1)
                if (at := behind(g, j, LAG + 1, STEPS, ROUNDS)) and at[1] % NF == NF - 1:
                    b = 2 * at[0] + at[1] // NF
                    dve.wait_ge(part_in, 16 * b + 16)
                    dve.wait_ge(y_out, 16 * b + 16)
                    dve.wait_ge(g_used, STEPS * at[0] + at[1] + 1)
                    for t in range(NT):
                        dve.tensor_tensor(out=y[:, t, :], in0=ps_y[:, t, :], in1=part[:, t, :], op=ALU.add) \
                            .then_inc(y_done, 1)

            walk_rounds(dve, step, LAG + 1, STEPS, ROUNDS)

        @block.tensor
        def _(pe):
            pe.wait_ge(w_low, len(pieces))

            def step(g, j, more):
                if more:
                    b, f = j // NF, j % NF
                    fs = slice(f * P, (f + 1) * P)
                    if f == 0:
                        pe.wait_ge(z_in[b], 32 * g + 32)
                    pe.wait_ge(gelu_done, STEPS * g + j + 1)
                    passes = [(w1[x][:, k, fs], zT[y][:, b, k, :]) for k in range(NC) for x, y in PASSES]
                    for m, (w, a) in enumerate(passes):
                        last = pe.matmul(ps_h[:, j % NG, :], w, a, start=m == 0, stop=m == len(passes) - 1)
                    last.then_inc(hidden, 1)
                if at := behind(g, j, LAG, STEPS, ROUNDS):
                    n = STEPS * at[0] + at[1]
                    b, f = 2 * at[0] + at[1] // NF, at[1] % NF
                    pe.wait_ge(g_low, NG + n + 1)
                    for t in range(NT):
                        if f == 0:
                            need(pe, y_done, NT * (b - 1) + t + 1)
                        gs = [a[:, at[1] % NG, t * P:(t + 1) * P] for a in (g_h, g_l)]
                        for m, (x, y) in enumerate(PASSES):
                            last = pe.matmul(ps_y[:, t, :], gs[x], w2[y][:, f, :],
                                             start=f == 0 and m == 0, stop=f == NF - 1 and m == 2)
                    last.then_inc(g_used, 1)

            walk_rounds(pe, step, LAG, STEPS, ROUNDS)


INPUTS = ("x", "ctxT", "bias", "mask", "WqT", "bq", "WkT", "bk", "WvT", "bv", "WoT", "bo", "W1T", "W2T",
          "ln_g", "ln_b", "rWT", "rb", "rawU", "rawV", "gamma")


def kernel(x, ctx_1024, fside_1x16xSxS2_0, mask_Bx1xSxS2_ik1, L0_xattn_Wq, L0_xattn_bq, L0_xattn_Wk, L0_xattn_bk,
           L0_xattn_Wv, L0_xattn_bv, L0_xattn_Wo, L0_xattn_bo, L0_ffn_W1, L0_ffn_W2, L0_ffn_ln_g, L0_ffn_ln_b,
           L0_ffn_router_W, L0_ffn_router_b, L0_ffn_raw_U, L0_ffn_raw_V, L0_ffn_gamma):
    import numpy as np
    import concourse.bacc as bacc
    from concourse.bass_utils import run_bass_kernel_spmd

    given = {
        "x": x, "ctxT": np.asarray(ctx_1024).transpose(0, 2, 1), "bias": fside_1x16xSxS2_0,
        "mask": np.asarray(mask_Bx1xSxS2_ik1)[:, 0],
        "WqT": np.asarray(L0_xattn_Wq).T, "bq": np.asarray(L0_xattn_bq).reshape(NC, P).T, "WkT": np.asarray(L0_xattn_Wk).T, "bk": np.asarray(L0_xattn_bk).reshape(NC, P).T,
        "WvT": np.asarray(L0_xattn_Wv).T, "bv": L0_xattn_bv, "WoT": np.asarray(L0_xattn_Wo).T, "bo": L0_xattn_bo,
        "W1T": np.asarray(L0_ffn_W1).T, "W2T": np.asarray(L0_ffn_W2).T, "ln_g": L0_ffn_ln_g, "ln_b": L0_ffn_ln_b,
        "rWT": np.asarray(L0_ffn_router_W).T, "rb": L0_ffn_router_b, "rawU": L0_ffn_raw_U, "rawV": L0_ffn_raw_V,
        "gamma": np.asarray(L0_ffn_gamma).reshape(-1),
    }
    nc = bacc.Bacc("TRN2", target_bir_lowering=False, num_devices=1)
    arrays, aps = {}, []
    for name in INPUTS:
        a = np.ascontiguousarray(given[name])
        arrays["in_" + name] = a
        aps.append(nc.dram_tensor("in_" + name, a.shape, mybir.dt.from_np(a.dtype), kind="ExternalInput").ap())
    out = nc.dram_tensor("out_x", (B, S, D), F32, kind="ExternalOutput").ap()
    build(nc, *aps, out)
    result = run_bass_kernel_spmd(nc, [arrays], core_ids=[0])
    return result.results[0]["out_x"]
```

```python
from contextlib import ExitStack

import concourse.bass as bass
from concourse import mybir

P = 128
F32 = mybir.dt.float32
F32R = mybir.dt.float32r
I32 = mybir.dt.int32
ALU = mybir.AluOpType
ACT = mybir.ActivationFunctionType
AX_X = mybir.AxisListType.X

PASSES = ((0, 0), (0, 1), (1, 0))

B, S, D, H = 8, 512, 512, 16
DK = D // H
NT = S // P
NC = D // P
HG = P // DK
VW = 2 * DK + 2
FF = 2048
NF = FF // P
NB = 256
NL = NB // P
LN_EPS = 1e-5
UNIT_EPS = 1e-6
TAU = 10.0
MASKED = 1.0e9
QSCALE = -1.0 / float(DK) ** 0.5


def build(nc, x, ctxT, bias, mask, WqT, bq, WkT, bk, WvT, bv, WoT, bo, W1T, W2T,
          ln_g, ln_b, rWT, rb, rawU, rawV, gamma, out):
    qh_d, ql_d, kh_d, kl_d = (
        nc.dram_tensor(n, (NC * B, P, S), F32, kind="Internal").ap() for n in ("qh_d", "ql_d", "kh_d", "kl_d"))
    v_d = nc.dram_tensor("v_d", (NC * B, S, HG * VW), F32, kind="Internal").ap()
    pos_d = nc.dram_tensor("pos_d", (B, S, S), F32, kind="Internal").ap()
    att_d = nc.dram_tensor("att_d", (NC * B, S, P), F32, kind="Internal").ap()
    part_d = nc.dram_tensor("part_d", (B, S, D), F32, kind="Internal").ap()
    zh_d, zl_d = (nc.dram_tensor(n, (B, P, NC, S), F32, kind="Internal").ap() for n in ("zh_d", "zl_d"))

    with ExitStack() as top:
        ident = top.enter_context(nc.sbuf_tensor("ident", [P, P], F32))
        ones = top.enter_context(nc.sbuf_tensor("ones", [P, P], F32))
        neg_half = top.enter_context(nc.sbuf_tensor("neg_half", [P, NT], F32))
        project(nc, ident, ones, neg_half, x, ctxT, mask, WqT, bq, WkT, bk, WvT, bv,
                qh_d, ql_d, kh_d, kl_d, v_d, pos_d)
        attend(nc, ident, bias, qh_d, ql_d, kh_d, kl_d, v_d, pos_d, att_d)
        mix(nc, ident, ones, neg_half, x, att_d, WoT, bo, ln_g, ln_b, rWT, rb, rawU, rawV, gamma,
            part_d, zh_d, zl_d)
        feed(nc, W1T, W2T, zh_d, zl_d, part_d, out)


def tokens(ap):
    return ap.rearrange("(t p) n -> p t n", p=P)


def need(eng, semaphore, count):
    if not isinstance(count, int) or count > 0:
        eng.wait_ge(semaphore, count)


def gate(eng, passed):
    eng.sem_inc(passed, 1)


def behind(g, j, lag, steps, rounds):
    if j - lag >= 0:
        return None if isinstance(g, int) and g == rounds else (g, j - lag)
    return None if isinstance(g, int) and g == 0 else (g - 1, j - lag + steps)


def walk_rounds(eng, step, last, steps, rounds):
    for j in range(steps):
        step(0, j, True)
    with eng.Fori(1, rounds) as g:
        for j in range(steps):
            step(g, j, True)
    for j in range(last):
        step(rounds, j, False)


def project(nc, ident, ones, neg_half, x, ctxT, mask, WqT, bq, WkT, bk, WvT, bv,
            qh_d, ql_d, kh_d, kl_d, v_d, pos_d):
    NPJ = 3 * NC
    NPB = 4
    NTB = 3
    with ExitStack() as ctx:
        def sb(name, shape, dt=F32):
            return ctx.enter_context(nc.sbuf_tensor("p_" + name, shape, dt))

        def sem(name):
            return ctx.enter_context(nc.semaphore("p_" + name))

        x_raw = sb("x_raw", [P, NT, D])
        c_raw = sb("c_raw", [P, NC, S])
        m_raw = sb("m_raw", [P, NT, S], I32)
        raws = [x_raw[:, :, :], c_raw[:, :, :], m_raw[:, :, :].bitcast(F32)]
        w_h = [sb(f"w{n}_h", [P, NC, D], F32R) for n in "qkv"]
        w_l = [sb(f"w{n}_l", [P, NC, D], F32R) for n in "qkv"]
        xn = sb("xn", [P, NT, D])
        xT_h, xT_l = sb("xT_h", [P, NC, S], F32R), sb("xT_l", [P, NC, S], F32R)
        cT_h, cT_l = sb("cT_h", [P, NC, S], F32R), sb("cT_l", [P, NC, S], F32R)
        q_f = sb("q_f", [P, 2, S])
        v_f = sb("v_f", [P, 2, D])
        qk = [sb(n, [P, NC, S], F32R) for n in ("q_h", "q_l", "k_h", "k_l")]
        v_s = sb("v_s", [P, NT, H * VW], F32R)
        v_s4 = v_s[:, :, :].rearrange("p t (h w) -> p t h w", h=H)
        pos = sb("pos", [P, NT, S])
        pos_min = sb("pos_min", [P, NT])
        q_fac = sb("q_fac", [P, NT])
        fac_cols = sb("fac_cols", [P, NT, P])
        fac_row = sb("fac_row", [P, S])
        bq_c, bk_c = sb("bq_c", [P, NC]), sb("bk_c", [P, NC])
        bv_r = sb("bv_r", [P, D])
        stats = sb("stats", [P, NT, 6])
        mv = sb("mv", [P, NT, 2])
        var_e = sb("var_e", [P, NT])
        rstd = sb("rstd", [P, NT])

        ps_t = ctx.enter_context(nc.psum_tensor("p_ps_t", [P, NTB, S], F32))
        ps_j = ctx.enter_context(nc.psum_tensor("p_ps_j", [P, NPB, D], F32))
        ps_f = ctx.enter_context(nc.psum_tensor("p_ps_f", [P, S], F32))

        consts_made = sem("consts_made")
        consts_zeroed = sem("consts_zeroed")
        small_in = sem("small_in")
        x_in, c_in, m_in = sem("x_in"), sem("c_in"), sem("m_in")
        raw_in = [x_in, c_in, m_in]
        w_high, w_low = sem("w_high"), sem("w_low")
        pos_done, min_done, fac_done, cols_done = sem("pos_done"), sem("min_done"), sem("fac_done"), sem("cols_done")
        stats_done, mv_done, var_done, rstd_done, xn_done = (
            sem("stats_done"), sem("mv_done"), sem("var_done"), sem("rstd_done"), sem("xn_done"))
        x_turned, xT_high, xT_low = sem("x_turned"), sem("xT_high"), sem("xT_low")
        cT_high, cT_low = sem("cT_high"), sem("cT_low")
        fac_turned, fac_row_done = sem("fac_turned"), sem("fac_row_done")
        projected, bank_free = sem("projected"), sem("bank_free")
        qf_done, q_high, q_low = sem("qf_done"), sem("q_high"), sem("q_low")
        k_high = sem("k_high")
        vf_done, v_high, v_low = sem("vf_done"), sem("v_high"), sem("v_low")
        pos_out, qk_out, v_out = sem("pos_out"), sem("qk_out"), sem("v_out")
        v_ones = sem("v_ones")
        passed = sem("passed")

        block = ctx.enter_context(nc.Block())

        @block.sync
        def _(sp):
            for n, w in enumerate((WqT, WkT, WvT)):
                sp.dma_start(raws[n], tokens(w)).then_inc(raw_in[n], 16)
            sp.dma_start(bq_c[:, :], bq).then_inc(small_in, 16)
            sp.dma_start(bk_c[:, :], bk).then_inc(small_in, 16)
            sp.dma_start(bv_r[:, :], bv.rearrange("(a n) -> a n", a=1).broadcast_to([P, D])).then_inc(small_in, 16)
            sp.sem_inc(pos_out, 16)
            sp.sem_inc(qk_out, 64)
            sp.sem_inc(v_out, 16 * NC)

            def load(b, seen):
                sp.wait_ge(w_low, 3)
                if seen:
                    sp.wait_ge(xn_done, NT * b)
                    sp.wait_ge(x_in, 16 * b + 16)
                sp.dma_start(x_raw[:, :, :], tokens(x[b])).then_inc(x_in, 16)
                if seen:
                    sp.wait_ge(cT_low, b)
                sp.dma_start(c_raw[:, :, :], tokens(ctxT[b])).then_inc(c_in, 16)
                if seen:
                    sp.wait_ge(pos_done, b)
                sp.dma_start(m_raw[:, :, :], tokens(mask[b])).then_inc(m_in, 16)

            def store(b):
                sp.wait_ge(pos_done, b + 1)
                sp.dma_start(tokens(pos_d[b]), pos[:, :, :]).then_inc(pos_out, 16)
                sp.wait_ge(q_high, NC * (b + 1))
                sp.wait_ge(q_low, NC * (b + 1))
                for n, dst in ((0, qh_d), (1, ql_d)):
                    sp.dma_start(dst.rearrange("(c b) p n -> b p c n", c=NC)[b],
                                 qk[n][:, :, :].bitcast(F32)).then_inc(qk_out, 16)
                sp.wait_ge(bank_free, NPB + NPJ * b + 2 * NC)
                for n, dst in ((2, kh_d), (3, kl_d)):
                    sp.dma_start(dst.rearrange("(c b) p n -> b p c n", c=NC)[b],
                                 qk[n][:, :, :].bitcast(F32)).then_inc(qk_out, 16)
                sp.wait_ge(v_high, NT * (b + 1))
                sp.wait_ge(v_low, NT * (b + 1))
                for c in range(NC):
                    sp.dma_start(tokens(v_d[B * c + b]),
                                 v_s[:, :, c * HG * VW:(c + 1) * HG * VW].bitcast(F32)).then_inc(v_out, 16)

            load(0, False)
            with sp.Fori(0, B - 1) as b:
                load(b + 1, True)
                store(b)
            store(B - 1)
            sp.wait_ge(pos_out, 16 * (B + 1))
            sp.wait_ge(qk_out, 64 * (B + 1))
            sp.wait_ge(v_out, 16 * NC * (B + 1))

        @block.gpsimd
        def _(pool):
            pool.memset(ident[:, :], 0.0).then_inc(consts_zeroed, 1)
            pool.memset(ones[:, :], 1.0).then_inc(consts_made, 1)
            pool.memset(neg_half[:, :], -0.5).then_inc(consts_made, 1)
            pool.wait_ge(consts_zeroed, 1)
            pool.affine_select(out=ident[:, :], in_=ident[:, :], compare_op=ALU.not_equal, fill=1.0, base=0,
                               pattern=[[-1, P]], channel_multiplier=1).then_inc(consts_made, 1)
            pool.wait_ge(consts_made, 3)
            with pool.Fori(0, B) as b:
                pool.wait_ge(var_done, b + 1)
                pool.tensor_tensor(out=rstd[:, :], in0=var_e[:, :], in1=neg_half[:, :], op=ALU.pow) \
                    .then_inc(rstd_done, 1)
                for c in range(NC):
                    pool.wait_ge(q_high, NC * b + c + 1)
                    pool.wait_ge(qk_out, 64 * (b + 1))
                    pool.tensor_tensor(out=qk[1][:, c, :], in0=q_f[:, c % 2, :], in1=qk[0][:, c, :].bitcast(F32),
                                       op=ALU.subtract).then_inc(q_low, 1)
                for t in range(NT):
                    pool.wait_ge(v_high, NT * b + t + 1)
                    pool.wait_ge(v_out, 16 * NC * (b + 1))
                    pool.tensor_tensor(
                        out=v_s4[:, t, :, DK:2 * DK],
                        in0=v_f[:, t % 2, :].rearrange("p (h d) -> p h d", h=H),
                        in1=v_s4[:, t, :, 0:DK].bitcast(F32), op=ALU.subtract).then_inc(v_low, 1)

        @block.vector
        def _(dve):
            dve.sem_inc(bank_free, NPB)
            dve.memset(v_s4[:, :, :, 2 * DK:2 * DK + 1].bitcast(F32), 1.0).then_inc(v_ones, 1)
            dve.memset(v_s4[:, :, :, 2 * DK + 1:VW].bitcast(F32), 0.0).then_inc(v_ones, 1)
            for n in range(3):
                dve.wait_ge(raw_in[n], 16)
                dve.tensor_copy(w_h[n][:, :, :], raws[n]).then_inc(w_high, 1)
                dve.wait_ge(w_high, n + 1)
                dve.tensor_tensor(out=w_l[n][:, :, :], in0=raws[n], in1=w_h[n][:, :, :].bitcast(F32),
                                  op=ALU.subtract).then_inc(w_low, 1)
            dve.wait_ge(consts_made, 3)
            dve.wait_ge(small_in, 48)
            with dve.Fori(0, B) as b:
                dve.wait_ge(x_in, 16 * b + 32)
                for t in range(NT):
                    dve.bn_stats(stats[:, t, :], x_raw[:, t, :]).then_inc(stats_done, 1)
                dve.wait_ge(stats_done, NT * (b + 1))
                gate(dve, passed)
                for t in range(NT):
                    dve.bn_aggr(mv[:, t, :], stats[:, t, :]).then_inc(mv_done, 1)
                dve.wait_ge(mv_done, NT * (b + 1))
                dve.tensor_scalar(var_e[:, :], mv[:, :, 1], LN_EPS, None, ALU.add).then_inc(var_done, 1)
                dve.wait_ge(m_in, 16 * b + 32)
                dve.wait_ge(pos_out, 16 * (b + 1))
                dve.tensor_scalar(pos[:, :, :], m_raw[:, :, :], 0.0, MASKED, ALU.is_equal, ALU.mult) \
                    .then_inc(pos_done, 1)
                dve.wait_ge(pos_done, b + 1)
                dve.tensor_reduce(pos_min[:, :], pos[:, :, :], AX_X, ALU.min).then_inc(min_done, 1)
                dve.wait_ge(min_done, b + 1)
                dve.tensor_scalar(q_fac[:, :], pos_min[:, :], 0.0, QSCALE, ALU.is_equal, ALU.mult) \
                    .then_inc(fac_done, 1)
                dve.wait_ge(fac_done, b + 1)
                for t in range(NT):
                    dve.tensor_scalar(fac_cols[:, t, :], ones[:, :], q_fac[:, t:t + 1], None, ALU.mult) \
                        .then_inc(cols_done, 1)
                dve.wait_ge(rstd_done, b + 1)
                for t in range(NT):
                    dve.tensor_scalar(xn[:, t, :], x_raw[:, t, :], mv[:, t, 0:1], rstd[:, t:t + 1],
                                      ALU.subtract, ALU.mult).then_inc(xn_done, 1)
                for c in range(NC):
                    dve.wait_ge(xT_high, NC * b + c + 1)
                    dve.tensor_tensor(out=xT_l[:, c, :], in0=ps_t[:, c % NTB, :], in1=xT_h[:, c, :].bitcast(F32),
                                      op=ALU.subtract).then_inc(xT_low, 1)
                dve.wait_ge(cT_high, b + 1)
                dve.tensor_tensor(out=cT_l[:, :, :], in0=c_raw[:, :, :], in1=cT_h[:, :, :].bitcast(F32),
                                  op=ALU.subtract).then_inc(cT_low, 1)
                dve.wait_ge(fac_row_done, b + 1)
                for c in range(NC):
                    n = NPJ * b + c
                    dve.wait_ge(projected, n + 1)
                    if c >= 2:
                        dve.wait_ge(q_low, NC * b + c - 1)
                    dve.scalar_tensor_tensor(out=q_f[:, c % 2, :], in0=ps_j[:, c % NPB, :], scalar=bq_c[:, c:c + 1],
                                             in1=fac_row[:, :], op0=ALU.add, op1=ALU.mult) \
                        .then_inc(bank_free, 1)
                for c in range(NC):
                    n = NC + c
                    dve.wait_ge(k_high, NC * b + c + 1)
                    dve.scalar_tensor_tensor(out=qk[3][:, c, :], in0=ps_j[:, n % NPB, :], scalar=bk_c[:, c:c + 1],
                                             in1=qk[2][:, c, :].bitcast(F32), op0=ALU.add, op1=ALU.subtract) \
                        .then_inc(bank_free, 1)
                for t in range(NT):
                    n = 2 * NC + t
                    dve.wait_ge(projected, NPJ * b + n + 1)
                    if t >= 2:
                        dve.wait_ge(v_low, NT * b + t - 1)
                    dve.tensor_tensor(out=v_f[:, t % 2, :], in0=ps_j[:, n % NPB, :], in1=bv_r[:, :], op=ALU.add) \
                        .then_inc(bank_free, 1)

        @block.scalar
        def _(act):
            act.wait_ge(small_in, 48)
            act.wait_ge(v_ones, 2)
            with act.Fori(0, B) as b:
                act.wait_ge(c_in, 16 * b + 32)
                act.activation(cT_h[:, :, :], c_raw[:, :, :], ACT.Copy).then_inc(cT_high, 1)
                act.wait_ge(fac_turned, b + 1)
                act.activation(fac_row[:, :], ps_f[:, :], ACT.Copy).then_inc(fac_row_done, 1)
                for c in range(NC):
                    act.wait_ge(x_turned, NC * b + c + 1)
                    act.activation(xT_h[:, c, :], ps_t[:, c % NTB, :], ACT.Copy).then_inc(xT_high, 1)
                act.wait_ge(qk_out, 64 * (b + 1))
                for c in range(NC):
                    act.wait_ge(bank_free, NPB + NPJ * b + c + 1)
                    act.activation(qk[0][:, c, :], q_f[:, c % 2, :], ACT.Copy).then_inc(q_high, 1)
                for c in range(NC):
                    n = NC + c
                    act.wait_ge(projected, NPJ * b + n + 1)
                    act.activation(qk[2][:, c, :], ps_j[:, n % NPB, :], ACT.Identity, bias=bk_c[:, c:c + 1]) \
                        .then_inc(k_high, 1)
                act.wait_ge(v_out, 16 * NC * (b + 1))
                for t in range(NT):
                    n = 2 * NC + t
                    act.wait_ge(bank_free, NPB + NPJ * b + n + 1)
                    act.activation(v_s4[:, t, :, 0:DK], v_f[:, t % 2, :].rearrange("p (h d) -> p h d", h=H),
                                   ACT.Copy).then_inc(v_high, 1)

        @block.tensor
        def _(pe):
            pe.wait_ge(w_low, 3)
            pe.wait_ge(consts_made, 3)
            with pe.Fori(0, B) as b:
                pe.wait_ge(cols_done, NT * (b + 1))
                for t in range(NT):
                    last = pe.matmul(ps_f[:, t * P:(t + 1) * P], fac_cols[:, t, :], ident[:, :], start=True, stop=True)
                last.then_inc(fac_turned, 1)
                pe.wait_ge(xn_done, NT * (b + 1))
                for c in range(NC):
                    if c >= NTB:
                        pe.wait_ge(xT_low, NC * b + c - NTB + 1)
                    for t in range(NT):
                        last = pe.transpose(ps_t[:, c % NTB, t * P:(t + 1) * P], xn[:, t, c * P:(c + 1) * P],
                                            ident[:, :])
                    last.then_inc(x_turned, 1)

                def product(n, pairs):
                    pe.wait_ge(bank_free, NPJ * b + n + 1)
                    for k, (w, m) in enumerate(pairs):
                        last = pe.matmul(ps_j[:, n % NPB, :], w, m, start=k == 0, stop=k == len(pairs) - 1)
                    last.then_inc(projected, 1)

                def features(w_h, w_l, a_h, a_l, c):
                    cs = slice(c * P, (c + 1) * P)
                    return [(w[:, k, cs], a[:, k, :]) for k in range(NC)
                            for w, a in ((w_h, a_h), (w_h, a_l), (w_l, a_h))]

                pe.wait_ge(xT_low, NC * (b + 1))
                for c in range(NC):
                    product(c, features(w_h[0], w_l[0], xT_h, xT_l, c))
                pe.wait_ge(cT_low, b + 1)
                for c in range(NC):
                    product(NC + c, features(w_h[1], w_l[1], cT_h, cT_l, c))
                for t in range(NT):
                    ts = slice(t * P, (t + 1) * P)
                    product(2 * NC + t, [(a[:, k, ts], w[:, k, :]) for k in range(NC)
                                         for a, w in ((cT_h, w_h[2]), (cT_h, w_l[2]), (cT_l, w_h[2]))])


def attend(nc, ident, bias, qh_d, ql_d, kh_d, kl_d, v_d, pos_d, att_d):
    UR = 2 * HG
    TR = UR * NT
    ROUNDS = NC * B // 2
    NS = 2
    NN = 8
    NE = 4
    NP = 4
    TURN, PV, BACK = 2, 8, 12
    HIGH, OUT = 2, 10
    LOW, NORM = 3, 14
    with ExitStack() as ctx:
        def sb(name, shape, dt=F32):
            return ctx.enter_context(nc.sbuf_tensor("a_" + name, shape, dt))

        def sem(name):
            return ctx.enter_context(nc.semaphore("a_" + name))

        q4 = sb("q4", [P, 2, HG, S], F32R)
        k4 = sb("k4", [P, 2, HG, S], F32R)
        v = sb("v", [P, 2, NT, HG * VW], F32R)
        pos = sb("pos", [P, 2, NT, S])
        bias_t = sb("bias_t", [P, HG, NT, S])
        nbm = sb("nbm", [P, NN, S])
        sc = sb("sc", [P, NE, S])
        nmax = sb("nmax", [P, NE])
        pr = sb("pr", [P, NE, S])
        pT_h, pT_l = sb("pT_h", [P, NP, NT, S], F32R), sb("pT_l", [P, NP, NT, S], F32R)
        o_sb = sb("o_sb", [2 * DK + 1, 2, S])
        rsum = sb("rsum", [P, 2, NT])
        o_low = sb("o_low", [P, 2, NT, DK])
        y = sb("y", [P, 2, NT, HG * DK])

        ps_s = ctx.enter_context(nc.psum_tensor("a_ps_s", [P, NS, S], F32))
        ps_t = ctx.enter_context(nc.psum_tensor("a_ps_t", [P, 2, S], F32))
        ps_o = ctx.enter_context(nc.psum_tensor("a_ps_o", [P, 2, S], F32))
        ps_c = ctx.enter_context(nc.psum_tensor("a_ps_c", [P, NT, 2 * DK + 1], F32))

        qkv_in = [sem("qkv_in0"), sem("qkv_in1")]
        pos_in = [sem("pos_in0"), sem("pos_in1")]
        bias_in = [sem(f"bias_in{i}") for i in range(HG)]
        nbm_done = sem("nbm_done")
        scored, summed, exped, turned, high, low, pv_done = (
            sem("scored"), sem("summed"), sem("exped"), sem("turned"), sem("high"), sem("low"), sem("pv_done"))
        o_copied, turned_back, inverted, y_done = sem("o_copied"), sem("turned_back"), sem("inverted"), sem("y_done")
        y_out = [sem("y_out0"), sem("y_out1")]
        passed = sem("passed")

        NLD = 9

        def lagged(g, j, lag):
            return behind(g, j, lag, TR, ROUNDS)

        def walk(eng, step, last):
            walk_rounds(eng, step, last, TR, ROUNDS)

        block = ctx.enter_context(nc.Block())

        @block.sync
        def _(sp):
            def load(g, j):
                n = 2 * g + j
                for t, (q_d, k_d) in enumerate(((qh_d, kh_d), (qh_d, kl_d), (ql_d, kh_d), (ql_d, kl_d))):
                    rows = slice(DK * t, DK * (t + 1))
                    sp.dma_start(q4[rows, j, :, :].bitcast(F32), q_d[n].rearrange("(i p) n -> p i n", p=DK)) \
                        .then_inc(qkv_in[j], 16)
                    sp.dma_start(k4[rows, j, :, :].bitcast(F32), k_d[n].rearrange("(i p) n -> p i n", p=DK)) \
                        .then_inc(qkv_in[j], 16)
                sp.dma_start(v[:, j, :, :].bitcast(F32), tokens(v_d[n])).then_inc(qkv_in[j], 16)

            def load_pos(g, j):
                sp.dma_start(pos[:, j, :, :], tokens(pos_d[g % (B // 2) * 2 + j])).then_inc(pos_in[j], 16)

            def store(g, j):
                sp.wait_ge(y_done, UR * g + HG * (j + 1))
                sp.dma_start(tokens(att_d[2 * g + j]), y[:, j, :, :]).then_inc(y_out[j], 16)

            for j in range(2):
                load_pos(0, j)
                load(0, j)
            sp.sem_inc(y_out[0], 16)
            sp.sem_inc(y_out[1], 16)
            with sp.Fori(0, ROUNDS - 1) as g:
                for j in range(2):
                    sp.wait_ge(nbm_done, TR * g + (j + 1) * NT * HG)
                    load_pos(g + 1, j)
                    sp.wait_ge(pv_done, TR * g + (j + 1) * NT * HG)
                    load(g + 1, j)
                    store(g, j)
            for j in range(2):
                store(ROUNDS - 1, j)
            for n in range(2):
                sp.wait_ge(y_out[n], 16 * (ROUNDS + 1))

        @block.gpsimd
        def _(pool):
            def load_bias(hg, i):
                pool.dma_start(bias_t[:, i, :, :], tokens(bias[0, hg * HG + i])).then_inc(bias_in[i], 16)

            def step(hg, g, j):
                b, i, qt = j // (NT * HG), j // NT % HG, j % NT
                if j % (NT * HG) == 0:
                    pool.wait_ge(pos_in[b], 16 * g + 16)
                if qt == 0:
                    pool.wait_ge(bias_in[i], 16 * (hg + 1))
                pool.wait_ge(summed, TR * g + j + 1)
                pool.tensor_tensor(out=nbm[:, j % NN, :], in0=pos[:, b, qt, :], in1=bias_t[:, i, qt, :],
                                   op=ALU.subtract).then_inc(nbm_done, 1)

            for i in range(HG):
                load_bias(0, i)
            for hg in range(NC):
                last = (hg + 1) * B // 2 - 1
                with pool.Fori(hg * (B // 2), last) as g:
                    for j in range(TR):
                        step(hg, g, j)
                for j in range(TR):
                    step(hg, last, j)
                    if hg < NC - 1 and j >= NT * HG + NT and j % NT == 0:
                        pool.wait_ge(nbm_done, TR * last + j)
                        load_bias(hg + 1, j // NT % HG - 1)
                if hg < NC - 1:
                    pool.wait_ge(nbm_done, TR * (last + 1))
                    load_bias(hg + 1, HG - 1)

        def tile(at):
            t = at[1]
            return t // (NT * HG), t // NT % HG, t % NT, t // NT

        def bank(at):
            return ps_t[:, at[1] % 2, :].rearrange("p (k n) -> p k n", k=NT)

        def turned_tile(a, at):
            return a[:, at[1] // NT % NP, :, at[1] % NT * P:(at[1] % NT + 1) * P]

        @block.tensor
        def _(pe):
            def step(g, j, more):
                if more:
                    b, i, qt, _ = tile((g, j))
                    if j % (NT * HG) == 0:
                        pe.wait_ge(qkv_in[b], 16 * NLD * g + 16 * NLD)
                    need(pe, summed, NN + TR * g + j - NS + 1 if lagged(g, j, NS) else 0)
                    pe.matmul(ps_s[:, j % NS, :], q4[:, b, i, qt * P:(qt + 1) * P], k4[:, b, i, :],
                              start=True, stop=True).then_inc(scored, 1)
                if at := lagged(g, j, PV):
                    n = TR * at[0] + at[1]
                    b, i, kt, u = tile(at)
                    if kt == 0:
                        pe.wait_ge(low, n + NT)
                        need(pe, o_copied, UR * at[0] + u - 1)
                    vt = v[:, b, kt, :].rearrange("p (h w) -> p h w", h=HG)
                    for part in (pT_h, pT_l):
                        last = pe.matmul(ps_o[0:2 * DK + 1, u % 2, :], vt[:, i, 0:2 * DK + 1], part[:, u % NP, kt, :],
                                         start=kt == 0 and part is pT_h, stop=kt == NT - 1 and part is pT_l)
                    last.then_inc(pv_done, 1)
                if (at := lagged(g, j, BACK)) and at[1] % NT == NT - 1:
                    u = at[1] // NT
                    pe.wait_ge(o_copied, UR * at[0] + u + 1)
                    need(pe, y_done, UR * at[0] + u)
                    for qt in range(NT):
                        last = pe.transpose(ps_c[:, qt, :], o_sb[:, u % 2, qt * P:(qt + 1) * P],
                                            ident[0:2 * DK + 1, 0:2 * DK + 1])
                    last.then_inc(turned_back, 1)
                if at := lagged(g, j, TURN):
                    n = TR * at[0] + at[1]
                    need(pe, low, n - 1)
                    pe.wait_ge(exped, n + 1)
                    for kt in range(NT):
                        last = pe.transpose(ps_t[:, at[1] % 2, kt * P:(kt + 1) * P],
                                            pr[:, at[1] % NE, kt * P:(kt + 1) * P], ident[:, :])
                    last.then_inc(turned, 1)

            walk(pe, step, BACK)

        @block.vector
        def _(dve):
            dve.sem_inc(summed, NN)

            def step(g, j, more):
                if more:
                    n = TR * g + j
                    dve.wait_ge(scored, n + 1)
                    dve.wait_ge(nbm_done, n + 1)
                    need(dve, exped, n - NE + 1)
                    gate(dve, passed)
                    dve.tensor_tensor_reduce(sc[:, j % NE, :], ps_s[:, j % NS, :], nbm[:, j % NN, :], 1.0, 3.0e38,
                                             ALU.add, ALU.min, nmax[:, j % NE:j % NE + 1]).then_inc(summed, 1)
                if at := lagged(g, j, LOW):
                    n = TR * at[0] + at[1]
                    dve.wait_ge(high, n + 1)
                    dve.tensor_tensor(out=turned_tile(pT_l, at), in0=bank(at),
                                      in1=turned_tile(pT_h, at).bitcast(F32), op=ALU.subtract).then_inc(low, 1)
                if (at := lagged(g, j, NORM)) and at[1] % NT == NT - 1:
                    b, i, _, u = tile(at)
                    n = UR * at[0] + u
                    dve.wait_ge(turned_back, n + 1)
                    dve.reciprocal(rsum[:, u % 2, :], ps_c[:, :, 2 * DK])
                    dve.tensor_copy(o_low[:, u % 2, :, :], ps_c[:, :, DK:2 * DK]).then_inc(inverted, 1)
                    dve.wait_ge(inverted, 2 * n + 1)
                    dve.tensor_tensor(out=o_low[:, u % 2, :, :], in0=ps_c[:, :, 0:DK], in1=o_low[:, u % 2, :, :],
                                      op=ALU.add).then_inc(inverted, 1)
                    dve.wait_ge(inverted, 2 * n + 2)
                    dve.wait_ge(y_out[b], 16 * at[0] + 16)
                    dve.tensor_tensor(out=y[:, b, :, i * DK:(i + 1) * DK], in0=o_low[:, u % 2, :, :],
                                      in1=rsum[:, u % 2, :].rearrange("p (t o) -> p t o", o=1).broadcast_to([P, NT, DK]),
                                      op=ALU.mult).then_inc(y_done, 1)

            walk(dve, step, NORM)

        @block.scalar
        def _(act):
            def step(g, j, more):
                if more:
                    n = TR * g + j
                    act.wait_ge(summed, NN + n + 1)
                    need(act, turned, n - NE + 1)
                    act.activation(pr[:, j % NE, :], sc[:, j % NE, :], ACT.Exp, scale=-1.0,
                                   bias=nmax[:, j % NE:j % NE + 1]).then_inc(exped, 1)
                if at := lagged(g, j, HIGH):
                    n = TR * at[0] + at[1]
                    act.wait_ge(turned, n + 1)
                    if at[1] % NT == 0:
                        need(act, pv_done, n - (NP - 1) * NT)
                    act.activation(turned_tile(pT_h, at), bank(at), ACT.Copy).then_inc(high, 1)
                if (at := lagged(g, j, OUT)) and at[1] % NT == NT - 1:
                    u = at[1] // NT
                    n = UR * at[0] + u
                    act.wait_ge(pv_done, TR * at[0] + at[1] + 1)
                    need(act, turned_back, n - 1)
                    act.activation(o_sb[:, u % 2, :], ps_o[0:2 * DK + 1, u % 2, :], ACT.Copy).then_inc(o_copied, 1)

            walk(act, step, OUT)


def mix(nc, ident, ones, neg_half, x, att_d, WoT, bo, ln_g, ln_b, rWT, rb, rawU, rawV, gamma, part_d, zh_d, zl_d):
    with ExitStack() as ctx:
        def sb(name, shape, dt=F32):
            return ctx.enter_context(nc.sbuf_tensor("m_" + name, shape, dt))

        def sem(name):
            return ctx.enter_context(nc.semaphore("m_" + name))

        att = sb("att", [P, NT, D])
        x_b = sb("x_b", [P, NT, D])
        aT = [sb("aT_h", [P, NC, S], F32R), sb("aT_l", [P, NC, S], F32R)]
        zT = [sb("zT_h", [P, NC, S], F32R), sb("zT_l", [P, NC, S], F32R)]
        hT = [sb("hT_h", [P, NL, S], F32R), sb("hT_l", [P, NL, S], F32R)]
        x1 = sb("x1", [P, 2, NT, D])
        z = sb("z", [P, NT, D])
        wo = [sb("wo_h", [P, NC, D], F32R), sb("wo_l", [P, NC, D], F32R)]
        ru = [sb("ru_h", [P, NC, 2 * NB], F32R), sb("ru_l", [P, NC, 2 * NB], F32R)]
        vg = [sb("vg_h", [P, NL, D], F32R), sb("vg_l", [P, NL, D], F32R)]
        bo_r, gam_r, rb_r, r_row = sb("bo_r", [P, D]), sb("gam_r", [P, D]), sb("rb_r", [P, NB]), sb("r_row", [P, NB])
        g_c, b_c = sb("g_c", [P, NC]), sb("b_c", [P, NC])
        b_cols = sb("b_cols", [P, NC, P])
        g_mean = sb("g_mean", [P, NB])
        rw_f = sb("rw_f", [P, NC, NB])
        rc, hl, sel = sb("rc", [P, NT, NB]), sb("hl", [P, NT, NB]), sb("sel", [P, NT, NB])
        r_abs, r_pos, u = sb("r_abs", [P, NT, NB]), sb("r_pos", [P, NT, NB]), sb("u", [P, NT, NB])
        w, u_kept, ln_w = sb("w", [P, NT, NB]), sb("u_kept", [P, NT, NB]), sb("ln_w", [P, NT, NB])
        top = sb("top", [P, NT, 8])
        ssum, tanh_s, coef = sb("ssum", [P, NT]), sb("tanh_s", [P, NT]), sb("coef", [P, NT])
        stats, mv = sb("stats", [P, NT, 6]), sb("mv", [P, NT, 2])
        var_e, rstd, var_z, eps_t = sb("var_e", [P, NT]), sb("rstd", [P, NT]), sb("var_z", [P, NT]), sb("eps_t", [P, NT])
        rs = sb("rs", [P, 2, NT])
        nrm, nrm_s, nrm_r = sb("nrm", [P, 2 * NL]), sb("nrm_s", [P, 2 * NL]), sb("nrm_r", [P, 2 * NL])

        ps_t = ctx.enter_context(nc.psum_tensor("m_ps_t", [P, 2, S], F32))
        ps_o = ctx.enter_context(nc.psum_tensor("m_ps_o", [P, NT, D], F32))
        ps_r = ctx.enter_context(nc.psum_tensor("m_ps_r", [P, 2, 2 * NB], F32))

        rows_in, w_in, lat_in = sem("rows_in"), sem("w_in"), sem("lat_in")
        lat_sq, lat_root, lat_max, lat_inv, lat_unit, lat_gam, lat_turned = (
            sem(n) for n in ("lat_sq", "lat_root", "lat_max", "lat_inv", "lat_unit", "lat_gam", "lat_turned"))
        g_scaled, g_summed, g_mean_done, g_centred = (
            sem(n) for n in ("g_scaled", "g_summed", "g_mean_done", "g_centred"))
        w_high, w_low = sem("w_high"), sem("w_low")
        att_in, x_in, xb_done = sem("att_in"), sem("x_in"), sem("xb_done")
        turned, t_high, t_low = sem("turned"), sem("t_high"), sem("t_low")
        o_ready, o_read = sem("o_ready"), sem("o_read")
        stats_done, mv_done, var_done, rstd_done, vz_done, z_done = (
            sem(n) for n in ("stats_done", "mv_done", "var_done", "rstd_done", "vz_done", "z_done"))
        eps_made = sem("eps_made")
        r_ready, r_read, hl_read = sem("r_ready"), sem("r_read"), sem("hl_read")
        clip_done, top_done, rep_done, sel_done = (
            sem(n) for n in ("clip_done", "top_done", "rep_done", "sel_done"))
        abs_done, pos_done, u_done, w_done, kept_done, ln_done, err_done, rest_done, al_done = (
            sem(n) for n in ("abs_done", "pos_done", "u_done", "w_done", "kept_done", "ln_done", "err_done",
                             "rest_done", "al_done"))
        sum_done, tanh_done, den_done, dinv_done, coef_done, hz_done = (
            sem(n) for n in ("sum_done", "tanh_done", "den_done", "dinv_done", "coef_done", "hz_done"))
        z_out, part_out = sem("z_out"), sem("part_out")
        passed = sem("passed")

        TURNS = 2 * NC + NL
        SUMS = 2 * NT

        def turns_of(b, last):
            n = 2 * NC + TURNS * b
            return (None, n, None) if last else (n, n + NC, n + NC + NL)

        def sums_of(b, last):
            n = NT + SUMS * b
            return (None, n) if last else (n, n + NT)

        def walk(eng, front, body):
            front()
            with eng.Fori(0, B // 2 - 1) as r:
                for p in range(2):
                    body(2 * r + p, p, False)
            body(B - 2, 0, False)
            body(B - 1, 1, True)

        block = ctx.enter_context(nc.Block())

        @block.sync
        def _(sp):
            def row(v, n):
                return v.rearrange("(a n) -> a n", a=1).broadcast_to([P, n])

            sp.dma_start(att[:, :, :], tokens(WoT)).then_inc(w_in, 16)
            sp.dma_start(rw_f[:, :, :], tokens(rWT)).then_inc(w_in, 16)
            sp.dma_start(z[:, 0:NL, :], tokens(rawU)).then_inc(lat_in, 16)
            sp.dma_start(z[:, NL:2 * NL, :], tokens(rawV)).then_inc(lat_in, 16)
            for dst, v, n in ((bo_r, bo, D), (gam_r, gamma, D), (rb_r, rb, NB)):
                sp.dma_start(dst[:, :], row(v, n)).then_inc(rows_in, 16)
            sp.dma_start(g_c[:, :], ln_g).then_inc(rows_in, 16)
            sp.dma_start(b_c[:, :], ln_b).then_inc(rows_in, 16)
            sp.sem_inc(part_out, 16)

            def load_att(b):
                for c in range(NC):
                    sp.dma_start(att[:, :, c * P:(c + 1) * P], tokens(att_d[B * c + b])).then_inc(att_in, 16)

            def load_x(b):
                sp.dma_start(x_b[:, :, :], tokens(x[b])).then_inc(x_in, 16)

            def store_z(b, n):
                sp.wait_ge(t_low, n + NC)
                sp.dma_start(zh_d[b], zT[0][:, :, :].bitcast(F32)).then_inc(z_out, 16)
                sp.dma_start(zl_d[b], zT[1][:, :, :].bitcast(F32)).then_inc(z_out, 16)

            def front():
                load_x(0)
                sp.wait_ge(w_low, 1)
                load_att(0)
                sp.wait_ge(turned, NC)
                load_att(1)
                sp.wait_ge(o_read, NT)
                load_x(1)
                store_z(0, NC)

            def body(b, p, last):
                t_att, _, t_z = turns_of(b, last)
                s_out, s_lat = sums_of(b, last)
                if not last and not (isinstance(b, int) and b == B - 2):
                    sp.wait_ge(turned, t_att + NC)
                    load_att(b + 2)
                    sp.wait_ge(o_read, s_out + NT)
                    load_x(b + 2)
                if not last:
                    store_z(b + 1, t_z)
                sp.wait_ge(o_read, s_lat + NT)
                sp.dma_start(tokens(part_d[b]), x1[:, p, :, :]).then_inc(part_out, 16)

            walk(sp, front, body)
            sp.wait_ge(z_out, 32 * B)
            sp.wait_ge(part_out, 16 * (B + 1))

        @block.gpsimd
        def _(pool):
            pool.memset(eps_t[:, :], LN_EPS).then_inc(eps_made, 1)
            pool.wait_ge(eps_made, 1)
            pool.wait_ge(rows_in, 16 * 5)

            def add_bo(b):
                pool.wait_ge(x_in, 16 * b + 16)
                for t in range(NT):
                    pool.tensor_tensor(out=x_b[:, t, :], in0=x_b[:, t, :], in1=bo_r[:, :], op=ALU.add) \
                        .then_inc(xb_done, 1)

            def roots(b, p):
                pool.wait_ge(var_done, b + 1)
                pool.tensor_tensor(out=rstd[:, :], in0=var_e[:, :], in1=neg_half[:, :], op=ALU.pow) \
                    .then_inc(rstd_done, 1)
                pool.wait_ge(rstd_done, b + 1)
                pool.tensor_tensor(out=var_z[:, :], in0=rstd[:, :], in1=rstd[:, :], op=ALU.mult).then_inc(vz_done, 1)
                pool.wait_ge(vz_done, 4 * b + 1)
                pool.tensor_tensor(out=var_z[:, :], in0=var_z[:, :], in1=mv[:, :, 1], op=ALU.mult).then_inc(vz_done, 1)
                pool.wait_ge(vz_done, 4 * b + 2)
                pool.tensor_tensor(out=var_z[:, :], in0=var_z[:, :], in1=eps_t[:, :], op=ALU.add).then_inc(vz_done, 1)
                pool.wait_ge(vz_done, 4 * b + 3)
                pool.tensor_tensor(out=rs[:, p, :], in0=var_z[:, :], in1=neg_half[:, :], op=ALU.pow) \
                    .then_inc(vz_done, 1)

            def front():
                add_bo(0)
                roots(0, 0)

            def body(b, p, last):
                if not last:
                    add_bo(b + 1)
                pool.wait_ge(kept_done, b + 1)
                pool.tensor_tensor(out=w[:, :, :], in0=u[:, :, :], in1=u_kept[:, :, :], op=ALU.subtract) \
                    .then_inc(err_done, 1)
                pool.wait_ge(err_done, b + 1)
                pool.tensor_tensor(out=w[:, :, :], in0=w[:, :, :], in1=r_pos[:, :, :], op=ALU.add) \
                    .then_inc(rest_done, 1)
                if not last:
                    roots(b + 1, 1 - p)

            walk(pool, front, body)

        @block.vector
        def _(dve):
            def split(n, hi, lo, src):
                dve.tensor_copy(hi, src).then_inc(w_high, 1)
                dve.wait_ge(w_high, n + 1)
                dve.tensor_tensor(out=lo, in0=src, in1=hi.bitcast(F32), op=ALU.subtract).then_inc(w_low, 1)

            dve.wait_ge(w_in, 32)
            split(0, wo[0][:, :, :], wo[1][:, :, :], att[:, :, :])
            dve.wait_ge(rows_in, 16 * 5)
            for c in range(NC):
                dve.tensor_scalar(b_cols[:, c, :], ones[:, :], b_c[:, c:c + 1], None, ALU.mult).then_inc(g_scaled, 1)
            for c in range(NC):
                dve.tensor_scalar(rc[:, c, :], rw_f[:, c, :], g_c[:, c:c + 1], None, ALU.mult).then_inc(g_scaled, 1)
            dve.wait_ge(lat_in, 32)
            for n in range(2 * NL):
                dve.tensor_tensor_reduce(x1[:, 1, n, :], z[:, n, :], z[:, n, :], 1.0, 0.0, ALU.mult, ALU.add,
                                         nrm[:, n:n + 1]).then_inc(lat_sq, 1)
            dve.wait_ge(lat_root, 1)
            dve.tensor_scalar(nrm[:, :], nrm_s[:, :], UNIT_EPS, None, ALU.max).then_inc(lat_max, 1)
            dve.wait_ge(lat_max, 1)
            dve.reciprocal(nrm_r[:, :], nrm[:, :]).then_inc(lat_inv, 1)
            dve.wait_ge(lat_inv, 1)
            for n in range(2 * NL):
                dve.tensor_scalar(x1[:, 0, n, :], z[:, n, :], nrm_r[:, n:n + 1], None, ALU.mult).then_inc(lat_unit, 1)
            dve.wait_ge(lat_unit, 2 * NL)
            for n in range(NL, 2 * NL):
                dve.tensor_tensor(out=x1[:, 1, n, :], in0=x1[:, 0, n, :], in1=gam_r[:, :], op=ALU.mult) \
                    .then_inc(lat_gam, 1)
            dve.wait_ge(lat_gam, NL)
            split(1, vg[0][:, :, :], vg[1][:, :, :], x1[:, 1, NL:2 * NL, :])
            dve.wait_ge(g_summed, 2)
            dve.tensor_scalar(g_mean[:, :], ps_r[:, 0, 0:NB], 1.0 / D, None, ALU.mult).then_inc(g_mean_done, 1)
            dve.tensor_tensor(out=r_row[:, :], in0=ps_r[:, 1, 0:NB], in1=rb_r[:, :], op=ALU.add) \
                .then_inc(g_mean_done, 1)
            dve.wait_ge(g_mean_done, 2)
            for c in range(NC):
                dve.tensor_tensor(out=rc[:, c, :], in0=rc[:, c, :], in1=g_mean[:, :], op=ALU.subtract) \
                    .then_inc(g_centred, 1)
            dve.wait_ge(g_centred, NC)
            split(2, ru[0][:, :, 0:NB], ru[1][:, :, 0:NB], rc[:, :, :])
            for h in range(2):
                dve.wait_ge(lat_turned, h + 1)
                split(3 + h, ru[0][:, 2 * h:2 * h + 2, NB:2 * NB], ru[1][:, 2 * h:2 * h + 2, NB:2 * NB],
                      ps_t[:, h, :].rearrange("p (c n) -> p c n", n=NB))
            dve.sem_inc(r_read, 2)

            def lows(n, dst, count):
                for c in range(count):
                    dve.wait_ge(t_high, n + c + 1)
                    dve.tensor_tensor(out=dst[1][:, c, :], in0=ps_t[:, c % 2, :], in1=dst[0][:, c, :].bitcast(F32),
                                      op=ALU.subtract).then_inc(t_low, 1)

            def residual(b, p, n):
                need(dve, part_out, 16 * b)
                for t in range(NT):
                    dve.wait_ge(xb_done, NT * b + t + 1)
                    dve.wait_ge(o_ready, n + t + 1)
                    dve.tensor_tensor(out=x1[:, p, t, :], in0=ps_o[:, t, :], in1=x_b[:, t, :], op=ALU.add) \
                        .then_inc(o_read, 1)
                for t in range(NT):
                    dve.wait_ge(o_read, n + t + 1)
                    dve.bn_stats(stats[:, t, :], x1[:, p, t, :]).then_inc(stats_done, 1)
                need(dve, vz_done, 4 * b)
                dve.wait_ge(stats_done, NT * (b + 1))
                gate(dve, passed)
                for t in range(NT):
                    dve.bn_aggr(mv[:, t, :], stats[:, t, :]).then_inc(mv_done, 1)
                dve.wait_ge(mv_done, NT * (b + 1))
                dve.tensor_scalar(var_e[:, :], mv[:, :, 1], LN_EPS, None, ALU.add).then_inc(var_done, 1)

            def normalise(b, p):
                dve.wait_ge(rstd_done, b + 1)
                for t in range(NT):
                    dve.tensor_scalar(z[:, t, :], x1[:, p, t, :], mv[:, t, 0:1], rstd[:, t:t + 1],
                                      ALU.subtract, ALU.mult).then_inc(z_done, 1)

            def route(b, p):
                dve.wait_ge(vz_done, 4 * b + 4)
                for t in range(NT):
                    dve.wait_ge(r_ready, NT * b + t + 1)
                    dve.scalar_tensor_tensor(out=rc[:, t, :], in0=ps_r[:, t % 2, 0:NB], scalar=rs[:, p, t:t + 1],
                                             in1=r_row[:, :], op0=ALU.mult, op1=ALU.add).then_inc(r_read, 1)
                dve.wait_ge(r_read, 2 + NT * (b + 1))
                dve.tensor_scalar(rc[:, :, :], rc[:, :, :], -TAU, TAU, ALU.max, ALU.min).then_inc(clip_done, 1)
                dve.wait_ge(clip_done, b + 1)
                gate(dve, passed)
                for t in range(NT):
                    dve.max(top[:, t, :], rc[:, t, :]).then_inc(top_done, 1)
                dve.wait_ge(top_done, NT * (b + 1))
                gate(dve, passed)
                for t in range(NT):
                    dve.match_replace(sel[:, t, :], top[:, t, :], rc[:, t, :], -1.0e30).then_inc(rep_done, 1)
                dve.wait_ge(rep_done, NT * (b + 1))
                dve.tensor_tensor(out=sel[:, :, :], in0=sel[:, :, :], in1=rc[:, :, :], op=ALU.not_equal) \
                    .then_inc(sel_done, 1)

            def weigh(b):
                dve.wait_ge(rest_done, b + 1)
                dve.wait_ge(ln_done, b + 1)
                dve.tensor_tensor(out=w[:, :, :], in0=w[:, :, :], in1=ln_w[:, :, :], op=ALU.add).then_inc(al_done, 1)
                dve.wait_ge(al_done, b + 1)
                dve.wait_ge(sel_done, b + 1)
                gate(dve, passed)
                for t in range(NT):
                    dve.tensor_tensor_reduce(sel[:, t, :], w[:, t, :], sel[:, t, :], 1.0, 0.0, ALU.mult, ALU.add,
                                             ssum[:, t:t + 1]).then_inc(sum_done, 1)
                dve.wait_ge(sum_done, NT * (b + 1))
                dve.tensor_scalar(coef[:, :], ssum[:, :], UNIT_EPS, None, ALU.add).then_inc(den_done, 1)
                dve.wait_ge(den_done, b + 1)
                dve.reciprocal(coef[:, :], coef[:, :]).then_inc(dinv_done, 1)
                dve.wait_ge(dinv_done, b + 1)
                dve.wait_ge(tanh_done, b + 1)
                dve.tensor_tensor(out=coef[:, :], in0=coef[:, :], in1=tanh_s[:, :], op=ALU.mult).then_inc(coef_done, 1)
                dve.wait_ge(coef_done, b + 1)
                dve.wait_ge(hl_read, 2 + NT * (b + 1))
                for t in range(NT):
                    dve.scalar_tensor_tensor(out=hl[:, t, :], in0=sel[:, t, :], scalar=coef[:, t:t + 1],
                                             in1=hl[:, t, :], op0=ALU.mult, op1=ALU.mult).then_inc(hz_done, 1)

            def front():
                lows(0, aT, NC)
                residual(0, 0, 0)
                normalise(0, 0)
                lows(NC, zT, NC)

            def body(b, p, last):
                t_att, t_lat, t_z = turns_of(b, last)
                s_out, s_lat = sums_of(b, last)
                if not last:
                    lows(t_att, aT, NC)
                route(b, p)
                if not last:
                    residual(b + 1, 1 - p, s_out)
                weigh(b)
                if not last:
                    normalise(b + 1, 1 - p)
                lows(t_lat, hT, NL)
                if not last:
                    lows(t_z, zT, NC)
                for t in range(NT):
                    dve.wait_ge(o_ready, s_lat + t + 1)
                    dve.tensor_tensor(out=x1[:, p, t, :], in0=ps_o[:, t, :], in1=x1[:, p, t, :], op=ALU.add) \
                        .then_inc(o_read, 1)

            walk(dve, front, body)

        @block.scalar
        def _(act):
            act.wait_ge(lat_sq, 2 * NL)
            act.activation(nrm_s[:, :], nrm[:, :], ACT.Sqrt).then_inc(lat_root, 1)
            act.sem_inc(hl_read, 2)

            def highs(n, dst, count):
                for c in range(count):
                    act.wait_ge(turned, n + c + 1)
                    act.activation(dst[0][:, c, :], ps_t[:, c % 2, :], ACT.Copy).then_inc(t_high, 1)

            def front():
                act.wait_ge(w_low, 5)
                highs(0, aT, NC)
                highs(NC, zT, NC)

            def body(b, p, last):
                t_att, t_lat, t_z = turns_of(b, last)
                if not last:
                    highs(t_att, aT, NC)
                for t in range(NT):
                    act.wait_ge(r_read, 2 + NT * b + t + 1)
                    act.activation(hl[:, t, :], ps_r[:, t % 2, NB:2 * NB], ACT.Copy).then_inc(hl_read, 1)
                act.wait_ge(clip_done, b + 1)
                act.activation(r_abs[:, :, :], rc[:, :, :], ACT.Abs).then_inc(abs_done, 1)
                act.activation(r_pos[:, :, :], rc[:, :, :], ACT.Relu).then_inc(pos_done, 1)
                act.wait_ge(abs_done, b + 1)
                act.activation(u[:, :, :], r_abs[:, :, :], ACT.Exp, scale=-1.0).then_inc(u_done, 1)
                act.wait_ge(u_done, b + 1)
                act.activation(w[:, :, :], u[:, :, :], ACT.Identity, bias=1.0).then_inc(w_done, 1)
                act.wait_ge(w_done, b + 1)
                act.activation(u_kept[:, :, :], w[:, :, :], ACT.Identity, bias=-1.0).then_inc(kept_done, 1)
                act.activation(ln_w[:, :, :], u[:, :, :], ACT.Ln, bias=1.0).then_inc(ln_done, 1)
                act.wait_ge(sum_done, NT * (b + 1))
                act.activation(tanh_s[:, :], ssum[:, :], ACT.Tanh).then_inc(tanh_done, 1)
                highs(t_lat, hT, NL)
                if not last:
                    act.wait_ge(z_out, 32 * (b + 1))
                    highs(t_z, zT, NC)

            walk(act, front, body)

        @block.tensor
        def _(pe):
            pe.wait_ge(g_scaled, 2 * NC)
            for c in range(NC):
                last = pe.matmul(ps_r[:, 0, 0:NB], ones[:, :], rc[:, c, :], start=c == 0, stop=c == NC - 1)
            last.then_inc(g_summed, 1)
            for c in range(NC):
                last = pe.matmul(ps_r[:, 1, 0:NB], b_cols[:, c, :], rw_f[:, c, :], start=c == 0, stop=c == NC - 1)
            last.then_inc(g_summed, 1)
            pe.wait_ge(lat_unit, 2 * NL)
            for c in range(NC):
                for n in range(NL):
                    last = pe.transpose(ps_t[:, c // 2, (c % 2 * NL + n) * P:(c % 2 * NL + n + 1) * P],
                                        x1[:, 0, n, c * P:(c + 1) * P], ident[:, :])
                if c % 2:
                    last.then_inc(lat_turned, 1)
            pe.wait_ge(w_low, 5)

            def turn(n, src, count):
                for c in range(count):
                    need(pe, t_low, n + c - 1)
                    for t in range(NT):
                        last = pe.transpose(ps_t[:, c % 2, t * P:(t + 1) * P], src[:, t, c * P:(c + 1) * P],
                                            ident[:, :])
                    last.then_inc(turned, 1)

            def sums(dst, a, w_, t, chunks):
                passes = [(a[m][:, k, t * P:(t + 1) * P], w_[n][:, k, :]) for k in range(chunks) for m, n in PASSES]
                for n, (stationary, moving) in enumerate(passes):
                    last = pe.matmul(dst, stationary, moving, start=n == 0, stop=n == len(passes) - 1)
                return last

            def project_out(n):
                for t in range(NT):
                    need(pe, o_read, n + t - NT + 1)
                    sums(ps_o[:, t, :], aT, wo, t, NC).then_inc(o_ready, 1)

            def front():
                pe.wait_ge(att_in, 16 * NC)
                turn(0, att, NC)
                pe.wait_ge(t_low, NC)
                project_out(0)
                pe.wait_ge(z_done, NT)
                turn(NC, z, NC)

            def body(b, p, last):
                t_att, t_lat, t_z = turns_of(b, last)
                s_out, s_lat = sums_of(b, last)
                if not last:
                    pe.wait_ge(att_in, 16 * NC * (b + 2))
                    turn(t_att, att, NC)
                pe.wait_ge(t_low, 2 * NC + TURNS * b)
                for t in range(NT):
                    pe.wait_ge(r_read, NT * b + t + 1)
                    pe.wait_ge(hl_read, NT * b + t + 1)
                    sums(ps_r[:, t % 2, :], zT, ru, t, NC).then_inc(r_ready, 1)
                if not last:
                    pe.wait_ge(t_low, t_att + NC)
                    project_out(s_out)
                pe.wait_ge(hz_done, NT * (b + 1))
                turn(t_lat, hl, NL)
                if not last:
                    pe.wait_ge(z_done, NT * (b + 2))
                    turn(t_z, z, NC)
                pe.wait_ge(t_low, t_lat + NL)
                for t in range(NT):
                    pe.wait_ge(o_read, s_lat + t - NT + 1)
                    sums(ps_o[:, t, :], hT, vg, t, NL).then_inc(o_ready, 1)

            walk(pe, front, body)


def feed(nc, W1T, W2T, zh_d, zl_d, part_d, out):
    LAG = 2
    NG = 4
    STEPS = 2 * NF
    ROUNDS = B // 2
    with ExitStack() as ctx:
        def sb(name, shape, dt=F32):
            return ctx.enter_context(nc.sbuf_tensor("f_" + name, shape, dt))

        def sem(name):
            return ctx.enter_context(nc.semaphore("f_" + name))

        w1 = [sb("w1_h", [P, NC, FF], F32R), sb("w1_l", [P, NC, FF], F32R)]
        w2 = [sb("w2_h", [P, NF, D], F32R), sb("w2_l", [P, NF, D], F32R)]
        zT = [sb("zT_h", [P, 2, NC, S], F32R), sb("zT_l", [P, 2, NC, S], F32R)]
        part = sb("part", [P, NT, D])
        y = sb("y", [P, NT, D])
        g_f = sb("g_f", [P, NG, S])
        g_h, g_l = sb("g_h", [P, NG, S], F32R), sb("g_l", [P, NG, S], F32R)
        ps_h = ctx.enter_context(nc.psum_tensor("f_ps_h", [P, NG, S], F32))
        ps_y = ctx.enter_context(nc.psum_tensor("f_ps_y", [P, NT, D], F32))

        stage_in = [sem("stage_in0"), sem("stage_in1")]
        w_high, w_low = sem("w_high"), sem("w_low")
        z_in = [sem("z_in0"), sem("z_in1")]
        part_in = sem("part_in")
        hidden, gelu_done, g_high, g_low, g_used = (
            sem("hidden"), sem("gelu_done"), sem("g_high"), sem("g_low"), sem("g_used"))
        y_done, y_out = sem("y_done"), sem("y_out")

        pieces = [(W1T[c * P:(c + 1) * P, :], w1, c) for c in range(NC)] + \
                 [(tokens(W2T[n * 4 * P:(n + 1) * 4 * P, :]), w2, n) for n in range(NF // 4)]
        stages = [part, y]

        def staged(n):
            ap = stages[n % 2][:, :, :]
            return ap.rearrange("p k n -> p (k n)") if pieces[n][1] is w1 else ap

        def placed(n, w):
            _, kind, m = pieces[n]
            return w[:, m, :] if kind is w1 else w[:, 4 * m:4 * m + 4, :]

        block = ctx.enter_context(nc.Block())

        @block.sync
        def _(sp):
            for n, (src, _, _) in enumerate(pieces):
                need(sp, w_low, n - 1)
                sp.dma_start(staged(n), src).then_inc(stage_in[n % 2], 16)
            sp.wait_ge(w_low, len(pieces))
            sp.sem_inc(y_out, 16)

            def load(g, j):
                for h, z_d in enumerate((zh_d, zl_d)):
                    sp.dma_start(zT[h][:, j, :, :].bitcast(F32), z_d[2 * g + j]).then_inc(z_in[j], 16)

            def load_part(b):
                sp.dma_start(part[:, :, :], tokens(part_d[b])).then_inc(part_in, 16)

            def store(b):
                sp.wait_ge(y_done, NT * (b + 1))
                sp.dma_start(tokens(out[b]), y[:, :, :]).then_inc(y_out, 16)

            load(0, 0)
            load(0, 1)
            load_part(0)
            with sp.Fori(0, ROUNDS - 1) as g:
                for j in range(2):
                    sp.wait_ge(hidden, STEPS * g + (j + 1) * NF)
                    load(g + 1, j)
                    store(2 * g + j)
                    load_part(2 * g + j + 1)
            store(B - 2)
            load_part(B - 1)
            store(B - 1)
            sp.wait_ge(y_out, 16 * (B + 1))

        @block.gpsimd
        def _(pool):
            pool.sem_inc(g_low, NG)
            with pool.Fori(0, B * NF // NG) as r:
                for k in range(NG):
                    pool.wait_ge(g_high, NG * r + k + 1)
                    pool.tensor_tensor(out=g_l[:, k, :], in0=g_f[:, k, :], in1=g_h[:, k, :].bitcast(F32),
                                       op=ALU.subtract).then_inc(g_low, 1)

        @block.scalar
        def _(act):
            act.sem_inc(gelu_done, NG)
            with act.Fori(0, B * NF // NG) as r:
                for k in range(NG):
                    act.wait_ge(hidden, NG * r + k + 1)
                    act.wait_ge(g_low, NG * r + k + 1)
                    act.activation(g_f[:, k, :], ps_h[:, k, :], ACT.Gelu).then_inc(gelu_done, 1)

        @block.vector
        def _(dve):
            for n in range(len(pieces)):
                kind = pieces[n][1]
                dve.wait_ge(stage_in[n % 2], 16 * (n // 2 + 1))
                dve.tensor_copy(placed(n, kind[0]), staged(n)).then_inc(w_high, 1)
                dve.wait_ge(w_high, n + 1)
                dve.tensor_tensor(out=placed(n, kind[1]), in0=staged(n), in1=placed(n, kind[0]).bitcast(F32),
                                  op=ALU.subtract).then_inc(w_low, 1)

            def step(g, j, more):
                if more:
                    n = STEPS * g + j
                    dve.wait_ge(gelu_done, NG + n + 1)
                    need(dve, g_used, n - NG + 1)
                    dve.tensor_copy(g_h[:, j % NG, :], g_f[:, j % NG, :]).then_inc(g_high, 1)
                if (at := behind(g, j, LAG + 1, STEPS, ROUNDS)) and at[1] % NF == NF - 1:
                    b = 2 * at[0] + at[1] // NF
                    dve.wait_ge(part_in, 16 * b + 16)
                    dve.wait_ge(y_out, 16 * b + 16)
                    dve.wait_ge(g_used, STEPS * at[0] + at[1] + 1)
                    for t in range(NT):
                        dve.tensor_tensor(out=y[:, t, :], in0=ps_y[:, t, :], in1=part[:, t, :], op=ALU.add) \
                            .then_inc(y_done, 1)

            walk_rounds(dve, step, LAG + 1, STEPS, ROUNDS)

        @block.tensor
        def _(pe):
            pe.wait_ge(w_low, len(pieces))

            def step(g, j, more):
                if more:
                    b, f = j // NF, j % NF
                    fs = slice(f * P, (f + 1) * P)
                    if f == 0:
                        pe.wait_ge(z_in[b], 32 * g + 32)
                    pe.wait_ge(gelu_done, STEPS * g + j + 1)
                    passes = [(w1[x][:, k, fs], zT[y][:, b, k, :]) for k in range(NC) for x, y in PASSES]
                    for m, (w, a) in enumerate(passes):
                        last = pe.matmul(ps_h[:, j % NG, :], w, a, start=m == 0, stop=m == len(passes) - 1)
                    last.then_inc(hidden, 1)
                if at := behind(g, j, LAG, STEPS, ROUNDS):
                    n = STEPS * at[0] + at[1]
                    b, f = 2 * at[0] + at[1] // NF, at[1] % NF
                    pe.wait_ge(g_low, NG + n + 1)
                    for t in range(NT):
                        if f == 0:
                            need(pe, y_done, NT * (b - 1) + t + 1)
                        gs = [a[:, at[1] % NG, t * P:(t + 1) * P] for a in (g_h, g_l)]
                        for m, (x, y) in enumerate(PASSES):
                            last = pe.matmul(ps_y[:, t, :], gs[x], w2[y][:, f, :],
                                             start=f == 0 and m == 0, stop=f == NF - 1 and m == 2)
                    last.then_inc(g_used, 1)

            walk_rounds(pe, step, LAG, STEPS, ROUNDS)


INPUTS = ("x", "ctxT", "bias", "mask", "WqT", "bq", "WkT", "bk", "WvT", "bv", "WoT", "bo", "W1T", "W2T",
          "ln_g", "ln_b", "rWT", "rb", "rawU", "rawV", "gamma")


def kernel(x, ctx_1024, fside_1x16xSxS2_0, mask_Bx1xSxS2_ik1, L0_xattn_Wq, L0_xattn_bq, L0_xattn_Wk, L0_xattn_bk,
           L0_xattn_Wv, L0_xattn_bv, L0_xattn_Wo, L0_xattn_bo, L0_ffn_W1, L0_ffn_W2, L0_ffn_ln_g, L0_ffn_ln_b,
           L0_ffn_router_W, L0_ffn_router_b, L0_ffn_raw_U, L0_ffn_raw_V, L0_ffn_gamma):
    import numpy as np
    import concourse.bacc as bacc
    from concourse.bass_utils import run_bass_kernel_spmd

    given = {
        "x": x, "ctxT": np.asarray(ctx_1024).transpose(0, 2, 1), "bias": fside_1x16xSxS2_0,
        "mask": np.asarray(mask_Bx1xSxS2_ik1)[:, 0],
        "WqT": np.asarray(L0_xattn_Wq).T, "bq": np.asarray(L0_xattn_bq).reshape(NC, P).T, "WkT": np.asarray(L0_xattn_Wk).T, "bk": np.asarray(L0_xattn_bk).reshape(NC, P).T,
        "WvT": np.asarray(L0_xattn_Wv).T, "bv": L0_xattn_bv, "WoT": np.asarray(L0_xattn_Wo).T, "bo": L0_xattn_bo,
        "W1T": np.asarray(L0_ffn_W1).T, "W2T": np.asarray(L0_ffn_W2).T, "ln_g": np.asarray(L0_ffn_ln_g).reshape(NC, P).T,
        "ln_b": np.asarray(L0_ffn_ln_b).reshape(NC, P).T,
        "rWT": np.asarray(L0_ffn_router_W).T, "rb": L0_ffn_router_b, "rawU": L0_ffn_raw_U, "rawV": L0_ffn_raw_V,
        "gamma": np.asarray(L0_ffn_gamma).reshape(-1),
    }
    nc = bacc.Bacc("TRN2", target_bir_lowering=False, num_devices=1)
    arrays, aps = {}, []
    for name in INPUTS:
        a = np.ascontiguousarray(given[name])
        arrays["in_" + name] = a
        aps.append(nc.dram_tensor("in_" + name, a.shape, mybir.dt.from_np(a.dtype), kind="ExternalInput").ap())
    out = nc.dram_tensor("out_x", (B, S, D), F32, kind="ExternalOutput").ap()
    build(nc, *aps, out)
    result = run_bass_kernel_spmd(nc, [arrays], core_ids=[0])
    return result.results[0]["out_x"]
```

```python
from contextlib import ExitStack

import concourse.bass as bass
from concourse import mybir

P = 128
F32 = mybir.dt.float32
F32R = mybir.dt.float32r
I32 = mybir.dt.int32
ALU = mybir.AluOpType
ACT = mybir.ActivationFunctionType
AX_X = mybir.AxisListType.X

PASSES = ((0, 0), (0, 1), (1, 0))

B, S, D, H = 8, 512, 512, 16
DK = D // H
NT = S // P
NC = D // P
HG = P // DK
VW = 2 * DK + 2
FF = 2048
NF = FF // P
NB = 256
NL = NB // P
LN_EPS = 1e-5
UNIT_EPS = 1e-6
TAU = 10.0
MASKED = 1.0e9
QSCALE = -1.0 / float(DK) ** 0.5


def build(nc, x, ctxT, bias, mask, WqT, bq, WkT, bk, WvT, bv, WoT, bo, W1T, W2T,
          ln_g, ln_b, rWT, rb, rawU, rawV, gamma, out):
    qh_d, ql_d, kh_d, kl_d = (
        nc.dram_tensor(n, (NC * B, P, S), F32, kind="Internal").ap() for n in ("qh_d", "ql_d", "kh_d", "kl_d"))
    v_d = nc.dram_tensor("v_d", (NC * B, S, HG * VW), F32, kind="Internal").ap()
    pos_d = nc.dram_tensor("pos_d", (B, S, S), F32, kind="Internal").ap()
    att_d = nc.dram_tensor("att_d", (NC * B, S, P), F32, kind="Internal").ap()
    part_d = nc.dram_tensor("part_d", (B, S, D), F32, kind="Internal").ap()
    zh_d, zl_d = (nc.dram_tensor(n, (B, P, NC, S), F32, kind="Internal").ap() for n in ("zh_d", "zl_d"))

    with ExitStack() as top:
        ident = top.enter_context(nc.sbuf_tensor("ident", [P, P], F32))
        ones = top.enter_context(nc.sbuf_tensor("ones", [P, P], F32))
        neg_half = top.enter_context(nc.sbuf_tensor("neg_half", [P, NT], F32))
        project(nc, ident, ones, neg_half, x, ctxT, mask, WqT, bq, WkT, bk, WvT, bv,
                qh_d, ql_d, kh_d, kl_d, v_d, pos_d)
        attend(nc, ident, bias, qh_d, ql_d, kh_d, kl_d, v_d, pos_d, att_d)
        mix(nc, ident, ones, neg_half, x, att_d, WoT, bo, ln_g, ln_b, rWT, rb, rawU, rawV, gamma,
            part_d, zh_d, zl_d)
        feed(nc, W1T, W2T, zh_d, zl_d, part_d, out)


def tokens(ap):
    return ap.rearrange("(t p) n -> p t n", p=P)


def need(eng, semaphore, count):
    if not isinstance(count, int) or count > 0:
        eng.wait_ge(semaphore, count)


def gate(eng, passed):
    eng.sem_inc(passed, 1)


def behind(g, j, lag, steps, rounds):
    if j - lag >= 0:
        return None if isinstance(g, int) and g == rounds else (g, j - lag)
    return None if isinstance(g, int) and g == 0 else (g - 1, j - lag + steps)


def walk_rounds(eng, step, last, steps, rounds):
    for j in range(steps):
        step(0, j, True)
    with eng.Fori(1, rounds) as g:
        for j in range(steps):
            step(g, j, True)
    for j in range(last):
        step(rounds, j, False)


def project(nc, ident, ones, neg_half, x, ctxT, mask, WqT, bq, WkT, bk, WvT, bv,
            qh_d, ql_d, kh_d, kl_d, v_d, pos_d):
    NPJ = 3 * NC
    NPB = 4
    NTB = 3
    with ExitStack() as ctx:
        def sb(name, shape, dt=F32):
            return ctx.enter_context(nc.sbuf_tensor("p_" + name, shape, dt))

        def sem(name):
            return ctx.enter_context(nc.semaphore("p_" + name))

        x_raw = sb("x_raw", [P, NT, D])
        c_raw = sb("c_raw", [P, NC, S])
        m_raw = sb("m_raw", [P, NT, S], I32)
        w_h = [sb(f"w{n}_h", [P, NC, D], F32R) for n in "qkv"]
        w_l = [sb(f"w{n}_l", [P, NC, D], F32R) for n in "qkv"]
        xn = sb("xn", [P, NT, D])
        xT_h, xT_l = sb("xT_h", [P, NC, S], F32R), sb("xT_l", [P, NC, S], F32R)
        cT_h, cT_l = sb("cT_h", [P, NC, S], F32R), sb("cT_l", [P, NC, S], F32R)
        q_f = sb("q_f", [P, 2, S])
        v_f = sb("v_f", [P, 2, D])
        qk = [sb(n, [P, NC, S], F32R) for n in ("q_h", "q_l", "k_h", "k_l")]
        v_s = sb("v_s", [P, NT, H * VW], F32R)
        v_s4 = v_s[:, :, :].rearrange("p t (h w) -> p t h w", h=H)
        pos = sb("pos", [P, NT, S])
        pos_min = sb("pos_min", [P, NT])
        q_fac = sb("q_fac", [P, NT])
        fac_cols = sb("fac_cols", [P, NT, P])
        fac_row = sb("fac_row", [P, S])
        bq_c, bk_c = sb("bq_c", [P, NC]), sb("bk_c", [P, NC])
        bv_r = sb("bv_r", [P, D])
        stats = sb("stats", [P, NT, 6])
        mv = sb("mv", [P, NT, 2])
        var_e = sb("var_e", [P, NT])
        rstd = sb("rstd", [P, NT])

        ps_t = ctx.enter_context(nc.psum_tensor("p_ps_t", [P, NTB, S], F32))
        ps_j = ctx.enter_context(nc.psum_tensor("p_ps_j", [P, NPB, D], F32))
        ps_f = ctx.enter_context(nc.psum_tensor("p_ps_f", [P, S], F32))

        consts_made = sem("consts_made")
        consts_zeroed = sem("consts_zeroed")
        small_in = sem("small_in")
        x_in, c_in, m_in = sem("x_in"), sem("c_in"), sem("m_in")
        kw_in, vw_in, qw_in = sem("kw_in"), sem("vw_in"), sem("qw_in")
        w_high, w_low = sem("w_high"), sem("w_low")
        pos_done, min_done, fac_done, cols_done = sem("pos_done"), sem("min_done"), sem("fac_done"), sem("cols_done")
        stats_done, mv_done, var_done, rstd_done, xn_done = (
            sem("stats_done"), sem("mv_done"), sem("var_done"), sem("rstd_done"), sem("xn_done"))
        x_turned, xT_high, xT_low = sem("x_turned"), sem("xT_high"), sem("xT_low")
        cT_high, cT_low = sem("cT_high"), sem("cT_low")
        fac_turned, fac_row_done = sem("fac_turned"), sem("fac_row_done")
        projected, bank_free = sem("projected"), sem("bank_free")
        qf_done, q_high, q_low = sem("qf_done"), sem("q_high"), sem("q_low")
        k_high = sem("k_high")
        vf_done, v_high, v_low = sem("vf_done"), sem("v_high"), sem("v_low")
        pos_out, k_out, q_out, v_out = sem("pos_out"), sem("k_out"), sem("q_out"), sem("v_out")
        v_ones = sem("v_ones")
        passed = sem("passed")

        K_AT, V_AT, Q_AT = 0, NC, NC + NT

        staging = ((1, xn[:, :, :], kw_in, WkT), (2, m_raw[:, :, :].bitcast(F32), vw_in, WvT),
                   (0, pos[:, :, :], qw_in, WqT))

        def walk(eng, body):
            with eng.Fori(0, B - 1) as b:
                body(b, True)
            body(B - 1, False)

        block = ctx.enter_context(nc.Block())

        @block.sync
        def _(sp):
            def load_weight(n):
                _, raw, loaded, source = staging[n]
                sp.dma_start(raw, tokens(source)).then_inc(loaded, 16)

            sp.sem_inc(pos_out, 16)
            sp.sem_inc(k_out, 32)
            sp.sem_inc(q_out, 32)
            sp.sem_inc(v_out, 16 * NC)

            def load_x(b):
                sp.dma_start(x_raw[:, :, :], tokens(x[b])).then_inc(x_in, 16)

            def load_c(b):
                sp.dma_start(c_raw[:, :, :], tokens(ctxT[b])).then_inc(c_in, 16)

            def load_m(b):
                sp.dma_start(m_raw[:, :, :], tokens(mask[b])).then_inc(m_in, 16)

            def store_qk(b, parts, out):
                for n, dst in parts:
                    sp.dma_start(dst.rearrange("(c b) p n -> b p c n", c=NC)[b],
                                 qk[n][:, :, :].bitcast(F32)).then_inc(out, 16)

            def body(b, more):
                if more:
                    sp.wait_ge(cT_low, b + 1)
                    load_c(b + 1)
                    sp.wait_ge(xn_done, NT * (b + 1))
                    load_x(b + 1)
                sp.wait_ge(bank_free, NPB + NPJ * b + K_AT + NC)
                store_qk(b, ((2, kh_d), (3, kl_d)), k_out)
                sp.wait_ge(pos_done, b + 1)
                sp.dma_start(tokens(pos_d[b]), pos[:, :, :]).then_inc(pos_out, 16)
                if more:
                    load_m(b + 1)
                sp.wait_ge(v_high, NT * (b + 1))
                sp.wait_ge(v_low, NT * (b + 1))
                for c in range(NC):
                    sp.dma_start(tokens(v_d[B * c + b]),
                                 v_s[:, :, c * HG * VW:(c + 1) * HG * VW].bitcast(F32)).then_inc(v_out, 16)
                sp.wait_ge(q_high, NC * (b + 1))
                sp.wait_ge(q_low, NC * (b + 1))
                store_qk(b, ((0, qh_d), (1, ql_d)), q_out)

            load_weight(0)
            load_c(0)
            load_x(0)
            sp.dma_start(bq_c[:, :], bq).then_inc(small_in, 16)
            sp.dma_start(bk_c[:, :], bk).then_inc(small_in, 16)
            sp.dma_start(bv_r[:, :], bv.rearrange("(a n) -> a n", a=1).broadcast_to([P, D])).then_inc(small_in, 16)
            load_weight(1)
            load_weight(2)
            sp.wait_ge(w_low, 2)
            load_m(0)
            walk(sp, body)
            sp.wait_ge(pos_out, 16 * (B + 1))
            sp.wait_ge(k_out, 32 * (B + 1))
            sp.wait_ge(q_out, 32 * (B + 1))
            sp.wait_ge(v_out, 16 * NC * (B + 1))

        @block.gpsimd
        def _(pool):
            pool.memset(ident[:, :], 0.0).then_inc(consts_zeroed, 1)
            pool.memset(ones[:, :], 1.0).then_inc(consts_made, 1)
            pool.memset(neg_half[:, :], -0.5).then_inc(consts_made, 1)
            pool.wait_ge(consts_zeroed, 1)
            pool.affine_select(out=ident[:, :], in_=ident[:, :], compare_op=ALU.not_equal, fill=1.0, base=0,
                               pattern=[[-1, P]], channel_multiplier=1).then_inc(consts_made, 1)
            pool.wait_ge(consts_made, 3)

            def body(b, more):
                pool.wait_ge(var_done, b + 1)
                pool.tensor_tensor(out=rstd[:, :], in0=var_e[:, :], in1=neg_half[:, :], op=ALU.pow) \
                    .then_inc(rstd_done, 1)
                for t in range(NT):
                    pool.wait_ge(v_high, NT * b + t + 1)
                    pool.wait_ge(v_out, 16 * NC * (b + 1))
                    pool.tensor_tensor(
                        out=v_s4[:, t, :, DK:2 * DK],
                        in0=v_f[:, t % 2, :].rearrange("p (h d) -> p h d", h=H),
                        in1=v_s4[:, t, :, 0:DK].bitcast(F32), op=ALU.subtract).then_inc(v_low, 1)
                for c in range(NC):
                    pool.wait_ge(q_high, NC * b + c + 1)
                    pool.wait_ge(q_out, 32 * (b + 1))
                    pool.tensor_tensor(out=qk[1][:, c, :], in0=q_f[:, c % 2, :], in1=qk[0][:, c, :].bitcast(F32),
                                       op=ALU.subtract).then_inc(q_low, 1)

            walk(pool, body)

        @block.vector
        def _(dve):
            dve.sem_inc(bank_free, NPB)
            dve.memset(v_s4[:, :, :, 2 * DK:2 * DK + 1].bitcast(F32), 1.0).then_inc(v_ones, 1)
            dve.memset(v_s4[:, :, :, 2 * DK + 1:VW].bitcast(F32), 0.0).then_inc(v_ones, 1)

            def weight_low(k):
                n, raw, _, _ = staging[k]
                dve.wait_ge(w_high, k + 1)
                dve.tensor_tensor(out=w_l[n][:, :, :], in0=raw, in1=w_h[n][:, :, :].bitcast(F32),
                                  op=ALU.subtract).then_inc(w_low, 1)

            def context_low(b):
                dve.wait_ge(cT_high, b + 1)
                dve.tensor_tensor(out=cT_l[:, :, :], in0=c_raw[:, :, :], in1=cT_h[:, :, :].bitcast(F32),
                                  op=ALU.subtract).then_inc(cT_low, 1)

            def key_low(b, c):
                n = K_AT + c
                dve.wait_ge(k_high, NC * b + c + 1)
                dve.scalar_tensor_tensor(out=qk[3][:, c, :], in0=ps_j[:, n % NPB, :], scalar=bk_c[:, c:c + 1],
                                         in1=qk[2][:, c, :].bitcast(F32), op0=ALU.add, op1=ALU.subtract) \
                    .then_inc(bank_free, 1)

            def body(b, more):
                dve.wait_ge(x_in, 16 * b + 16)
                for t in range(NT):
                    dve.bn_stats(stats[:, t, :], x_raw[:, t, :]).then_inc(stats_done, 1)
                dve.wait_ge(stats_done, NT * (b + 1))
                gate(dve, passed)
                for t in range(NT):
                    dve.bn_aggr(mv[:, t, :], stats[:, t, :]).then_inc(mv_done, 1)
                dve.wait_ge(mv_done, NT * (b + 1))
                dve.tensor_scalar(var_e[:, :], mv[:, :, 1], LN_EPS, None, ALU.add).then_inc(var_done, 1)
                key_low(b, 0)
                dve.wait_ge(rstd_done, b + 1)
                for t in range(NT):
                    dve.tensor_scalar(xn[:, t, :], x_raw[:, t, :], mv[:, t, 0:1], rstd[:, t:t + 1],
                                      ALU.subtract, ALU.mult).then_inc(xn_done, 1)
                for c in range(1, NC):
                    key_low(b, c)
                for c in range(NC):
                    dve.wait_ge(xT_high, NC * b + c + 1)
                    dve.tensor_tensor(out=xT_l[:, c, :], in0=ps_t[:, c % NTB, :], in1=xT_h[:, c, :].bitcast(F32),
                                      op=ALU.subtract).then_inc(xT_low, 1)
                dve.wait_ge(m_in, 16 * b + 16)
                dve.wait_ge(pos_out, 16 * (b + 1))
                dve.tensor_scalar(pos[:, :, :], m_raw[:, :, :], 0.0, MASKED, ALU.is_equal, ALU.mult) \
                    .then_inc(pos_done, 1)
                dve.wait_ge(pos_done, b + 1)
                dve.tensor_reduce(pos_min[:, :], pos[:, :, :], AX_X, ALU.min).then_inc(min_done, 1)
                dve.wait_ge(min_done, b + 1)
                dve.tensor_scalar(q_fac[:, :], pos_min[:, :], 0.0, QSCALE, ALU.is_equal, ALU.mult) \
                    .then_inc(fac_done, 1)
                dve.wait_ge(fac_done, b + 1)
                for t in range(NT):
                    dve.tensor_scalar(fac_cols[:, t, :], ones[:, :], q_fac[:, t:t + 1], None, ALU.mult) \
                        .then_inc(cols_done, 1)
                for t in range(NT):
                    n = V_AT + t
                    dve.wait_ge(projected, NPJ * b + n + 1)
                    if t >= 2:
                        dve.wait_ge(v_low, NT * b + t - 1)
                    dve.tensor_tensor(out=v_f[:, t % 2, :], in0=ps_j[:, n % NPB, :], in1=bv_r[:, :], op=ALU.add) \
                        .then_inc(bank_free, 1)
                if more:
                    context_low(b + 1)
                dve.wait_ge(fac_row_done, b + 1)
                for c in range(NC):
                    n = Q_AT + c
                    dve.wait_ge(projected, NPJ * b + n + 1)
                    if c >= 2:
                        dve.wait_ge(q_low, NC * b + c - 1)
                    dve.scalar_tensor_tensor(out=q_f[:, c % 2, :], in0=ps_j[:, n % NPB, :], scalar=bq_c[:, c:c + 1],
                                             in1=fac_row[:, :], op0=ALU.add, op1=ALU.mult) \
                        .then_inc(bank_free, 1)

            weight_low(0)
            context_low(0)
            weight_low(1)
            weight_low(2)
            dve.wait_ge(consts_made, 3)
            dve.wait_ge(small_in, 48)
            walk(dve, body)

        @block.scalar
        def _(act):
            def weight_high(k):
                n, raw, loaded, _ = staging[k]
                act.wait_ge(loaded, 16)
                act.activation(w_h[n][:, :, :], raw, ACT.Copy).then_inc(w_high, 1)

            def context_high(b):
                act.wait_ge(c_in, 16 * b + 16)
                act.activation(cT_h[:, :, :], c_raw[:, :, :], ACT.Copy).then_inc(cT_high, 1)

            def body(b, more):
                act.wait_ge(k_out, 32 * (b + 1))
                for c in range(NC):
                    n = K_AT + c
                    act.wait_ge(projected, NPJ * b + n + 1)
                    act.activation(qk[2][:, c, :], ps_j[:, n % NPB, :], ACT.Identity, bias=bk_c[:, c:c + 1]) \
                        .then_inc(k_high, 1)
                for c in range(NC):
                    act.wait_ge(x_turned, NC * b + c + 1)
                    act.activation(xT_h[:, c, :], ps_t[:, c % NTB, :], ACT.Copy).then_inc(xT_high, 1)
                act.wait_ge(v_out, 16 * NC * (b + 1))
                for t in range(NT):
                    act.wait_ge(bank_free, NPB + NPJ * b + V_AT + t + 1)
                    act.activation(v_s4[:, t, :, 0:DK], v_f[:, t % 2, :].rearrange("p (h d) -> p h d", h=H),
                                   ACT.Copy).then_inc(v_high, 1)
                if more:
                    context_high(b + 1)
                act.wait_ge(fac_turned, b + 1)
                act.activation(fac_row[:, :], ps_f[:, :], ACT.Copy).then_inc(fac_row_done, 1)
                act.wait_ge(q_out, 32 * (b + 1))
                for c in range(NC):
                    act.wait_ge(bank_free, NPB + NPJ * b + Q_AT + c + 1)
                    act.activation(qk[0][:, c, :], q_f[:, c % 2, :], ACT.Copy).then_inc(q_high, 1)

            weight_high(0)
            context_high(0)
            weight_high(1)
            weight_high(2)
            act.wait_ge(small_in, 48)
            act.wait_ge(v_ones, 2)
            walk(act, body)

        @block.tensor
        def _(pe):
            pe.wait_ge(consts_made, 3)

            def body(b, more):
                def product(n, pairs):
                    pe.wait_ge(bank_free, NPJ * b + n + 1)
                    for k, (w, m) in enumerate(pairs):
                        last = pe.matmul(ps_j[:, n % NPB, :], w, m, start=k == 0, stop=k == len(pairs) - 1)
                    last.then_inc(projected, 1)

                def features(w, a, c):
                    cs = slice(c * P, (c + 1) * P)
                    return [(w[m][:, k, cs], a[n][:, k, :]) for k in range(NC) for m, n in PASSES]

                pe.wait_ge(w_low, 1)
                pe.wait_ge(cT_low, b + 1)
                for c in range(NC):
                    product(K_AT + c, features((w_h[1], w_l[1]), (cT_h, cT_l), c))
                pe.wait_ge(xn_done, NT * (b + 1))
                for c in range(NC):
                    if c >= NTB:
                        pe.wait_ge(xT_low, NC * b + c - NTB + 1)
                    for t in range(NT):
                        last = pe.transpose(ps_t[:, c % NTB, t * P:(t + 1) * P], xn[:, t, c * P:(c + 1) * P],
                                            ident[:, :])
                    last.then_inc(x_turned, 1)
                pe.wait_ge(w_low, 2)
                for t in range(NT):
                    ts = slice(t * P, (t + 1) * P)
                    product(V_AT + t, [(a[:, k, ts], w[:, k, :]) for k in range(NC)
                                       for a, w in ((cT_h, w_h[2]), (cT_h, w_l[2]), (cT_l, w_h[2]))])
                pe.wait_ge(cols_done, NT * (b + 1))
                for t in range(NT):
                    last = pe.matmul(ps_f[:, t * P:(t + 1) * P], fac_cols[:, t, :], ident[:, :], start=True, stop=True)
                last.then_inc(fac_turned, 1)
                pe.wait_ge(w_low, 3)
                pe.wait_ge(xT_low, NC * (b + 1))
                for c in range(NC):
                    product(Q_AT + c, features((w_h[0], w_l[0]), (xT_h, xT_l), c))

            walk(pe, body)


def attend(nc, ident, bias, qh_d, ql_d, kh_d, kl_d, v_d, pos_d, att_d):
    UR = 2 * HG
    TR = UR * NT
    ROUNDS = NC * B // 2
    NS = 2
    NN = 8
    NE = 4
    NP = 4
    TURN, PV, BACK = 2, 8, 12
    HIGH, OUT, COPY = 2, 10, 13
    LOW, NORM = 3, 15
    with ExitStack() as ctx:
        def sb(name, shape, dt=F32):
            return ctx.enter_context(nc.sbuf_tensor("a_" + name, shape, dt))

        def sem(name):
            return ctx.enter_context(nc.semaphore("a_" + name))

        q4 = sb("q4", [P, 2, HG, S], F32R)
        k4 = sb("k4", [P, 2, HG, S], F32R)
        v = sb("v", [P, 2, NT, HG * VW], F32R)
        pos = sb("pos", [P, 2, NT, S])
        bias_t = sb("bias_t", [P, HG, NT, S])
        nbm = sb("nbm", [P, NN, S])
        sc = sb("sc", [P, NE, S])
        nmax = sb("nmax", [P, NE])
        pr = sb("pr", [P, NE, S])
        pT_h, pT_l = sb("pT_h", [P, NP, NT, S], F32R), sb("pT_l", [P, NP, NT, S], F32R)
        o_sb = sb("o_sb", [2 * DK + 1, 2, S])
        rsum = sb("rsum", [P, 2, NT])
        c_sb = sb("c_sb", [P, 2, NT, 2 * DK + 1])
        o_sum = sb("o_sum", [P, 2, NT, DK])
        y = sb("y", [P, 2, NT, HG * DK])

        ps_s = ctx.enter_context(nc.psum_tensor("a_ps_s", [P, NS, S], F32))
        ps_t = ctx.enter_context(nc.psum_tensor("a_ps_t", [P, 2, S], F32))
        ps_o = ctx.enter_context(nc.psum_tensor("a_ps_o", [P, 2, S], F32))
        ps_c = ctx.enter_context(nc.psum_tensor("a_ps_c", [P, NT, 2 * DK + 1], F32))

        qkv_in = [sem("qkv_in0"), sem("qkv_in1")]
        pos_in = [sem("pos_in0"), sem("pos_in1")]
        bias_in = [sem(f"bias_in{i}") for i in range(HG)]
        nbm_done = sem("nbm_done")
        scored, summed, exped, turned, high, low, pv_done = (
            sem("scored"), sem("summed"), sem("exped"), sem("turned"), sem("high"), sem("low"), sem("pv_done"))
        o_copied, turned_back, c_copied = sem("o_copied"), sem("turned_back"), sem("c_copied")
        inverted, y_done = sem("inverted"), sem("y_done")
        y_out = [sem("y_out0"), sem("y_out1")]
        passed = sem("passed")

        NLD = 9

        def lagged(g, j, lag):
            return behind(g, j, lag, TR, ROUNDS)

        def walk(eng, step, last):
            walk_rounds(eng, step, last, TR, ROUNDS)

        block = ctx.enter_context(nc.Block())

        @block.sync
        def _(sp):
            def load(g, j):
                n = 2 * g + j
                for t, (q_d, k_d) in enumerate(((qh_d, kh_d), (qh_d, kl_d), (ql_d, kh_d), (ql_d, kl_d))):
                    rows = slice(DK * t, DK * (t + 1))
                    sp.dma_start(q4[rows, j, :, :].bitcast(F32), q_d[n].rearrange("(i p) n -> p i n", p=DK)) \
                        .then_inc(qkv_in[j], 16)
                    sp.dma_start(k4[rows, j, :, :].bitcast(F32), k_d[n].rearrange("(i p) n -> p i n", p=DK)) \
                        .then_inc(qkv_in[j], 16)
                sp.dma_start(v[:, j, :, :].bitcast(F32), tokens(v_d[n])).then_inc(qkv_in[j], 16)

            def load_pos(g, j):
                sp.dma_start(pos[:, j, :, :], tokens(pos_d[g % (B // 2) * 2 + j])).then_inc(pos_in[j], 16)

            def store(g, j):
                sp.wait_ge(y_done, UR * g + HG * (j + 1))
                sp.dma_start(tokens(att_d[2 * g + j]), y[:, j, :, :]).then_inc(y_out[j], 16)

            load_pos(0, 0)
            load(0, 0)
            sp.wait_ge(bias_in[HG - 1], 16)
            load_pos(0, 1)
            load(0, 1)
            sp.sem_inc(y_out[0], 16)
            sp.sem_inc(y_out[1], 16)
            with sp.Fori(0, ROUNDS - 1) as g:
                for j in range(2):
                    sp.wait_ge(nbm_done, TR * g + (j + 1) * NT * HG)
                    load_pos(g + 1, j)
                    sp.wait_ge(pv_done, TR * g + (j + 1) * NT * HG)
                    load(g + 1, j)
                    store(g, j)
            for j in range(2):
                store(ROUNDS - 1, j)
            for n in range(2):
                sp.wait_ge(y_out[n], 16 * (ROUNDS + 1))

        @block.gpsimd
        def _(pool):
            def load_bias(hg, i):
                pool.dma_start(bias_t[:, i, :, :], tokens(bias[0, hg * HG + i])).then_inc(bias_in[i], 16)

            def step(hg, g, j):
                b, i, qt = j // (NT * HG), j // NT % HG, j % NT
                if j % (NT * HG) == 0:
                    pool.wait_ge(pos_in[b], 16 * g + 16)
                if qt == 0:
                    pool.wait_ge(bias_in[i], 16 * (hg + 1))
                pool.wait_ge(summed, TR * g + j + 1)
                pool.tensor_tensor(out=nbm[:, j % NN, :], in0=pos[:, b, qt, :], in1=bias_t[:, i, qt, :],
                                   op=ALU.subtract).then_inc(nbm_done, 1)

            load_bias(0, 0)
            pool.wait_ge(qkv_in[0], 16 * NLD)
            for i in range(1, HG):
                load_bias(0, i)
            for hg in range(NC):
                last = (hg + 1) * B // 2 - 1
                with pool.Fori(hg * (B // 2), last) as g:
                    for j in range(TR):
                        step(hg, g, j)
                for j in range(TR):
                    step(hg, last, j)
                    if hg < NC - 1 and j >= NT * HG + NT and j % NT == 0:
                        pool.wait_ge(nbm_done, TR * last + j)
                        load_bias(hg + 1, j // NT % HG - 1)
                if hg < NC - 1:
                    pool.wait_ge(nbm_done, TR * (last + 1))
                    load_bias(hg + 1, HG - 1)

        def tile(at):
            t = at[1]
            return t // (NT * HG), t // NT % HG, t % NT, t // NT

        def bank(at):
            return ps_t[:, at[1] % 2, :].rearrange("p (k n) -> p k n", k=NT)

        def turned_tile(a, at):
            return a[:, at[1] // NT % NP, :, at[1] % NT * P:(at[1] % NT + 1) * P]

        @block.tensor
        def _(pe):
            def step(g, j, more):
                if more:
                    b, i, qt, _ = tile((g, j))
                    if j % (NT * HG) == 0:
                        pe.wait_ge(qkv_in[b], 16 * NLD * g + 16 * NLD)
                    need(pe, summed, NN + TR * g + j - NS + 1 if lagged(g, j, NS) else 0)
                    pe.matmul(ps_s[:, j % NS, :], q4[:, b, i, qt * P:(qt + 1) * P], k4[:, b, i, :],
                              start=True, stop=True).then_inc(scored, 1)
                if at := lagged(g, j, PV):
                    n = TR * at[0] + at[1]
                    b, i, kt, u = tile(at)
                    if kt == 0:
                        pe.wait_ge(low, n + NT)
                        need(pe, o_copied, UR * at[0] + u - 1)
                    vt = v[:, b, kt, :].rearrange("p (h w) -> p h w", h=HG)
                    for part in (pT_h, pT_l):
                        last = pe.matmul(ps_o[0:2 * DK + 1, u % 2, :], vt[:, i, 0:2 * DK + 1], part[:, u % NP, kt, :],
                                         start=kt == 0 and part is pT_h, stop=kt == NT - 1 and part is pT_l)
                    last.then_inc(pv_done, 1)
                if (at := lagged(g, j, BACK)) and at[1] % NT == NT - 1:
                    u = at[1] // NT
                    pe.wait_ge(o_copied, UR * at[0] + u + 1)
                    need(pe, c_copied, UR * at[0] + u)
                    for qt in range(NT):
                        last = pe.transpose(ps_c[:, qt, :], o_sb[:, u % 2, qt * P:(qt + 1) * P],
                                            ident[0:2 * DK + 1, 0:2 * DK + 1])
                    last.then_inc(turned_back, 1)
                if at := lagged(g, j, TURN):
                    n = TR * at[0] + at[1]
                    need(pe, low, n - 1)
                    pe.wait_ge(exped, n + 1)
                    for kt in range(NT):
                        last = pe.transpose(ps_t[:, at[1] % 2, kt * P:(kt + 1) * P],
                                            pr[:, at[1] % NE, kt * P:(kt + 1) * P], ident[:, :])
                    last.then_inc(turned, 1)

            walk(pe, step, BACK)

        @block.vector
        def _(dve):
            dve.sem_inc(summed, NN)

            def step(g, j, more):
                if more:
                    n = TR * g + j
                    dve.wait_ge(scored, n + 1)
                    dve.wait_ge(nbm_done, n + 1)
                    need(dve, exped, n - NE + 1)
                    gate(dve, passed)
                    dve.tensor_tensor_reduce(sc[:, j % NE, :], ps_s[:, j % NS, :], nbm[:, j % NN, :], 1.0, 3.0e38,
                                             ALU.add, ALU.min, nmax[:, j % NE:j % NE + 1]).then_inc(summed, 1)
                norm = (at := lagged(g, j, NORM)) and at[1] % NT == NT - 1
                if norm:
                    b, i, _, u = tile(at)
                    n = UR * at[0] + u
                    dve.wait_ge(c_copied, n + 1)
                    dve.reciprocal(rsum[:, u % 2, :], c_sb[:, u % 2, :, 2 * DK]).then_inc(inverted, 1)
                    dve.tensor_tensor(out=o_sum[:, u % 2, :, :], in0=c_sb[:, u % 2, :, 0:DK],
                                      in1=c_sb[:, u % 2, :, DK:2 * DK], op=ALU.add).then_inc(inverted, 1)
                if low_at := lagged(g, j, LOW):
                    dve.wait_ge(high, TR * low_at[0] + low_at[1] + 1)
                    dve.tensor_tensor(out=turned_tile(pT_l, low_at), in0=bank(low_at),
                                      in1=turned_tile(pT_h, low_at).bitcast(F32), op=ALU.subtract).then_inc(low, 1)
                if norm:
                    dve.wait_ge(inverted, 2 * n + 2)
                    dve.wait_ge(y_out[b], 16 * at[0] + 16)
                    dve.tensor_tensor(out=y[:, b, :, i * DK:(i + 1) * DK], in0=o_sum[:, u % 2, :, :],
                                      in1=rsum[:, u % 2, :].rearrange("p (t o) -> p t o", o=1).broadcast_to([P, NT, DK]),
                                      op=ALU.mult).then_inc(y_done, 1)

            walk(dve, step, NORM)

        @block.scalar
        def _(act):
            def step(g, j, more):
                if more:
                    n = TR * g + j
                    act.wait_ge(summed, NN + n + 1)
                    need(act, turned, n - NE + 1)
                    act.activation(pr[:, j % NE, :], sc[:, j % NE, :], ACT.Exp, scale=-1.0,
                                   bias=nmax[:, j % NE:j % NE + 1]).then_inc(exped, 1)
                if at := lagged(g, j, HIGH):
                    n = TR * at[0] + at[1]
                    act.wait_ge(turned, n + 1)
                    if at[1] % NT == 0:
                        need(act, pv_done, n - (NP - 1) * NT)
                    act.activation(turned_tile(pT_h, at), bank(at), ACT.Copy).then_inc(high, 1)
                if (at := lagged(g, j, OUT)) and at[1] % NT == NT - 1:
                    u = at[1] // NT
                    n = UR * at[0] + u
                    act.wait_ge(pv_done, TR * at[0] + at[1] + 1)
                    need(act, turned_back, n - 1)
                    act.activation(o_sb[:, u % 2, :], ps_o[0:2 * DK + 1, u % 2, :], ACT.Copy).then_inc(o_copied, 1)

                if (at := lagged(g, j, COPY)) and at[1] % NT == NT - 1:
                    u = at[1] // NT
                    n = UR * at[0] + u
                    act.wait_ge(turned_back, n + 1)
                    need(act, y_done, n - 1)
                    act.activation(c_sb[:, u % 2, :, :], ps_c[:, :, :], ACT.Copy).then_inc(c_copied, 1)

            walk(act, step, COPY)


def mix(nc, ident, ones, neg_half, x, att_d, WoT, bo, ln_g, ln_b, rWT, rb, rawU, rawV, gamma, part_d, zh_d, zl_d):
    with ExitStack() as ctx:
        def sb(name, shape, dt=F32):
            return ctx.enter_context(nc.sbuf_tensor("m_" + name, shape, dt))

        def sem(name):
            return ctx.enter_context(nc.semaphore("m_" + name))

        att = sb("att", [P, NT, D])
        x_b = sb("x_b", [P, NT, D])
        aT = [sb("aT_h", [P, NC, S], F32R), sb("aT_l", [P, NC, S], F32R)]
        zT = [sb("zT_h", [P, NC, S], F32R), sb("zT_l", [P, NC, S], F32R)]
        hT = [sb("hT_h", [P, NL, S], F32R), sb("hT_l", [P, NL, S], F32R)]
        x1 = sb("x1", [P, 2, NT, D])
        z = sb("z", [P, NT, D])
        wo = [sb("wo_h", [P, NC, D], F32R), sb("wo_l", [P, NC, D], F32R)]
        ru = [sb("ru_h", [P, NC, 2 * NB], F32R), sb("ru_l", [P, NC, 2 * NB], F32R)]
        vg = [sb("vg_h", [P, NL, D], F32R), sb("vg_l", [P, NL, D], F32R)]
        bo_r, gam_r, rb_r, r_row = sb("bo_r", [P, D]), sb("gam_r", [P, D]), sb("rb_r", [P, NB]), sb("r_row", [P, NB])
        g_c, b_c = sb("g_c", [P, NC]), sb("b_c", [P, NC])
        b_cols = sb("b_cols", [P, NC, P])
        g_mean = sb("g_mean", [P, NB])
        rw_f = sb("rw_f", [P, NC, NB])
        rc, hl, sel = sb("rc", [P, NT, NB]), sb("hl", [P, NT, NB]), sb("sel", [P, NT, NB])
        r_abs, u = sb("r_abs", [P, NT, NB]), sb("u", [P, NT, NB])
        w, ln_w = sb("w", [P, NT, NB]), sb("ln_w", [P, NT, NB])
        top = sb("top", [P, NT, 8])
        ssum, tanh_s, coef = sb("ssum", [P, NT]), sb("tanh_s", [P, NT]), sb("coef", [P, NT])
        stats, mv = sb("stats", [P, NT, 6]), sb("mv", [P, NT, 2])
        var_e, rstd, var_z, eps_t = sb("var_e", [P, NT]), sb("rstd", [P, NT]), sb("var_z", [P, NT]), sb("eps_t", [P, NT])
        rs = sb("rs", [P, 2, NT])
        nrm, nrm_s, nrm_r = sb("nrm", [P, 2 * NL]), sb("nrm_s", [P, 2 * NL]), sb("nrm_r", [P, 2 * NL])

        ps_t = ctx.enter_context(nc.psum_tensor("m_ps_t", [P, 2, S], F32))
        ps_o = ctx.enter_context(nc.psum_tensor("m_ps_o", [P, NT, D], F32))
        ps_r = ctx.enter_context(nc.psum_tensor("m_ps_r", [P, 2, 2 * NB], F32))

        rows_in, w_in, lat_in = sem("rows_in"), sem("w_in"), sem("lat_in")
        lat_sq, lat_root, lat_max, lat_inv, lat_unit, lat_gam, lat_turned = (
            sem(n) for n in ("lat_sq", "lat_root", "lat_max", "lat_inv", "lat_unit", "lat_gam", "lat_turned"))
        g_scaled, g_summed, g_mean_done, g_centred = (
            sem(n) for n in ("g_scaled", "g_summed", "g_mean_done", "g_centred"))
        w_high, w_low = sem("w_high"), sem("w_low")
        att_in, x_in, xb_done = sem("att_in"), sem("x_in"), sem("xb_done")
        turned, t_high, t_low = sem("turned"), sem("t_high"), sem("t_low")
        o_ready, o_read = sem("o_ready"), sem("o_read")
        stats_done, mv_done, var_done, rstd_done, vz_done, z_done = (
            sem(n) for n in ("stats_done", "mv_done", "var_done", "rstd_done", "vz_done", "z_done"))
        eps_made = sem("eps_made")
        r_ready, r_read, hl_read = sem("r_ready"), sem("r_read"), sem("hl_read")
        clip_done, top_done, rep_done, sel_done = (
            sem(n) for n in ("clip_done", "top_done", "rep_done", "sel_done"))
        abs_done, u_done, w_done, ln_done, err_done, rest_done, al_done = (
            sem(n) for n in ("abs_done", "u_done", "w_done", "ln_done", "err_done", "rest_done", "al_done"))
        sum_done, tanh_done, den_done, dinv_done, coef_done, hz_done = (
            sem(n) for n in ("sum_done", "tanh_done", "den_done", "dinv_done", "coef_done", "hz_done"))
        z_out, part_out = sem("z_out"), sem("part_out")
        passed = sem("passed")

        TURNS = 2 * NC + NL
        SUMS = 2 * NT

        def turns_of(b, last):
            n = 2 * NC + TURNS * b
            return (None, n, None) if last else (n, n + NC, n + NC + NL)

        def sums_of(b, last):
            n = NT + SUMS * b
            return (None, n) if last else (n, n + NT)

        def walk(eng, front, body):
            front()
            with eng.Fori(0, B // 2 - 1) as r:
                for p in range(2):
                    body(2 * r + p, p, False)
            body(B - 2, 0, False)
            body(B - 1, 1, True)

        block = ctx.enter_context(nc.Block())

        @block.sync
        def _(sp):
            def row(v, n):
                return v.rearrange("(a n) -> a n", a=1).broadcast_to([P, n])

            sp.dma_start(att[:, :, :], tokens(WoT)).then_inc(w_in, 16)
            sp.dma_start(rw_f[:, :, :], tokens(rWT)).then_inc(w_in, 16)
            sp.dma_start(z[:, 0:NL, :], tokens(rawU)).then_inc(lat_in, 16)
            sp.dma_start(z[:, NL:2 * NL, :], tokens(rawV)).then_inc(lat_in, 16)
            for dst, v, n in ((bo_r, bo, D), (gam_r, gamma, D), (rb_r, rb, NB)):
                sp.dma_start(dst[:, :], row(v, n)).then_inc(rows_in, 16)
            sp.dma_start(g_c[:, :], ln_g).then_inc(rows_in, 16)
            sp.dma_start(b_c[:, :], ln_b).then_inc(rows_in, 16)
            sp.sem_inc(part_out, 16)

            def load_att(b):
                for c in range(NC):
                    sp.dma_start(att[:, :, c * P:(c + 1) * P], tokens(att_d[B * c + b])).then_inc(att_in, 16)

            def load_x(b):
                sp.dma_start(x_b[:, :, :], tokens(x[b])).then_inc(x_in, 16)

            def store_z(b, n):
                sp.wait_ge(t_low, n + NC)
                sp.dma_start(zh_d[b], zT[0][:, :, :].bitcast(F32)).then_inc(z_out, 16)
                sp.dma_start(zl_d[b], zT[1][:, :, :].bitcast(F32)).then_inc(z_out, 16)

            def front():
                load_x(0)
                sp.wait_ge(w_low, 1)
                load_att(0)
                sp.wait_ge(turned, NC)
                load_att(1)
                sp.wait_ge(o_read, NT)
                load_x(1)
                store_z(0, NC)

            def body(b, p, last):
                t_att, _, t_z = turns_of(b, last)
                s_out, s_lat = sums_of(b, last)
                if not last and not (isinstance(b, int) and b == B - 2):
                    sp.wait_ge(turned, t_att + NC)
                    load_att(b + 2)
                    sp.wait_ge(o_read, s_out + NT)
                    load_x(b + 2)
                if not last:
                    store_z(b + 1, t_z)
                sp.wait_ge(o_read, s_lat + NT)
                sp.dma_start(tokens(part_d[b]), x1[:, p, :, :]).then_inc(part_out, 16)

            walk(sp, front, body)
            sp.wait_ge(z_out, 32 * B)
            sp.wait_ge(part_out, 16 * (B + 1))

        @block.gpsimd
        def _(pool):
            pool.memset(eps_t[:, :], LN_EPS).then_inc(eps_made, 1)
            pool.wait_ge(eps_made, 1)
            pool.wait_ge(rows_in, 16 * 5)

            def add_bo(b):
                pool.wait_ge(x_in, 16 * b + 16)
                for t in range(NT):
                    pool.tensor_tensor(out=x_b[:, t, :], in0=x_b[:, t, :], in1=bo_r[:, :], op=ALU.add) \
                        .then_inc(xb_done, 1)

            def roots(b, p):
                pool.wait_ge(var_done, b + 1)
                pool.tensor_tensor(out=rstd[:, :], in0=var_e[:, :], in1=neg_half[:, :], op=ALU.pow) \
                    .then_inc(rstd_done, 1)
                pool.wait_ge(rstd_done, b + 1)
                pool.tensor_tensor(out=var_z[:, :], in0=rstd[:, :], in1=rstd[:, :], op=ALU.mult).then_inc(vz_done, 1)
                pool.wait_ge(vz_done, 4 * b + 1)
                pool.tensor_tensor(out=var_z[:, :], in0=var_z[:, :], in1=mv[:, :, 1], op=ALU.mult).then_inc(vz_done, 1)
                pool.wait_ge(vz_done, 4 * b + 2)
                pool.tensor_tensor(out=var_z[:, :], in0=var_z[:, :], in1=eps_t[:, :], op=ALU.add).then_inc(vz_done, 1)
                pool.wait_ge(vz_done, 4 * b + 3)
                pool.tensor_tensor(out=rs[:, p, :], in0=var_z[:, :], in1=neg_half[:, :], op=ALU.pow) \
                    .then_inc(vz_done, 1)

            def front():
                add_bo(0)
                roots(0, 0)

            def body(b, p, last):
                if not last:
                    add_bo(b + 1)
                if not last:
                    roots(b + 1, 1 - p)

            walk(pool, front, body)

        @block.vector
        def _(dve):
            def split(n, hi, lo, src):
                dve.tensor_copy(hi, src).then_inc(w_high, 1)
                dve.wait_ge(w_high, n + 1)
                dve.tensor_tensor(out=lo, in0=src, in1=hi.bitcast(F32), op=ALU.subtract).then_inc(w_low, 1)

            dve.wait_ge(w_in, 32)
            split(0, wo[0][:, :, :], wo[1][:, :, :], att[:, :, :])
            dve.wait_ge(rows_in, 16 * 5)
            for c in range(NC):
                dve.tensor_scalar(b_cols[:, c, :], ones[:, :], b_c[:, c:c + 1], None, ALU.mult).then_inc(g_scaled, 1)
            for c in range(NC):
                dve.tensor_scalar(rc[:, c, :], rw_f[:, c, :], g_c[:, c:c + 1], None, ALU.mult).then_inc(g_scaled, 1)
            dve.wait_ge(lat_in, 32)
            for n in range(2 * NL):
                dve.tensor_tensor_reduce(x1[:, 1, n, :], z[:, n, :], z[:, n, :], 1.0, 0.0, ALU.mult, ALU.add,
                                         nrm[:, n:n + 1]).then_inc(lat_sq, 1)
            dve.wait_ge(lat_root, 1)
            dve.tensor_scalar(nrm[:, :], nrm_s[:, :], UNIT_EPS, None, ALU.max).then_inc(lat_max, 1)
            dve.wait_ge(lat_max, 1)
            dve.reciprocal(nrm_r[:, :], nrm[:, :]).then_inc(lat_inv, 1)
            dve.wait_ge(lat_inv, 1)
            for n in range(2 * NL):
                dve.tensor_scalar(x1[:, 0, n, :], z[:, n, :], nrm_r[:, n:n + 1], None, ALU.mult).then_inc(lat_unit, 1)
            dve.wait_ge(lat_unit, 2 * NL)
            for n in range(NL, 2 * NL):
                dve.tensor_tensor(out=x1[:, 1, n, :], in0=x1[:, 0, n, :], in1=gam_r[:, :], op=ALU.mult) \
                    .then_inc(lat_gam, 1)
            dve.wait_ge(lat_gam, NL)
            split(1, vg[0][:, :, :], vg[1][:, :, :], x1[:, 1, NL:2 * NL, :])
            dve.wait_ge(g_summed, 2)
            dve.tensor_scalar(g_mean[:, :], ps_r[:, 0, 0:NB], 1.0 / D, None, ALU.mult).then_inc(g_mean_done, 1)
            dve.tensor_tensor(out=r_row[:, :], in0=ps_r[:, 1, 0:NB], in1=rb_r[:, :], op=ALU.add) \
                .then_inc(g_mean_done, 1)
            dve.wait_ge(g_mean_done, 2)
            for c in range(NC):
                dve.tensor_tensor(out=rc[:, c, :], in0=rc[:, c, :], in1=g_mean[:, :], op=ALU.subtract) \
                    .then_inc(g_centred, 1)
            dve.wait_ge(g_centred, NC)
            split(2, ru[0][:, :, 0:NB], ru[1][:, :, 0:NB], rc[:, :, :])
            for h in range(2):
                dve.wait_ge(lat_turned, h + 1)
                split(3 + h, ru[0][:, 2 * h:2 * h + 2, NB:2 * NB], ru[1][:, 2 * h:2 * h + 2, NB:2 * NB],
                      ps_t[:, h, :].rearrange("p (c n) -> p c n", n=NB))
            dve.sem_inc(r_read, 2)

            def lows(n, dst, count):
                for c in range(count):
                    dve.wait_ge(t_high, n + c + 1)
                    dve.tensor_tensor(out=dst[1][:, c, :], in0=ps_t[:, c % 2, :], in1=dst[0][:, c, :].bitcast(F32),
                                      op=ALU.subtract).then_inc(t_low, 1)

            def residual(b, p, n, tiles):
                if tiles[0] == 0:
                    need(dve, part_out, 16 * b)
                for t in tiles:
                    dve.wait_ge(xb_done, NT * b + t + 1)
                    dve.wait_ge(o_ready, n + t + 1)
                    dve.tensor_tensor(out=x1[:, p, t, :], in0=ps_o[:, t, :], in1=x_b[:, t, :], op=ALU.add) \
                        .then_inc(o_read, 1)

            def moments(b, p, n):
                for t in range(NT):
                    dve.wait_ge(o_read, n + t + 1)
                    dve.bn_stats(stats[:, t, :], x1[:, p, t, :]).then_inc(stats_done, 1)
                need(dve, vz_done, 4 * b)
                dve.wait_ge(stats_done, NT * (b + 1))
                gate(dve, passed)
                for t in range(NT):
                    dve.bn_aggr(mv[:, t, :], stats[:, t, :]).then_inc(mv_done, 1)
                dve.wait_ge(mv_done, NT * (b + 1))
                dve.tensor_scalar(var_e[:, :], mv[:, :, 1], LN_EPS, None, ALU.add).then_inc(var_done, 1)

            def normalise(b, p):
                dve.wait_ge(rstd_done, b + 1)
                for t in range(NT):
                    dve.tensor_scalar(z[:, t, :], x1[:, p, t, :], mv[:, t, 0:1], rstd[:, t:t + 1],
                                      ALU.subtract, ALU.mult).then_inc(z_done, 1)

            def route(b, p):
                dve.wait_ge(vz_done, 4 * b + 4)
                for t in range(NT):
                    dve.wait_ge(r_ready, NT * b + t + 1)
                    dve.scalar_tensor_tensor(out=rc[:, t, :], in0=ps_r[:, t % 2, 0:NB], scalar=rs[:, p, t:t + 1],
                                             in1=r_row[:, :], op0=ALU.mult, op1=ALU.add).then_inc(r_read, 1)
                dve.wait_ge(r_read, 2 + NT * (b + 1))
                dve.tensor_scalar(rc[:, :, :], rc[:, :, :], -TAU, TAU, ALU.max, ALU.min).then_inc(clip_done, 1)
                dve.wait_ge(clip_done, b + 1)
                gate(dve, passed)
                for t in range(NT):
                    dve.max(top[:, t, :], rc[:, t, :]).then_inc(top_done, 1)
                dve.wait_ge(top_done, NT * (b + 1))
                gate(dve, passed)
                for t in range(NT):
                    dve.match_replace(sel[:, t, :], top[:, t, :], rc[:, t, :], -1.0e30).then_inc(rep_done, 1)
                dve.wait_ge(rep_done, NT * (b + 1))
                dve.tensor_tensor(out=sel[:, :, :], in0=sel[:, :, :], in1=rc[:, :, :], op=ALU.not_equal) \
                    .then_inc(sel_done, 1)

            def weigh(b):
                dve.wait_ge(w_done, b + 1)
                dve.scalar_tensor_tensor(out=w[:, :, :], in0=w[:, :, :], scalar=-1.0, in1=u[:, :, :],
                                         op0=ALU.add, op1=ALU.subtract).then_inc(err_done, 1)
                dve.wait_ge(err_done, b + 1)
                dve.scalar_tensor_tensor(out=w[:, :, :], in0=rc[:, :, :], scalar=0.0, in1=w[:, :, :],
                                         op0=ALU.max, op1=ALU.subtract).then_inc(rest_done, 1)
                dve.wait_ge(rest_done, b + 1)
                dve.wait_ge(ln_done, b + 1)
                dve.tensor_tensor(out=w[:, :, :], in0=w[:, :, :], in1=ln_w[:, :, :], op=ALU.add).then_inc(al_done, 1)
                dve.wait_ge(al_done, b + 1)
                dve.wait_ge(sel_done, b + 1)
                gate(dve, passed)
                for t in range(NT):
                    dve.tensor_tensor_reduce(sel[:, t, :], w[:, t, :], sel[:, t, :], 1.0, 0.0, ALU.mult, ALU.add,
                                             ssum[:, t:t + 1]).then_inc(sum_done, 1)
                dve.wait_ge(sum_done, NT * (b + 1))
                dve.tensor_scalar(coef[:, :], ssum[:, :], UNIT_EPS, None, ALU.add).then_inc(den_done, 1)
                dve.wait_ge(den_done, b + 1)
                dve.reciprocal(coef[:, :], coef[:, :]).then_inc(dinv_done, 1)
                dve.wait_ge(dinv_done, b + 1)
                dve.wait_ge(tanh_done, b + 1)
                dve.tensor_tensor(out=coef[:, :], in0=coef[:, :], in1=tanh_s[:, :], op=ALU.mult).then_inc(coef_done, 1)
                dve.wait_ge(coef_done, b + 1)
                dve.wait_ge(hl_read, 2 + NT * (b + 1))
                for t in range(NT):
                    dve.scalar_tensor_tensor(out=hl[:, t, :], in0=sel[:, t, :], scalar=coef[:, t:t + 1],
                                             in1=hl[:, t, :], op0=ALU.mult, op1=ALU.mult).then_inc(hz_done, 1)

            def front():
                lows(0, aT, NC)
                residual(0, 0, 0, range(NT))
                moments(0, 0, 0)
                normalise(0, 0)
                lows(NC, zT, NC)

            def body(b, p, last):
                t_att, t_lat, t_z = turns_of(b, last)
                s_out, s_lat = sums_of(b, last)
                if not last:
                    lows(t_att, aT, NC)
                route(b, p)
                weigh(b)
                if not last:
                    residual(b + 1, 1 - p, s_out, range(0, NT // 2))
                lows(t_lat, hT, NL)
                if not last:
                    residual(b + 1, 1 - p, s_out, range(NT // 2, NT))
                    moments(b + 1, 1 - p, s_out)
                if not last:
                    normalise(b + 1, 1 - p)
                for t in range(NT):
                    dve.wait_ge(o_ready, s_lat + t + 1)
                    dve.tensor_tensor(out=x1[:, p, t, :], in0=ps_o[:, t, :], in1=x1[:, p, t, :], op=ALU.add) \
                        .then_inc(o_read, 1)
                if not last:
                    lows(t_z, zT, NC)

            walk(dve, front, body)

        @block.scalar
        def _(act):
            act.wait_ge(lat_sq, 2 * NL)
            act.activation(nrm_s[:, :], nrm[:, :], ACT.Sqrt).then_inc(lat_root, 1)
            act.sem_inc(hl_read, 2)

            def highs(n, dst, count):
                for c in range(count):
                    act.wait_ge(turned, n + c + 1)
                    act.activation(dst[0][:, c, :], ps_t[:, c % 2, :], ACT.Copy).then_inc(t_high, 1)

            def front():
                act.wait_ge(w_low, 5)
                highs(0, aT, NC)
                highs(NC, zT, NC)

            def body(b, p, last):
                t_att, t_lat, t_z = turns_of(b, last)
                if not last:
                    highs(t_att, aT, NC)
                for t in range(NT):
                    act.wait_ge(r_read, 2 + NT * b + t + 1)
                    act.activation(hl[:, t, :], ps_r[:, t % 2, NB:2 * NB], ACT.Copy).then_inc(hl_read, 1)
                act.wait_ge(clip_done, b + 1)
                act.activation(r_abs[:, :, :], rc[:, :, :], ACT.Abs).then_inc(abs_done, 1)
                act.wait_ge(abs_done, b + 1)
                act.activation(u[:, :, :], r_abs[:, :, :], ACT.Exp, scale=-1.0).then_inc(u_done, 1)
                act.wait_ge(u_done, b + 1)
                act.activation(w[:, :, :], u[:, :, :], ACT.Identity, bias=1.0).then_inc(w_done, 1)
                act.activation(ln_w[:, :, :], u[:, :, :], ACT.Ln, bias=1.0).then_inc(ln_done, 1)
                act.wait_ge(sum_done, NT * (b + 1))
                act.activation(tanh_s[:, :], ssum[:, :], ACT.Tanh).then_inc(tanh_done, 1)
                highs(t_lat, hT, NL)
                if not last:
                    act.wait_ge(z_out, 32 * (b + 1))
                    highs(t_z, zT, NC)

            walk(act, front, body)

        @block.tensor
        def _(pe):
            pe.wait_ge(g_scaled, 2 * NC)
            for c in range(NC):
                last = pe.matmul(ps_r[:, 0, 0:NB], ones[:, :], rc[:, c, :], start=c == 0, stop=c == NC - 1)
            last.then_inc(g_summed, 1)
            for c in range(NC):
                last = pe.matmul(ps_r[:, 1, 0:NB], b_cols[:, c, :], rw_f[:, c, :], start=c == 0, stop=c == NC - 1)
            last.then_inc(g_summed, 1)
            pe.wait_ge(lat_unit, 2 * NL)
            for c in range(NC):
                for n in range(NL):
                    last = pe.transpose(ps_t[:, c // 2, (c % 2 * NL + n) * P:(c % 2 * NL + n + 1) * P],
                                        x1[:, 0, n, c * P:(c + 1) * P], ident[:, :])
                if c % 2:
                    last.then_inc(lat_turned, 1)
            pe.wait_ge(w_low, 5)

            def turn(n, src, count):
                for c in range(count):
                    need(pe, t_low, n + c - 1)
                    for t in range(NT):
                        last = pe.transpose(ps_t[:, c % 2, t * P:(t + 1) * P], src[:, t, c * P:(c + 1) * P],
                                            ident[:, :])
                    last.then_inc(turned, 1)

            def sums(dst, a, w_, t, chunks):
                passes = [(a[m][:, k, t * P:(t + 1) * P], w_[n][:, k, :]) for k in range(chunks) for m, n in PASSES]
                for n, (stationary, moving) in enumerate(passes):
                    last = pe.matmul(dst, stationary, moving, start=n == 0, stop=n == len(passes) - 1)
                return last

            def project_out(n):
                for t in range(NT):
                    need(pe, o_read, n + t - NT + 1)
                    sums(ps_o[:, t, :], aT, wo, t, NC).then_inc(o_ready, 1)

            def front():
                pe.wait_ge(att_in, 16 * NC)
                turn(0, att, NC)
                pe.wait_ge(t_low, NC)
                project_out(0)
                pe.wait_ge(z_done, NT)
                turn(NC, z, NC)

            def body(b, p, last):
                t_att, t_lat, t_z = turns_of(b, last)
                s_out, s_lat = sums_of(b, last)
                if not last:
                    pe.wait_ge(att_in, 16 * NC * (b + 2))
                    turn(t_att, att, NC)
                pe.wait_ge(t_low, 2 * NC + TURNS * b)
                for t in range(NT):
                    pe.wait_ge(r_read, NT * b + t + 1)
                    pe.wait_ge(hl_read, NT * b + t + 1)
                    sums(ps_r[:, t % 2, :], zT, ru, t, NC).then_inc(r_ready, 1)
                if not last:
                    pe.wait_ge(t_low, t_att + NC)
                    project_out(s_out)
                pe.wait_ge(hz_done, NT * (b + 1))
                turn(t_lat, hl, NL)
                pe.wait_ge(t_low, t_lat + NL)
                for t in range(NT):
                    pe.wait_ge(o_read, s_lat + t - NT + 1)
                    sums(ps_o[:, t, :], hT, vg, t, NL).then_inc(o_ready, 1)
                if not last:
                    pe.wait_ge(z_done, NT * (b + 2))
                    turn(t_z, z, NC)

            walk(pe, front, body)


def feed(nc, W1T, W2T, zh_d, zl_d, part_d, out):
    LAG = 2
    NG = 4
    STEPS = 2 * NF
    ROUNDS = B // 2
    with ExitStack() as ctx:
        def sb(name, shape, dt=F32):
            return ctx.enter_context(nc.sbuf_tensor("f_" + name, shape, dt))

        def sem(name):
            return ctx.enter_context(nc.semaphore("f_" + name))

        w1 = [sb("w1_h", [P, NC, FF], F32R), sb("w1_l", [P, NC, FF], F32R)]
        w2 = [sb("w2_h", [P, NF, D], F32R), sb("w2_l", [P, NF, D], F32R)]
        zT = [sb("zT_h", [P, 2, NC, S], F32R), sb("zT_l", [P, 2, NC, S], F32R)]
        part = sb("part", [P, NT, D])
        y = sb("y", [P, NT, D])
        g_f = sb("g_f", [P, NG, S])
        g_h, g_l = sb("g_h", [P, NG, S], F32R), sb("g_l", [P, NG, S], F32R)
        ps_h = ctx.enter_context(nc.psum_tensor("f_ps_h", [P, NG, S], F32))
        ps_y = ctx.enter_context(nc.psum_tensor("f_ps_y", [P, NT, D], F32))

        stage_in = [sem("stage_in0"), sem("stage_in1")]
        w_high, w_low = sem("w_high"), sem("w_low")
        z_in = [sem("z_in0"), sem("z_in1")]
        part_in = sem("part_in")
        hidden, gelu_done, g_high, g_low, g_used = (
            sem("hidden"), sem("gelu_done"), sem("g_high"), sem("g_low"), sem("g_used"))
        y_done, y_out = sem("y_done"), sem("y_out")

        NQ = 4
        NPC = 2 * NF // NQ
        stages = [part, y]

        def source(n):
            rows = slice(n // 2 * NQ * P, (n // 2 + 1) * NQ * P)
            return tokens(W1T[:, rows] if n % 2 == 0 else W2T[rows, :])

        def placed(n, part):
            if n % 2 == 0:
                return w1[part][:, :, n // 2 * NQ * P:(n // 2 + 1) * NQ * P]
            return w2[part][:, n // 2 * NQ:(n // 2 + 1) * NQ, :]

        def pieces_before(g, j):
            if not isinstance(g, int) or g > 0 or j >= NF:
                return ()
            if j == 0:
                return 0, 1
            return {1: (j // NQ * 2 + 2,), 2: (j // NQ * 2 + 3,)}.get(j % NQ, ()) if j < NF - NQ else ()

        block = ctx.enter_context(nc.Block())

        @block.sync
        def _(sp):
            def load(g, j):
                for h, z_d in enumerate((zh_d, zl_d)):
                    sp.dma_start(zT[h][:, j, :, :].bitcast(F32), z_d[2 * g + j]).then_inc(z_in[j], 16)

            def load_part(b):
                sp.dma_start(part[:, :, :], tokens(part_d[b])).then_inc(part_in, 16)

            def store(b):
                sp.wait_ge(y_done, NT * (b + 1))
                sp.dma_start(tokens(out[b]), y[:, :, :]).then_inc(y_out, 16)

            for n in range(NPC):
                need(sp, w_low, n - 1)
                sp.dma_start(stages[n % 2][:, :, :], source(n)).then_inc(stage_in[n % 2], 16)
                if n in (0, 3):
                    load(0, n // 3)
            sp.wait_ge(w_low, NPC)
            sp.sem_inc(y_out, 16)
            load_part(0)
            with sp.Fori(0, ROUNDS - 1) as g:
                for j in range(2):
                    sp.wait_ge(hidden, STEPS * g + (j + 1) * NF)
                    load(g + 1, j)
                    store(2 * g + j)
                    load_part(2 * g + j + 1)
            store(B - 2)
            load_part(B - 1)
            store(B - 1)
            sp.wait_ge(y_out, 16 * (B + 1))

        @block.gpsimd
        def _(pool):
            pool.sem_inc(g_low, NG)
            with pool.Fori(0, B * NF // NG) as r:
                for k in range(NG):
                    pool.wait_ge(g_high, NG * r + k + 1)
                    pool.tensor_tensor(out=g_l[:, k, :], in0=g_f[:, k, :], in1=g_h[:, k, :].bitcast(F32),
                                       op=ALU.subtract).then_inc(g_low, 1)

        @block.scalar
        def _(act):
            act.sem_inc(gelu_done, NG)

            def step(g, j, more):
                for n in pieces_before(g, j):
                    act.wait_ge(stage_in[n % 2], 16 * (n // 2 + 1))
                    act.activation(placed(n, 0), stages[n % 2][:, :, :], ACT.Copy).then_inc(w_high, 1)
                n = STEPS * g + j
                act.wait_ge(hidden, n + 1)
                act.wait_ge(g_low, n + 1)
                act.activation(g_f[:, j % NG, :], ps_h[:, j % NG, :], ACT.Gelu).then_inc(gelu_done, 1)

            walk_rounds(act, step, 0, STEPS, ROUNDS)

        @block.vector
        def _(dve):
            def step(g, j, more):
                for n in pieces_before(g, j):
                    dve.wait_ge(w_high, n + 1)
                    dve.tensor_tensor(out=placed(n, 1), in0=stages[n % 2][:, :, :], in1=placed(n, 0).bitcast(F32),
                                      op=ALU.subtract).then_inc(w_low, 1)
                if more:
                    n = STEPS * g + j
                    dve.wait_ge(gelu_done, NG + n + 1)
                    need(dve, g_used, n - NG + 1)
                    dve.tensor_copy(g_h[:, j % NG, :], g_f[:, j % NG, :]).then_inc(g_high, 1)
                if (at := behind(g, j, LAG + 1, STEPS, ROUNDS)) and at[1] % NF == NF - 1:
                    b = 2 * at[0] + at[1] // NF
                    dve.wait_ge(part_in, 16 * b + 16)
                    dve.wait_ge(y_out, 16 * b + 16)
                    dve.wait_ge(g_used, STEPS * at[0] + at[1] + 1)
                    for t in range(NT):
                        dve.tensor_tensor(out=y[:, t, :], in0=ps_y[:, t, :], in1=part[:, t, :], op=ALU.add) \
                            .then_inc(y_done, 1)

            walk_rounds(dve, step, LAG + 1, STEPS, ROUNDS)

        @block.tensor
        def _(pe):
            def step(g, j, more):
                if more:
                    b, f = j // NF, j % NF
                    if isinstance(g, int) and b == 0 and f % NQ == 0:
                        pe.wait_ge(w_low, f // NQ * 2 + 1)
                    fs = slice(f * P, (f + 1) * P)
                    if f == 0:
                        pe.wait_ge(z_in[b], 32 * g + 32)
                    pe.wait_ge(gelu_done, STEPS * g + j + 1)
                    passes = [(w1[x][:, k, fs], zT[y][:, b, k, :]) for k in range(NC) for x, y in PASSES]
                    for m, (w, a) in enumerate(passes):
                        last = pe.matmul(ps_h[:, j % NG, :], w, a, start=m == 0, stop=m == len(passes) - 1)
                    last.then_inc(hidden, 1)
                if at := behind(g, j, LAG, STEPS, ROUNDS):
                    n = STEPS * at[0] + at[1]
                    b, f = 2 * at[0] + at[1] // NF, at[1] % NF
                    pe.wait_ge(g_low, NG + n + 1)
                    if isinstance(n, int) and n < NF and f % NQ == 0:
                        pe.wait_ge(w_low, f // NQ * 2 + 2)
                    for t in range(NT):
                        if f == 0:
                            need(pe, y_done, NT * (b - 1) + t + 1)
                        gs = [a[:, at[1] % NG, t * P:(t + 1) * P] for a in (g_h, g_l)]
                        for m, (x, y) in enumerate(PASSES):
                            last = pe.matmul(ps_y[:, t, :], gs[x], w2[y][:, f, :],
                                             start=f == 0 and m == 0, stop=f == NF - 1 and m == 2)
                    last.then_inc(g_used, 1)

            walk_rounds(pe, step, LAG, STEPS, ROUNDS)


INPUTS = ("x", "ctxT", "bias", "mask", "WqT", "bq", "WkT", "bk", "WvT", "bv", "WoT", "bo", "W1T", "W2T",
          "ln_g", "ln_b", "rWT", "rb", "rawU", "rawV", "gamma")


def kernel(x, ctx_1024, fside_1x16xSxS2_0, mask_Bx1xSxS2_ik1, L0_xattn_Wq, L0_xattn_bq, L0_xattn_Wk, L0_xattn_bk,
           L0_xattn_Wv, L0_xattn_bv, L0_xattn_Wo, L0_xattn_bo, L0_ffn_W1, L0_ffn_W2, L0_ffn_ln_g, L0_ffn_ln_b,
           L0_ffn_router_W, L0_ffn_router_b, L0_ffn_raw_U, L0_ffn_raw_V, L0_ffn_gamma):
    import numpy as np
    import concourse.bacc as bacc
    from concourse.bass_utils import run_bass_kernel_spmd

    given = {
        "x": x, "ctxT": np.asarray(ctx_1024).transpose(0, 2, 1), "bias": fside_1x16xSxS2_0,
        "mask": np.asarray(mask_Bx1xSxS2_ik1)[:, 0],
        "WqT": np.asarray(L0_xattn_Wq).T, "bq": np.asarray(L0_xattn_bq).reshape(NC, P).T, "WkT": np.asarray(L0_xattn_Wk).T, "bk": np.asarray(L0_xattn_bk).reshape(NC, P).T,
        "WvT": np.asarray(L0_xattn_Wv).T, "bv": L0_xattn_bv, "WoT": np.asarray(L0_xattn_Wo).T, "bo": L0_xattn_bo,
        "W1T": np.asarray(L0_ffn_W1).T, "W2T": np.asarray(L0_ffn_W2).T, "ln_g": np.asarray(L0_ffn_ln_g).reshape(NC, P).T,
        "ln_b": np.asarray(L0_ffn_ln_b).reshape(NC, P).T,
        "rWT": np.asarray(L0_ffn_router_W).T, "rb": L0_ffn_router_b, "rawU": L0_ffn_raw_U, "rawV": L0_ffn_raw_V,
        "gamma": np.asarray(L0_ffn_gamma).reshape(-1),
    }
    nc = bacc.Bacc("TRN2", target_bir_lowering=False, num_devices=1)
    arrays, aps = {}, []
    for name in INPUTS:
        a = np.ascontiguousarray(given[name])
        arrays["in_" + name] = a
        aps.append(nc.dram_tensor("in_" + name, a.shape, mybir.dt.from_np(a.dtype), kind="ExternalInput").ap())
    out = nc.dram_tensor("out_x", (B, S, D), F32, kind="ExternalOutput").ap()
    build(nc, *aps, out)
    result = run_bass_kernel_spmd(nc, [arrays], core_ids=[0])
    return result.results[0]["out_x"]
```
